# Optimizing a Trainium2 kernel written in Bass

```python
import numpy as np
import jax
import jax.numpy as jnp

def _softmax(x, axis=-1):
    return jax.nn.softmax(x, axis=axis)

def _gelu(x):
    return jax.nn.gelu(x, approximate=True)

def _silu(x):
    return jax.nn.silu(x)

def _sigmoid(x):
    return jax.nn.sigmoid(x)

def _layernorm(x, axis=-1, eps=1e-05):
    m = jnp.mean(x, axis=axis, keepdims=True)
    v = jnp.var(x, axis=axis, keepdims=True)
    return (x - m) / jnp.sqrt(v + eps)

def _scatter_add(tgt, idx, src, axis=0):
    return tgt.at[idx].add(src)

def _segment_sum(src, seg, n):
    return jax.ops.segment_sum(src, seg, n)
kernel_name = 'mk_decoder_preln_d2_seqx_r8_975dae'

def setup_inputs(seed: int=0):
    np.random.seed(seed)
    _w = jnp.asarray

    def _rec_inputs():
        import jax
        import jax.numpy as jnp
        _rk = jax.random.key(seed)
        x = 7.22e-05 + 1 * jax.random.normal(jax.random.fold_in(_rk, 1), (16, 56, 256), jnp.float32)
        _lenS = 56 - jax.random.randint(jax.random.fold_in(_rk, 7), (16,), 0, max(1, 56 // 4) + 1, jnp.int32)
        _lenS2 = 1500 - jax.random.randint(jax.random.fold_in(_rk, 8), (16,), 0, max(1, 1500 // 4) + 1, jnp.int32)
        _ctx_512P = jax.random.normal(jax.random.fold_in(_rk, 11), (16, 16, 64), jnp.float32)
        _ctx_512c = jax.random.dirichlet(jax.random.fold_in(_rk, 511), 0.3 * jnp.ones((16,), jnp.float32), (16, 1500))
        _ctx_512t = jnp.einsum('bsk,bkd->bsd', _ctx_512c, _ctx_512P)
        _ctx_512t = _ctx_512t * jax.lax.rsqrt(jnp.mean(jnp.square(_ctx_512t)) + 1e-12) * 0.953939
        ctx_512 = -0.000514642 + 1.00011 * (_ctx_512t + 0.3 * jax.random.normal(jax.random.fold_in(_rk, 611), (16, 1500, 64), jnp.float32))
        return (x, ctx_512)
    x, ctx_512 = _rec_inputs()

    def _L0_attn_setup():
        import jax, jax.numpy as jnp
        import numpy as np
        B, T, C = (4, 512, 256)

        def _scan_op(a, bb):
            g_i, v_i = a
            g_j, v_j = bb
            return (g_j * g_i, g_j * v_i + v_j)
        key = jax.random.key(seed)
        k1, k2 = jax.random.split(key)
        x = jax.random.normal(k1, (B, T, C), dtype=jnp.float32)
        W = jax.random.normal(k2, (2 * C, C), dtype=jnp.float32) * (1.0 / np.sqrt(C))
        b = jnp.zeros((2 * C,), dtype=jnp.float32)
        return {'x': x, 'W': W, 'b': b}
    _L0_attn_all = _L0_attn_setup()
    _L0_attn_in = {k: v for k, v in _L0_attn_all.items() if k in ('W', 'b')}
    del _L0_attn_all

    def _L0_xattn_setup():
        import jax, jax.numpy as jnp
        import numpy as np
        B, S, H, NH, L = (2, 256, 256, 16, 64)
        HD = H // NH
        key = jax.random.key(seed)
        k1, k2, k3, k4, k5 = jax.random.split(key, 5)
        scale = 0.02
        return {'q': jax.random.normal(k1, (B, S, H), dtype=jnp.float32), 'latent_kv': jax.random.normal(k2, (B, S, L), dtype=jnp.float32), 'Wq': jax.random.normal(k3, (H, H), dtype=jnp.float32) * scale, 'Wkv_expand': jax.random.normal(k4, (2 * H, L), dtype=jnp.float32) * scale, 'Wout': jax.random.normal(k5, (H, H), dtype=jnp.float32) * scale}
    _L0_xattn_all = _L0_xattn_setup()
    _L0_xattn_in = {k: v for k, v in _L0_xattn_all.items() if k in ('Wq', 'Wkv_expand', 'Wout')}
    del _L0_xattn_all

    def _L0_ffn_setup():
        import jax, jax.numpy as jnp
        import numpy as np
        H = 256
        I = 128
        K = 8
        E = 128
        TOPK = 4
        EPS = 1e-08
        key = jax.random.key(seed)
        ks = jax.random.split(key, 10)
        s = 0.02
        return {'x': jax.random.normal(ks[0], (4, 256, H), jnp.float32), 'w_router': jax.random.normal(ks[1], (H, E), jnp.float32) * s, 'w_gate': jax.random.normal(ks[2], (H, K * I), jnp.float32) * s, 'w_up': jax.random.normal(ks[3], (H, K * I), jnp.float32) * s, 'w_down': jax.random.normal(ks[4], (I, H), jnp.float32) * s, 'amplitudes': jax.random.normal(ks[5], (E, K, 2), jnp.float32) * 0.1, 'expert_scale': jnp.ones((E,), jnp.float32), 'shared_w_gate': jax.random.normal(ks[6], (H, 2 * I), jnp.float32) * s, 'shared_w_up': jax.random.normal(ks[7], (H, 2 * I), jnp.float32) * s, 'shared_w_down': jax.random.normal(ks[8], (2 * I, H), jnp.float32) * s}
    _L0_ffn_all = _L0_ffn_setup()
    _L0_ffn_in = {k: v for k, v in _L0_ffn_all.items() if k in ('w_router', 'w_gate', 'w_up', 'w_down', 'amplitudes', 'expert_scale', 'shared_w_gate', 'shared_w_up', 'shared_w_down')}
    del _L0_ffn_all

    def _L1_attn_setup():
        import jax, jax.numpy as jnp
        import numpy as np
        D_MODEL = 256
        D_STATE = 64
        EXPAND = 2
        N_HEADS = 64
        NGROUPS = 1
        MIMO_RANK = 1
        D_INNER = EXPAND * D_MODEL
        HEAD_DIM = D_INNER // N_HEADS
        HEADS_PER_GROUP = N_HEADS // NGROUPS
        SSD_SCALE = (D_STATE * MIMO_RANK) ** (-0.5)
        EPS = 1e-06
        BATCH, SEQ = (2, 256)

        def _rms(v):
            return v * jax.lax.rsqrt(jnp.mean(v * v, axis=-1, keepdims=True) + EPS)

        def _rope(v, phi):
            v1, v2 = (v[..., 0::2], v[..., 1::2])
            c, s = (jnp.cos(phi), jnp.sin(phi))
            r1 = v1 * c - v2 * s
            r2 = v1 * s + v2 * c
            return jnp.stack([r1, r2], axis=-1).reshape(v.shape)
        key = jax.random.key(seed)
        ks = jax.random.split(key, 10)
        d_in_proj = 2 * D_INNER + 2 * NGROUPS * MIMO_RANK * D_STATE + N_HEADS
        return {'x': jax.random.normal(ks[0], (BATCH, SEQ, D_MODEL), jnp.float32), 'W_in': jax.random.normal(ks[1], (D_MODEL, d_in_proj), jnp.float32) * 0.02, 'W_out': jax.random.normal(ks[2], (D_INNER, D_MODEL), jnp.float32) * 0.02, 'dt_bias': jax.random.normal(ks[3], (N_HEADS,), jnp.float32) * 0.1, 'A_log': jnp.log(jax.random.uniform(ks[4], (N_HEADS,), jnp.float32, 1.0, 16.0)), 'D_param': jnp.ones((N_HEADS,), jnp.float32), 'B_bias': jax.random.normal(ks[5], (N_HEADS, D_STATE), jnp.float32) * 0.02, 'C_bias': jax.random.normal(ks[6], (N_HEADS, D_STATE), jnp.float32) * 0.02, 'rope_freqs': jax.random.uniform(ks[7], (N_HEADS, D_STATE // 2), jnp.float32, 0.0, 1.0), 'norm_w': jnp.ones((D_INNER,), jnp.float32)}
    _L1_attn_all = _L1_attn_setup()
    _L1_attn_in = {k: v for k, v in _L1_attn_all.items() if k in ('W_in', 'W_out', 'dt_bias', 'A_log', 'D_param', 'B_bias', 'C_bias', 'rope_freqs', 'norm_w')}
    del _L1_attn_all

    def _L1_xattn_setup():
        import jax, jax.numpy as jnp
        import numpy as np
        B, S, L = (2, 128, 128)
        DIM_Q, H, K, D_C, D_CQ, R = (256, 16, 128, 64, 192, 64)

        def _rope_tables(length, dim):
            inv = 1.0 / 10000.0 ** (jnp.arange(0, dim, 2, dtype=jnp.float32) / dim)
            f = jnp.arange(length, dtype=jnp.float32)[:, None] * inv[None, :]
            sin = jnp.repeat(jnp.sin(f), 2, axis=-1)
            cos = jnp.repeat(jnp.cos(f), 2, axis=-1)
            return (sin, cos)

        def _rotate_half(x):
            half = x.shape[-1] // 2
            return jnp.concatenate([-x[..., half:], x[..., :half]], axis=-1)

        def _apply_rope(x, sin, cos):
            return x * cos + _rotate_half(x) * sin
        key = jax.random.key(seed)
        ks = jax.random.split(key, 8)
        return {'hidden_q': jax.random.normal(ks[0], (B, S, DIM_Q), jnp.float32), 'kv_c': jax.random.normal(ks[1], (B, L, D_C), jnp.float32), 'Wq': jax.random.normal(ks[2], (H * K, DIM_Q), jnp.float32) / np.sqrt(DIM_Q).astype(np.float32), 'w_kc_q': jax.random.normal(ks[3], (H, K, D_CQ), jnp.float32) / np.sqrt(K).astype(np.float32), 'w_kc_kv': jax.random.normal(ks[4], (H, K, D_C), jnp.float32) / np.sqrt(K).astype(np.float32), 'W_qr': jax.random.normal(ks[5], (H, D_CQ, R), jnp.float32) / np.float32(np.sqrt(D_CQ) * np.sqrt(R)), 'W_kr': jax.random.normal(ks[6], (H, D_C, R), jnp.float32) / np.sqrt(D_C).astype(np.float32), 'Wo': jax.random.normal(ks[7], (DIM_Q, H * K), jnp.float32) / np.sqrt(H * K).astype(np.float32)}
    _L1_xattn_all = _L1_xattn_setup()
    _L1_xattn_in = {k: v for k, v in _L1_xattn_all.items() if k in ('Wq', 'w_kc_q', 'w_kc_kv', 'W_qr', 'W_kr', 'Wo')}
    del _L1_xattn_all

    def _L1_ffn_setup():
        import jax, jax.numpy as jnp
        import numpy as np
        LHS_BITS = 8
        RHS_BITS = 8

        def fake_quant(x, bits, axes):
            qmax = 2.0 ** (bits - 1) - 1.0
            amax = jnp.max(jnp.abs(x), axis=axes, keepdims=True)
            scale = jnp.where(amax > 0, amax / qmax, jnp.ones_like(amax))
            q = jnp.clip(jnp.round(x / scale), -qmax, qmax) * scale
            return x + jax.lax.stop_gradient(q - x)
        key = jax.random.key(seed)
        k1, k2, k3 = jax.random.split(key, 3)
        B, S, D, F = (4, 256, 256, 256)
        x = jax.random.normal(k1, (B, S, D), dtype=jnp.float32)
        kernel = jax.random.normal(k2, (D, F), dtype=jnp.float32) * (1.0 / np.sqrt(D))
        bias = jax.random.normal(k3, (F,), dtype=jnp.float32) * 0.02
        return {'x': x, 'kernel': kernel, 'bias': bias}
    _L1_ffn_all = _L1_ffn_setup()
    _L1_ffn_in = {k: v for k, v in _L1_ffn_all.items() if k in ('kernel', 'bias')}
    del _L1_ffn_all
    return {'x': x, 'ctx_512': ctx_512, 'L0_attn_W': _L0_attn_in['W'], 'L0_attn_b': _L0_attn_in['b'], 'L0_xattn_Wq': _L0_xattn_in['Wq'], 'L0_xattn_Wkv_expand': _L0_xattn_in['Wkv_expand'], 'L0_xattn_Wout': _L0_xattn_in['Wout'], 'L0_ffn_w_router': _L0_ffn_in['w_router'], 'L0_ffn_w_gate': _L0_ffn_in['w_gate'], 'L0_ffn_w_up': _L0_ffn_in['w_up'], 'L0_ffn_w_down': _L0_ffn_in['w_down'], 'L0_ffn_amplitudes': _L0_ffn_in['amplitudes'], 'L0_ffn_expert_scale': _L0_ffn_in['expert_scale'], 'L0_ffn_shared_w_gate': _L0_ffn_in['shared_w_gate'], 'L0_ffn_shared_w_up': _L0_ffn_in['shared_w_up'], 'L0_ffn_shared_w_down': _L0_ffn_in['shared_w_down'], 'L1_attn_W_in': _L1_attn_in['W_in'], 'L1_attn_W_out': _L1_attn_in['W_out'], 'L1_attn_dt_bias': _L1_attn_in['dt_bias'], 'L1_attn_A_log': _L1_attn_in['A_log'], 'L1_attn_D_param': _L1_attn_in['D_param'], 'L1_attn_B_bias': _L1_attn_in['B_bias'], 'L1_attn_C_bias': _L1_attn_in['C_bias'], 'L1_attn_rope_freqs': _L1_attn_in['rope_freqs'], 'L1_attn_norm_w': _L1_attn_in['norm_w'], 'L1_xattn_Wq': _L1_xattn_in['Wq'], 'L1_xattn_w_kc_q': _L1_xattn_in['w_kc_q'], 'L1_xattn_w_kc_kv': _L1_xattn_in['w_kc_kv'], 'L1_xattn_W_qr': _L1_xattn_in['W_qr'], 'L1_xattn_W_kr': _L1_xattn_in['W_kr'], 'L1_xattn_Wo': _L1_xattn_in['Wo'], 'L1_ffn_kernel': _L1_ffn_in['kernel'], 'L1_ffn_bias': _L1_ffn_in['bias']}

def reference(x, ctx_512, L0_attn_W, L0_attn_b, L0_xattn_Wq, L0_xattn_Wkv_expand, L0_xattn_Wout, L0_ffn_w_router, L0_ffn_w_gate, L0_ffn_w_up, L0_ffn_w_down, L0_ffn_amplitudes, L0_ffn_expert_scale, L0_ffn_shared_w_gate, L0_ffn_shared_w_up, L0_ffn_shared_w_down, L1_attn_W_in, L1_attn_W_out, L1_attn_dt_bias, L1_attn_A_log, L1_attn_D_param, L1_attn_B_bias, L1_attn_C_bias, L1_attn_rope_freqs, L1_attn_norm_w, L1_xattn_Wq, L1_xattn_w_kc_q, L1_xattn_w_kc_kv, L1_xattn_W_qr, L1_xattn_W_kr, L1_xattn_Wo, L1_ffn_kernel, L1_ffn_bias):
    import jax
    import jax.numpy as jnp

    def _L0_attn_ref(x, W, b):
        import jax, jax.numpy as jnp
        import numpy as np
        B, T, C = (4, 512, 256)

        def _scan_op(a, bb):
            g_i, v_i = a
            g_j, v_j = bb
            return (g_j * g_i, g_j * v_i + v_j)
        params = jnp.einsum('btc,dc->btd', x, W) + b
        gates, values = jnp.split(params, 2, axis=-1)
        gates = jax.nn.sigmoid(gates)
        values = jnp.tanh(values)
        _, hidden = jax.lax.associative_scan(_scan_op, (gates, values), axis=1)
        return hidden

    def _L0_xattn_ref(q, latent_kv, Wq, Wkv_expand, Wout):
        import jax, jax.numpy as jnp
        import numpy as np
        B, S, H, NH, L = (2, 256, 256, 16, 64)
        HD = H // NH
        b, sq, _ = q.shape
        sk = latent_kv.shape[1]
        qp = q @ Wq.T
        kv = latent_kv @ Wkv_expand.T
        k, v = jnp.split(kv, 2, axis=-1)
        qh = qp.reshape(b, sq, NH, HD).transpose(0, 2, 1, 3)
        kh = k.reshape(b, sk, NH, HD).transpose(0, 2, 1, 3)
        vh = v.reshape(b, sk, NH, HD).transpose(0, 2, 1, 3)
        inv_sqrt_d = 1.0 / jnp.sqrt(jnp.float32(HD))
        scores = jnp.einsum('bhqd,bhkd->bhqk', qh, kh) * inv_sqrt_d
        causal = jnp.tril(jnp.ones((sq, sk), dtype=bool))
        scores = jnp.where(causal, scores, jnp.finfo(scores.dtype).min)
        attn = jax.nn.softmax(scores, axis=-1)
        out = jnp.einsum('bhqk,bhkd->bhqd', attn, vh)
        out = out.transpose(0, 2, 1, 3).reshape(b, sq, H)
        return out @ Wout.T

    def _L0_ffn_ref(x, w_router, w_gate, w_up, w_down, amplitudes, expert_scale, shared_w_gate, shared_w_up, shared_w_down):
        import jax, jax.numpy as jnp
        import numpy as np
        H = 256
        I = 128
        K = 8
        E = 128
        TOPK = 4
        EPS = 1e-08
        B, S, _ = x.shape
        T = B * S
        xt = x.reshape(T, H)
        probs = jax.nn.softmax(xt @ w_router, axis=-1)
        topk_p, topk_idx = jax.lax.top_k(probs, TOPK)
        topk_w = topk_p / (jnp.sum(topk_p, axis=-1, keepdims=True) + EPS)
        gate = (xt @ w_gate).reshape(T, K, I)
        up = (xt @ w_up).reshape(T, K, I)
        basis = jax.nn.silu(gate) * up
        p = amplitudes[..., 0] ** 2 + amplitudes[..., 1] ** 2
        mix = p / (jnp.sum(p, axis=-1, keepdims=True) + EPS)
        mix_sel = mix[topk_idx]
        mixed = jnp.einsum('tek,tki->tei', mix_sel, basis)
        down = jnp.einsum('tei,ih->teh', mixed, w_down)
        coeff = topk_w * expert_scale[topk_idx]
        out = jnp.einsum('teh,te->th', down, coeff)
        shared = jax.nn.silu(xt @ shared_w_gate) * (xt @ shared_w_up) @ shared_w_down
        out = out + shared
        return out.reshape(B, S, H)

    def _L1_attn_ref(x, W_in, W_out, dt_bias, A_log, D_param, B_bias, C_bias, rope_freqs, norm_w):
        import jax, jax.numpy as jnp
        import numpy as np
        D_MODEL = 256
        D_STATE = 64
        EXPAND = 2
        N_HEADS = 64
        NGROUPS = 1
        MIMO_RANK = 1
        D_INNER = EXPAND * D_MODEL
        HEAD_DIM = D_INNER // N_HEADS
        HEADS_PER_GROUP = N_HEADS // NGROUPS
        SSD_SCALE = (D_STATE * MIMO_RANK) ** (-0.5)
        EPS = 1e-06
        BATCH, SEQ = (2, 256)

        def _rms(v):
            return v * jax.lax.rsqrt(jnp.mean(v * v, axis=-1, keepdims=True) + EPS)

        def _rope(v, phi):
            v1, v2 = (v[..., 0::2], v[..., 1::2])
            c, s = (jnp.cos(phi), jnp.sin(phi))
            r1 = v1 * c - v2 * s
            r2 = v1 * s + v2 * c
            return jnp.stack([r1, r2], axis=-1).reshape(v.shape)
        Bsz, T, _ = x.shape
        zxbcdt = x @ W_in
        z = zxbcdt[..., :D_INNER]
        xs = zxbcdt[..., D_INNER:2 * D_INNER]
        o = 2 * D_INNER
        gn = NGROUPS * D_STATE
        Braw = zxbcdt[..., o:o + gn].reshape(Bsz, T, NGROUPS, D_STATE)
        Craw = zxbcdt[..., o + gn:o + 2 * gn].reshape(Bsz, T, NGROUPS, D_STATE)
        dt_raw = zxbcdt[..., o + 2 * gn:]
        dt = jax.nn.softplus(dt_raw + dt_bias)
        a = jnp.exp(-jnp.exp(A_log) * dt)
        Bh = jnp.repeat(_rms(Braw), HEADS_PER_GROUP, axis=2) + B_bias
        Ch = jnp.repeat(_rms(Craw), HEADS_PER_GROUP, axis=2) + C_bias
        phi = jnp.cumsum(dt, axis=1)[..., None] * rope_freqs
        Bh = _rope(Bh, phi)
        Ch = _rope(Ch, phi)
        xh = xs.reshape(Bsz, T, N_HEADS, HEAD_DIM)
        u = xh * dt[..., None]

        def step(h, inp):
            a_t, u_t, b_t, c_t = inp
            h = a_t[..., None, None] * h + u_t[..., None] * b_t[:, :, None, :]
            y = jnp.einsum('bhpn,bhn->bhp', h, c_t)
            return (h, y)
        h0 = jnp.zeros((Bsz, N_HEADS, HEAD_DIM, D_STATE), x.dtype)
        xs_time = (a.transpose(1, 0, 2), u.transpose(1, 0, 2, 3), Bh.transpose(1, 0, 2, 3), Ch.transpose(1, 0, 2, 3))
        _, ys = jax.lax.scan(step, h0, xs_time)
        ys = ys.transpose(1, 0, 2, 3)
        y = SSD_SCALE * ys + D_param[None, None, :, None] * xh
        y = y.reshape(Bsz, T, D_INNER)
        g = y * jax.nn.silu(z)
        y = g * jax.lax.rsqrt(jnp.mean(g * g, axis=-1, keepdims=True) + EPS) * norm_w
        return y @ W_out

    def _L1_xattn_ref(hidden_q, kv_c, Wq, w_kc_q, w_kc_kv, W_qr, W_kr, Wo):
        import jax, jax.numpy as jnp
        import numpy as np
        B, S, L = (2, 128, 128)
        DIM_Q, H, K, D_C, D_CQ, R = (256, 16, 128, 64, 192, 64)

        def _rope_tables(length, dim):
            inv = 1.0 / 10000.0 ** (jnp.arange(0, dim, 2, dtype=jnp.float32) / dim)
            f = jnp.arange(length, dtype=jnp.float32)[:, None] * inv[None, :]
            sin = jnp.repeat(jnp.sin(f), 2, axis=-1)
            cos = jnp.repeat(jnp.cos(f), 2, axis=-1)
            return (sin, cos)

        def _rotate_half(x):
            half = x.shape[-1] // 2
            return jnp.concatenate([-x[..., half:], x[..., :half]], axis=-1)

        def _apply_rope(x, sin, cos):
            return x * cos + _rotate_half(x) * sin
        Bv, Sv, _ = hidden_q.shape
        _, Lv, _ = kv_c.shape
        q_hk = (hidden_q @ Wq.T).reshape(Bv, Sv, H, K)
        q_big = jnp.einsum('bshk,hkq->bshq', q_hk, w_kc_q)
        sin_q, cos_q = _rope_tables(Sv, D_CQ)
        q_big = _apply_rope(q_big, sin_q[None, :, None, :], cos_q[None, :, None, :])
        sin_k, cos_k = _rope_tables(Lv, D_C)
        kv_r = _apply_rope(kv_c, sin_k[None], cos_k[None])
        q_r = jnp.einsum('bshq,hqr->bhsr', q_big, W_qr)
        k_r = jnp.einsum('bld,hdr->bhlr', kv_r, W_kr)
        scores = jnp.einsum('bhsr,bhlr->bhsl', q_r, k_r)
        attn = jax.nn.softmax(scores, axis=-1)
        ctx_c = jnp.einsum('bhsl,bld->bhsd', attn, kv_r)
        ctx_lat = jnp.einsum('bhsd,hkd->bhsk', ctx_c, w_kc_kv)
        ctx = ctx_lat.transpose(0, 2, 1, 3).reshape(Bv, Sv, H * K)
        return ctx @ Wo.T

    def _L1_ffn_ref(x, kernel, bias):
        import jax, jax.numpy as jnp
        import numpy as np
        LHS_BITS = 8
        RHS_BITS = 8

        def fake_quant(x, bits, axes):
            qmax = 2.0 ** (bits - 1) - 1.0
            amax = jnp.max(jnp.abs(x), axis=axes, keepdims=True)
            scale = jnp.where(amax > 0, amax / qmax, jnp.ones_like(amax))
            q = jnp.clip(jnp.round(x / scale), -qmax, qmax) * scale
            return x + jax.lax.stop_gradient(q - x)
        bq = fake_quant(bias, RHS_BITS, -1)
        xq = fake_quant(x, LHS_BITS, -1)
        kq = fake_quant(kernel, RHS_BITS, 0)
        y = jnp.einsum('bsd,df->bsf', xq, kq)
        y = y + bq[None, None, :]
        y = jax.nn.relu(y)
        return fake_quant(y, LHS_BITS, -1)
    x = x + _L0_attn_ref(_layernorm(x, axis=-1), L0_attn_W, L0_attn_b)
    x = x + _L0_xattn_ref(_layernorm(x, axis=-1), ctx_512, L0_xattn_Wq, L0_xattn_Wkv_expand, L0_xattn_Wout)
    x = x + _L0_ffn_ref(_layernorm(x, axis=-1), L0_ffn_w_router, L0_ffn_w_gate, L0_ffn_w_up, L0_ffn_w_down, L0_ffn_amplitudes, L0_ffn_expert_scale, L0_ffn_shared_w_gate, L0_ffn_shared_w_up, L0_ffn_shared_w_down)
    x = x + _L1_attn_ref(_layernorm(x, axis=-1), L1_attn_W_in, L1_attn_W_out, L1_attn_dt_bias, L1_attn_A_log, L1_attn_D_param, L1_attn_B_bias, L1_attn_C_bias, L1_attn_rope_freqs, L1_attn_norm_w)
    x = x + _L1_xattn_ref(_layernorm(x, axis=-1), ctx_512, L1_xattn_Wq, L1_xattn_w_kc_q, L1_xattn_w_kc_kv, L1_xattn_W_qr, L1_xattn_W_kr, L1_xattn_Wo)
    x = x + _L1_ffn_ref(_layernorm(x, axis=-1), L1_ffn_kernel, L1_ffn_bias)
    return x

_drawn_inputs = setup_inputs


def setup_inputs(seed=0):
    import zlib

    import numpy as np

    out = dict(_drawn_inputs(seed))
    spreads = {'L0_attn_b': (0.0, 0.1),
     'L0_ffn_expert_scale': (1.0, 0.6),
     'L1_attn_D_param': (1.0, 0.535),
     'L1_attn_norm_w': (1.0, 0.6)}
    factors = {'L0_xattn_Wq': 26.433,
     'L0_ffn_w_router': 8.0,
     'L0_ffn_w_gate': 8.0,
     'L0_ffn_w_up': 8.0,
     'L0_ffn_w_down': 8.0,
     'L0_ffn_amplitudes': 8.0,
     'L0_ffn_shared_w_gate': 3.633,
     'L0_ffn_shared_w_up': 3.673,
     'L0_ffn_shared_w_down': 3.628,
     'L1_attn_B_bias': 27.839,
     'L1_attn_C_bias': 28.79,
     'L1_attn_rope_freqs': 200.0,
     'L1_ffn_bias': 17.448,
     'L1_attn_dt_bias': 6.097,
     'L1_attn_A_log': 39.24}
    for name, (base, spread) in spreads.items():
        noise = np.random.default_rng([zlib.crc32(name.encode()), seed]).standard_normal(out[name].shape)
        drawn = base * np.exp(spread * noise) if base else spread * noise
        out[name] = jnp.asarray(drawn.astype(out[name].dtype))
    for name, factor in factors.items():
        out[name] = (out[name] * factor).astype(out[name].dtype)
    return out
```

```python
from contextlib import ExitStack

import concourse.bass as bass
from concourse import mybir

F32 = mybir.dt.float32
F16 = mybir.dt.float16
BF16 = mybir.dt.bfloat16
ALU = mybir.AluOpType
ACT = mybir.ActivationFunctionType
AX = mybir.AxisListType.X
XY = mybir.AxisListType.XY

P = 128
B, T, TP = 16, 56, 64
PAIRS = B // 2
HB = B // 2
NT = HB * T
BT = B * T
C = 256
KC = C // P
XH, XD, XDP = 16, 16, 32
E, TOPK, KB = 128, 4, 8
NEG = -1e30
LN_EPS = 1e-5
NH, HD, DS = 64, 8, 64
DI = NH * HD
SSM_TRIPS = (NH // 2 - 4) // 2
LH, DC, RQ = 16, 64, 96
S, KT = 1500, 12
KP = S // KT
LR = LH * T
LS = 2 * KT
TWO_PI = 6.2831845
HALF_PI = 1.5707963
ROUND = 12582912.0


class Own:

    def __init__(self, eng, sem):
        self.eng, self.sem, self.n, self.i, self.per = eng, sem, 0, None, 0

    def enter(self, i, per):
        self.i, self.per, self.base = i, per, self.n
        self.n = 0

    def leave(self, trips):
        assert self.n == self.per, (self.n, self.per)
        self.n, self.i = self.base + trips * self.per, None

    def done(self, ins):
        ins.then_inc(self.sem, 1)
        self.n += 1

    def wait(self):
        if self.i is None:
            self.eng.wait_ge(self.sem, self.n)
        else:
            self.eng.wait_ge(self.sem, self.i * self.per + (self.base + self.n))

    def step(self, ins):
        self.done(ins)
        self.wait()


def decoder(nc, A, out):
    with ExitStack() as ctx:
        def sb(name, shape, dt=F32, where=ctx):
            return where.enter_context(nc.sbuf_tensor(name, shape, dt))

        def sem(name):
            return ctx.enter_context(nc.semaphore(name))

        PS = ctx.enter_context(nc.psum_tensor("PS", [P, 8, 512], F32))

        def bank(k, b=HB, t=T, rows=slice(0, P)):
            return PS[rows, k, 0:b * t].rearrange("p (b t) -> p b t", t=t)

        xT = sb("xT", [P, KC, B, TP])
        xn = sb("xn", [P, KC, B, TP])
        xc = sb("xc", [P, KC, NT])
        sq = sb("sq", [P, KC, NT])
        std = sb("std", [P, NT])
        avg = sb("avg", [P, P])
        ident = sb("ident", [P, P])
        epsc = sb("epsc", [P, 1])

        def half(t, c, hf):
            return t[:, c, HB * hf:HB * hf + HB, 0:T]

        def cols(t):
            return t.rearrange("p (b t) -> p b t", t=T)

        wzx = sb("wzx", [P, KC, 2 * DI])
        wbc = sb("wbc", [P, KC, 4, P])
        wdt = sb("wdt", [P, KC, NH])
        wmo = sb("wmo", [P, DI // P, C])
        sel = sb("sel", [NH, NH // 2, 2])
        sgn = sb("sgn", [NH, P])
        eye = sb("eye", [P, 2 * PAIRS * T])
        frow = sb("frow", [NH, P])
        bias = sb("bias", [P, 4, NH // 2])
        dtb = sb("dtb", [NH, 1])
        alog = sb("alog", [NH, 1])
        dbc = sb("dbc", [P, NH])
        nw = sb("nw", [P, DI // P])
        keept = sb("keept", [NH, NT])
        cst = sb("cst", [P, 4])
        rqt = sb("rqt", [RQ, 4, T])
        p2 = ExitStack()
        w0 = sb("w0", [P, KC, 2 * C], where=p2)
        b0 = sb("b0", [P, 4], where=p2)
        gate_s = sb("gate_s", [P, KC, NT], where=p2)
        val_s = sb("val_s", [P, KC, NT], where=p2)
        hid = sb("hid", [P, KC, NT], where=p2)

        wxq = sb("wxq", [P, KC, XH * XDP], where=p2)
        wxk = sb("wxk", [64, XH * XDP], where=p2)
        wxv = sb("wxv", [64, C], where=p2)
        wxo = sb("wxo", [P, 4, C], where=p2)
        ctxs = sb("ctxs", [64, B, TP], where=p2)
        ctxp = sb("ctxp", [64, 2, 2, TP], where=p2)
        maskc = sb("maskc", [P, T], where=p2)
        qp = sb("qp", [P, 4, 2, TP], where=p2)
        kp = sb("kp", [P, 4, 2, TP], where=p2)
        vp = sb("vp", [P, 2, XH, XDP], where=p2)
        sc = sb("sc", [P, XH, T], where=p2)
        pr = sb("pr", [P, XH, TP], where=p2)
        mxs = sb("mxs", [P, XH], where=p2)
        sms = sb("sms", [P, XH], where=p2)
        pt = sb("pt", [P, 8, P], where=p2)
        oT = sb("oT", [P, 4, B, TP], where=p2)

        wr = sb("wr", [P, KC, E], where=p2)
        wg = sb("wg", [P, KC, KB * P], where=p2)
        wu = sb("wu", [P, KC, KB * P], where=p2)
        wd = sb("wd", [P, C], where=p2)
        wsg = sb("wsg", [P, KC, C], where=p2)
        wsu = sb("wsu", [P, KC, C], where=p2)
        wsd = sb("wsd", [P, KC, C], where=p2)
        amps = sb("amps", [P, 2, KB], where=p2)
        escale = sb("escale", [P, 1], where=p2)
        mix = sb("mix", [P, KB], where=p2)
        mixb = sb("mixb", [P, KB, P], where=p2)
        msum = sb("msum", [P, 1], where=p2)
        keep = sb("keep", [P, PAIRS * E], where=p2)
        logit = sb("logit", [P, PAIRS, E], where=p2)
        top8 = sb("top8", [P, PAIRS, 8], where=p2)
        above = sb("above", [P, PAIRS, E], where=p2)
        level = sb("level", [P, PAIRS, E], where=p2)
        place = sb("place", [P, PAIRS, E], where=p2)
        expo = sb("expo", [P, PAIRS, E], where=p2)
        room = sb("room", [P, PAIRS], where=p2)
        zsum = sb("zsum", [P, PAIRS], where=p2)
        tsum = sb("tsum", [P, PAIRS], where=p2)
        coT = sb("coT", [P, B, TP], where=p2)
        sgl = sb("sgl", [P, 2, NT], where=p2)
        gu = sb("gu", [P, 2, NT], where=p2)
        wgu = sb("wgu", [P, NT], where=p2)
        acc = sb("acc", [P, 2, NT], where=p2)
        shr = sb("shr", [P, 2, 2, NT], where=p2)
        p2.close()
        p4 = ExitStack()
        dtc = sb("dtc", [NH, B, TP], where=p4)
        cum = sb("cum", [NH, B * T], where=p4)
        aT = sb("aT", [NH, B, T], where=p4)
        dtt = sb("dtt", [P, PAIRS, NH], where=p4)
        bcn = sb("bcn", [P, 4, BT], where=p4)
        siz = sb("siz", [P, PAIRS, DI], where=p4)
        dx = sb("dx", [P, PAIRS, DI], where=p4)
        ua = sb("ua", [P, PAIRS, DI], where=p4)
        ya = ua
        f2 = sb("f2", [NH, 2, P], where=p4)
        uh = sb("uh", [P, 2, PAIRS, 2 * HD], where=p4)
        turn = sb("turn", [P, BT], where=p4)
        frac = sb("frac", [P, 2, BT], where=p4)
        absf = sb("absf", [P, BT], where=p4)
        sn = sb("sn", [P, 2, BT], where=p4)
        cs = sb("cs", [P, 2, BT], where=p4)
        rt = sb("rt", [P, 4, BT], where=p4)
        rb = sb("rb", [P, 2, BT + 8], where=p4)
        rc = sb("rc", [P, 2, BT + 8], where=p4)
        ab = sb("ab", [P, 2, BT], where=p4)
        dec = sb("dec", [P, BT], where=p4)
        mt = sb("mt", [P, 2, BT + 8], where=p4)
        yss = sb("yss", [P, PAIRS], where=p4)
        bsq, bst = frac[:, 0, 0:NT], frac[:, 1, 0:NT]
        dts = cs[0:NH].rearrange("p s (k n) -> p (s k) n", k=2)
        gT = rt
        ysq = frac
        p4.close()
        p5 = ExitStack()
        rkc = sb("rkc", [KP, KT, DC], where=p5)
        rks = sb("rks", [KP, KT, DC], where=p5)
        lwq = sb("lwq", [P, 2, KC, P], where=p5)
        lwc = sb("lwc", [P, 2, 2 * RQ], where=p5)
        lwr = sb("lwr", [DC, 2, 2 * RQ], where=p5)
        lwk = sb("lwk", [DC, 2, P], where=p5)
        lwv = sb("lwv", [P, 2, DC], where=p5)
        lwo = sb("lwo", [P, 2, C], where=p5)
        wab = sb("wab", [RQ, 2, 2, P], where=p5)
        wvo = sb("wvo", [DC, LH, C], where=p5)
        qh = sb("qh", [P, 2, NT], where=p5)
        rp4 = sb("rp4", [RQ, 4, NT], where=p5)
        rot = sb("rot", [RQ, 2, 2, NT], where=p5)
        qa = sb("qa", [P, B, LH, T], F16, where=p5)
        kvx = sb("kvx", [KP, 2, KT, DC], where=p5)
        kvr = sb("kvr", [KP, 2, KT, 2 * DC + 1], where=p5)
        kvt = sb("kvt", [KP, KT, DC], where=p5)
        khi = sb("khi", [P, 2, S], F16, where=p5)
        klo = sb("klo", [DC + 1, 2, S], F16, where=p5)
        qb1 = sb("qb1", [P, 2, LR], F16, where=p5)
        qb2 = sb("qb2", [DC + 1, 2, LR], F16, where=p5)
        rmx = sb("rmx", [2 * T, LH // 2], where=p5)
        rmn = sb("rmn", [LH // 2, 2 * T], F16, where=p5)
        pe3 = sb("pe3", [KP, 3, NT], where=p5)
        cx = sb("cx", [DC + 1, 2, NT], where=p5)
        rden = sb("rden", [DC + 1, 2, NT], where=p5)
        cn = sb("cn", [DC, LH, T], where=p5)
        ones = sb("ones", [P, P], where=p5)
        p5.close()
        p6 = ExitStack()
        xt = sb("xt", [P, PAIRS, C], where=p6)
        xq = sb("xq", [P, PAIRS, C], where=p6)
        xi = sb("xi", [P, PAIRS, C], BF16, where=p6)
        xiT = sb("xiT", [P, KC, PAIRS * P], BF16, where=p6)
        kw = sb("kw", [P, KC, C], where=p6)
        kwi = sb("kwi", [P, KC, C], BF16, where=p6)
        kwT = sb("kwT", [P, KC, C], BF16, where=p6)
        kdg = sb("kdg", [P, KC, P], where=p6)
        skb = sb("skb", [P, C], where=p6)
        bq = sb("bq", [P, C], where=p6)
        bqi = sb("bqi", [P, C], where=p6)
        one6 = sb("one6", [P, P], where=p6)
        identb = sb("identb", [P, P], BF16, where=p6)
        st6 = sb("st6", [P, PAIRS, 6], where=p6)
        mv6 = sb("mv6", [P, PAIRS, 2], where=p6)
        sx = sb("sx", [P, 4, PAIRS], where=p6)
        sk = sb("sk", [P, 4, KC], where=p6)
        sbq = sb("sbq", [P, 4], where=p6)
        sy = sb("sy", [P, 4, PAIRS], where=p6)
        y6 = sb("y6", [P, PAIRS, C], where=p6)
        p6.close()
        s_x = sem("x_loaded")
        s_w1 = sem("w1_loaded")
        s_w2 = sem("w2_loaded")
        s_const = sem("const_ready")
        s_xr = sem("x_ready")
        s_mean = sem("ln_mean")
        s_cen = sem("ln_centred")
        s_sq = sem("ln_squared")
        s_var = sem("ln_var")
        s_std = sem("ln_std")
        s_xn = sem("ln_out")
        own_v = sem("vector_own")
        own_a = sem("scalar_own")
        own_g = sem("gpsimd_own")
        s_par = sem("l0_params")
        s_pact = sem("l0_activated")
        x_cp = sem("xa_ctx_copied")
        x_qm, x_km, x_vm = sem("xa_q_mm"), sem("xa_k_mm"), sem("xa_v_mm")
        x_qc, x_kc, x_vc = sem("xa_q_copied"), sem("xa_k_copied"), sem("xa_v_copied")
        x_sm, x_sh, x_ex, x_pr = sem("xa_scores"), sem("xa_shifted"), sem("xa_exp"), sem("xa_probs")
        x_tm, x_tc = sem("xa_pt_mm"), sem("xa_pt_copied")
        x_om, x_oc, x_wm = sem("xa_o_mm"), sem("xa_o_copied"), sem("xa_out_mm")
        s_gate = sem("tensor_gate")
        s_out = sem("stored")
        s_w3 = sem("w3_loaded")
        s_keep = sem("moe_keep")
        e_mix = sem("moe_mix")
        e_lm, e_lc, e_sh, e_ex, e_co = sem("moe_logits"), sem("moe_logits_copied"), sem("moe_shifted"), sem("moe_exp"), sem("moe_coeff")
        e_tm, e_tc = sem("moe_coT_mm"), sem("moe_coT")
        e_gm, e_um, e_si, e_pd = sem("moe_gate_mm"), sem("moe_up_mm"), sem("moe_silu"), sem("moe_product")
        e_ac, e_dm = sem("moe_acc"), sem("moe_down_mm")
        a_scr = nc.dram_tensor("decay_scratch", (NH // 2, 2, PAIRS, 2, T), F32, kind="Internal").ap()
        s_w4 = sem("w4_loaded")
        s_c4 = sem("ssm_const")
        d_mm, d_abs, d_th, d_ln, d_dt, d_cum = (sem("ssm_" + n) for n in ("dt_mm", "dt_abs", "dt_tanh", "dt_ln", "dt", "cum"))
        d_ng, d_ex, d_a, d_st = (sem("ssm_" + n) for n in ("neg_a", "decay_exp", "decay", "decay_stored"))
        d_tm, d_tc = sem("ssm_dtt_mm"), sem("ssm_dtt")
        b_mm, b_sq, b_ms, b_sd, b_n = (sem("ssm_bc_" + n) for n in ("mm", "squared", "mean", "std", "normed"))
        z_mm, z_si, z_u = sem("ssm_zx_mm"), sem("ssm_silu"), sem("ssm_u")
        m_f2, m_u, m_phi, m_fr, m_ab, m_sin = (sem("ssm_" + n) for n in ("f2", "uh", "phi", "frac", "absf", "sin"))
        m_tb, m_tc, m_rb, m_rc, m_sc = (sem("ssm_" + n) for n in ("tb", "tc", "rotB", "rotC", "scan"))
        m_abc = [sem(f"ssm_a_bcast_{n}") for n in range(2)]
        m_g, m_mt, m_y, m_yc = (sem("ssm_" + n) for n in ("g", "mt", "y", "y_copied"))
        g_g, g_sq, g_sd, g_n, g_tm, g_tc, g_wm = (sem("ssm_out_" + n) for n in ("gated", "squared", "std", "normed", "t_mm", "t", "mm"))
        s_w5, s_c5 = sem("w5_loaded"), sem("latent_const")
        k_ld = [sem(f"lq_weights_{n}") for n in range(2)]
        k_w, k_wc, k_q, k_qc, k_b, k_p, k_r, k_a, k_hi, k_lo = (sem("lq_" + n) for n in (
            "w_mm", "w_copied", "proj", "proj_copied", "big", "products", "rotated", "abs_mm", "high", "low"))
        c_ld = [sem(f"kv_loaded_{n}") for n in range(2)]
        c_row = [sem(f"max_row_{n}") for n in range(2)]
        c_rp, c_tm, c_khi, c_klo, c_qb, c_mm, c_mr, c_mt, c_mn = (sem("la_" + n) for n in (
            "roped", "kT_mm", "k_high", "k_low", "q_slot", "max_mm", "max", "max_t", "max_neg"))
        c_sm, c_ex, c_pv, c_cx, c_rd, c_bc, c_cn, c_om, c_xu = (sem("la_" + n) for n in (
            "scores", "exp", "pv", "ctx_copied", "recip", "recip_bcast", "ctx_normed", "out_mm", "x_updated"))
        s_w6, s_c6 = sem("w6_loaded"), sem("ffn_const")
        f_xm, f_xc, f_va, f_sd, f_xi = (sem("ffn_" + n) for n in ("x_mm", "x_copied", "variance", "std", "x_int"))
        f_tm, f_tc, f_ki, f_km, f_kc, f_ym = (sem("ffn_" + n) for n in ("xT_mm", "xT", "k_int", "k_mm", "k_ready", "y_mm"))
        f_o = sem("ffn_out")
        block = ctx.enter_context(nc.Block())

        @block.sync
        def _(sp):
            sp.dma_start(xT[:], A["xT"].rearrange("(c p) b t -> p c b t", p=P)).then_inc(s_x, 16)
            sp.dma_start(w0[:], A["W0"].rearrange("(c p) n -> p c n", p=P)).then_inc(s_w1, 16)
            sp.dma_start(b0[:], A["b0"]).then_inc(s_w1, 16)
            sp.dma_start(wxq[:], A["Wxq"].rearrange("(c p) n -> p c n", p=P)).then_inc(s_w2, 16)
            sp.dma_start(wxk[:], A["Wxk"]).then_inc(s_w2, 16)
            sp.dma_start(wxv[:], A["Wxv"]).then_inc(s_w2, 16)
            sp.dma_start(wxo[:], A["Wxo"].rearrange("(c p) n -> p c n", p=P)).then_inc(s_w2, 16)
            sp.dma_start(ctxs[:], A["ctx56"]).then_inc(s_w2, 16)
            sp.dma_start(maskc[:], A["causal"]).then_inc(s_w2, 16)
            sp.dma_start(wr[:], A["Wr"].rearrange("(c p) n -> p c n", p=P)).then_inc(s_w3, 16)
            sp.dma_start(wg[:], A["Wg"].rearrange("(c p) n -> p c n", p=P)).then_inc(s_w3, 16)
            sp.dma_start(wu[:], A["Wu"].rearrange("(c p) n -> p c n", p=P)).then_inc(s_w3, 16)
            sp.dma_start(wd[:], A["Wd"]).then_inc(s_w3, 16)
            sp.dma_start(wsg[:], A["Wsg"].rearrange("(c p) n -> p c n", p=P)).then_inc(s_w3, 16)
            sp.dma_start(wsu[:], A["Wsu"].rearrange("(c p) n -> p c n", p=P)).then_inc(s_w3, 16)
            sp.dma_start(wsd[:], A["Wsd"].rearrange("(c p) n -> p c n", p=P)).then_inc(s_w3, 16)
            sp.dma_start(amps[:], A["amps"]).then_inc(s_w3, 16)
            sp.dma_start(escale[:], A["escale"]).then_inc(s_w3, 16)
            for t, src in ((wzx, A["Wzx"].rearrange("(c p) n -> p c n", p=P)), (wbc, A["Wbc"].rearrange("(c p) k n -> p c k n", p=P)),
                           (wdt, A["Wdt"].rearrange("(c p) n -> p c n", p=P)),
                           (wmo, A["Wmo"].rearrange("(c p) n -> p c n", p=P)), (sel, A["sel"]), (eye, A["eye"]),
                           (frow, A["frow"]), (sgn, A["sgn"]), (bias, A["bcbias"]), (dtb, A["dtb"]), (alog, A["alog"]),
                           (dbc, A["Dp"].broadcast_to((P, NH))), (nw, A["nw"])):
                sp.dma_start(t[:], src).then_inc(s_w4, 16)
            sp.wait_ge(d_a, 2)
            for h2 in range(2):
                for b2 in range(2):
                    sp.dma_start(a_scr[:, b2, :, h2, :], aT[h2::2, b2::2, :]).then_inc(d_st, 16)
            sp.wait_ge(d_st, 64)

            def ssm_load(hp, slot):
                for b2 in range(2):
                    src = a_scr[hp, b2] if isinstance(hp, int) else a_scr[bass.ds(hp, 1), b2]
                    src = src.rearrange("i h t -> (i h t)") if isinstance(hp, int) else src.rearrange("o i h t -> o (i h t)")
                    if isinstance(hp, int):
                        src = src.unsqueeze(0)
                    sp.dma_start(ab[64 * b2:64 * b2 + 64, slot, :], src.broadcast_to((64, BT))).then_inc(m_abc[slot], 16)

            for hp in range(3):
                if hp >= 2:
                    sp.wait_ge(m_sc, hp - 1)
                ssm_load(hp, hp % 2)
            with sp.Fori(0, SSM_TRIPS) as j:
                for d in range(2):
                    sp.wait_ge(m_sc, 2 * j + (2 + d))
                    ssm_load(2 * j + 3 + d, (1 + d) % 2)
            sp.wait_ge(m_sc, NH // 2 - 2)
            ssm_load(NH // 2 - 1, 1)
            sp.dma_start(rqt[:], A["rqt"]).then_inc(s_w5, 16)
            sp.wait_ge(s_xr, 10)
            sp.dma_start(rkc[:], A["rkc"]).then_inc(s_w5, 16)
            sp.dma_start(rks[:], A["rks"]).then_inc(s_w5, 16)

            def latent_weights(h, slot):
                hs = slice(h, h + 1) if isinstance(h, int) else bass.ds(h, 1)
                for t, a in ((lwq[:, slot, :, :], A["Lwq"][hs].rearrange("o p c n -> p (o c) n")),
                             (lwc[:, slot, :], A["Lwc"][hs].rearrange("o p n -> p (o n)")),
                             (lwr[:, slot, :], A["Lwr"][hs].rearrange("o p n -> p (o n)")),
                             (lwk[:, slot, :], A["Lwk"][hs].rearrange("o p n -> p (o n)")),
                             (lwv[:, slot, :], A["Lwv"][hs].rearrange("o p n -> p (o n)")),
                             (lwo[:, slot, :], A["Lwo"][hs].rearrange("o p n -> p (o n)"))):
                    sp.dma_start(t, a).then_inc(k_ld[slot], 16)

            def latent_context(b, slot):
                bs = slice(b, b + 1) if isinstance(b, int) else bass.ds(b, 1)
                sp.dma_start(kvx[:, slot, :, :].rearrange("p j d -> p (j d)"),
                             A["ctx"][bs].rearrange("o (p j) d -> (o p) (j d)", j=KT)).then_inc(c_ld[slot], 16)

            latent_weights(0, 0)
            latent_weights(1, 1)
            latent_context(0, 0)
            latent_context(1, 1)
            with sp.Fori(0, LH // 2 - 1) as j:
                for d in range(2):
                    sp.wait_ge(k_b, 4 * j + (2 + 2 * d))
                    latent_weights(2 * j + (2 + d), d)
            with sp.Fori(0, B // 2 - 1) as j:
                for d in range(2):
                    sp.wait_ge(c_rp, 2 * j + (1 + d))
                    latent_context(2 * j + (2 + d), d)
            sp.wait_ge(s_xr, 11)
            sp.dma_start(kw[:], A["kT"].rearrange("(c p) d -> p c d", p=P)).then_inc(s_w6, 16)
            sp.dma_start(bq[:], A["fb"].broadcast_to((P, C))).then_inc(s_w6, 16)
            for i in range(PAIRS):
                sp.wait_ge(f_o, i + 1)
                for b2 in range(2):
                    sp.dma_start(out[2 * i + b2], y6[64 * b2:64 * b2 + T, i, :]).then_inc(s_out, 16)
            sp.wait_ge(s_out, 16 * B)

        def ln_pe(pe, k):
            for hf in range(2):
                pe.wait_ge(s_xr, 2 * k + hf + 1)
                for c in range(KC):
                    mm = pe.matmul(bank(hf), avg[:], half(xT, c, hf), start=c == 0, stop=c == KC - 1)
                mm.then_inc(s_mean, 1)
            for hf in range(2):
                pe.wait_ge(s_sq, 2 * k + hf + 1)
                for c in range(KC):
                    mm = pe.matmul(bank(2 + hf), avg[:], cols(sq[:, c, :]), start=c == 0, stop=c == KC - 1)
                mm.then_inc(s_var, 1)

        def ln_act(act, k):
            for hf in range(2):
                act.wait_ge(s_cen, 2 * k + hf + 1)
                if hf == 1:
                    act.wait_ge(s_var, 2 * k + 1)
                act.activation(sq[:], xc[:], ACT.Square).then_inc(s_sq, 1)
                act.wait_ge(s_var, 2 * k + hf + 1)
                act.activation(std[:], PS[:, 2 + hf, 0:NT], ACT.Sqrt, bias=epsc[:]).then_inc(s_std, 1)

        def ln_dve(v, own, k):
            for hf in range(2):
                v.wait_ge(s_mean, 2 * k + hf + 1)
                for c in range(KC):
                    ins = v.tensor_tensor(cols(xc[:, c, :]), half(xT, c, hf), bank(hf), ALU.subtract)
                ins.then_inc(s_cen, 1)
                v.wait_ge(s_std, 2 * k + hf + 1)
                own.step(v.reciprocal(std[:], std[:]))
                for c in range(KC):
                    ins = v.tensor_tensor(half(xn, c, hf), cols(xc[:, c, :]), cols(std[:]), ALU.mult)
                ins.then_inc(s_xn, 1)
                v.wait_ge(s_xn, 2 * k + hf + 1)

        @block.gpsimd
        def _(g):
            own = Own(g, own_g)
            g.memset(avg[:], 1.0 / C).then_inc(s_const, 1)
            g.memset(epsc[:], LN_EPS).then_inc(s_const, 1)
            g.memset(xn[:], 0.0).then_inc(s_const, 1)
            own.step(g.memset(ident[:], 0.0))
            g.affine_select(out=ident[:], in_=ident[:], compare_op=ALU.not_equal, fill=1.0, base=0,
                            pattern=[[-1, P]], channel_multiplier=1).then_inc(s_const, 1)
            g.memset(vp[:], 0.0).then_inc(s_const, 1)
            g.memset(pr[:], 0.0).then_inc(s_const, 1)
            g.wait_ge(s_w2, 16 * 6)
            for b in range(2):
                ins = g.tensor_copy(ctxp[:, :, b, :], ctxs[:, 0:2, :])
            ins.then_inc(x_cp, 1)
            with g.Fori(0, PAIRS - 1) as i:
                g.wait_ge(x_vm, i + 1)
                for b in range(2):
                    ins = g.tensor_copy(ctxp[:, :, b, :], ctxs[:, bass.ds(2 * i + 2, 2), :])
                ins.then_inc(x_cp, 1)
            own.step(g.memset(keep[:], 1.0))
            g.memset(keep[:].rearrange("p (i e) -> p i e", e=E)[:, :, 0:1], 0.0).then_inc(s_keep, 1)
            own.step(g.memset(keept[:], 1.0))
            g.memset(cols(keept[:])[:, :, 0:1], 0.0).then_inc(s_c4, 1)
            for n, c in enumerate((0.5, 1e-6, HALF_PI, 0.0)):
                g.memset(cst[:, n:n + 1], c).then_inc(s_c4, 1)
            g.wait_ge(s_xr, 8)
            g.memset(dtc[:], 0.0).then_inc(s_c4, 1)
            g.memset(rb[:], 0.0).then_inc(s_c4, 1)
            g.memset(rc[:], 0.0).then_inc(s_c4, 1)
            g.memset(mt[:], 0.0).then_inc(s_c4, 1)
            g.wait_ge(s_c4, 9)
            g.wait_ge(s_w4, 16 * 13)
            own.step(g.tensor_tensor(frow[:], frow[:], sgn[:], ALU.mult))
            g.wait_ge(z_u, PAIRS)

            def ssm_rotate(hp, slot):
                if not isinstance(hp, int) or hp >= 2:
                    g.wait_ge(m_phi, hp - 1)
                    g.wait_ge(m_y, hp - 1)
                s = sel[:, hp, :] if isinstance(hp, int) else sel[:, bass.ds(hp, 1), :].rearrange("p o h -> p (o h)")
                g.tensor_tensor(f2[:, slot, :].rearrange("p (h n) -> p h n", h=2), frow[:].rearrange("p (h n) -> p h n", h=2),
                                s.unsqueeze(2).broadcast_to((NH, 2, DS)), ALU.mult).then_inc(m_f2, 1)
                at = slice(hp * 2 * HD, (hp + 1) * 2 * HD) if isinstance(hp, int) else bass.ds(hp * (2 * HD), 2 * HD)
                g.tensor_copy(uh[:, slot, :, :], ua[:, :, at]).then_inc(m_u, 1)
                g.wait_ge(m_tb, hp + 1)
                g.tensor_tensor(rb[:, slot, 0:BT], rt[:, 0, :], rt[:, 1, :], ALU.add).then_inc(m_rb, 1)
                g.wait_ge(m_tc, hp + 1)
                g.tensor_tensor(rc[:, slot, 0:BT], rt[:, 2, :], rt[:, 3, :], ALU.add).then_inc(m_rc, 1)

            for hp in range(3):
                ssm_rotate(hp, hp % 2)
            with g.Fori(0, SSM_TRIPS) as j:
                for d in range(2):
                    ssm_rotate(2 * j + 3 + d, (1 + d) % 2)
            ssm_rotate(NH // 2 - 1, 1)
            g.wait_ge(s_xr, 10)
            g.memset(kvr[:, :, :, 2 * DC:2 * DC + 1], 1.0).then_inc(s_c5, 1)
            g.wait_ge(s_c5, 1)
            g.memset(klo[DC:DC + 1, :, :], 1.0).then_inc(s_c5, 1)
            g.wait_ge(s_c5, 2)
            g.memset(ones[:], 1.0).then_inc(s_c5, 1)
            g.wait_ge(s_c5, 3)
            g.wait_ge(s_w5, 48)

            def rope_context(b, slot, nth):
                g.wait_ge(c_ld[slot], 16 * nth)
                if not isinstance(b, int) or b >= 2:
                    g.wait_ge(c_pv, LS * b - (LS - 3))
                kx, kr = kvx[:, slot, :, :], kvr[:, slot, :, 0:DC]
                own.done(g.tensor_tensor(kvt[:, :, 0:DC // 2], kx[:, :, DC // 2:DC], rks[:, :, 0:DC // 2], ALU.mult))
                own.done(g.tensor_tensor(kvt[:, :, DC // 2:DC], kx[:, :, 0:DC // 2], rks[:, :, DC // 2:DC], ALU.mult))
                own.step(g.tensor_tensor(kr, kx, rkc[:], ALU.mult))
                own.done(g.tensor_tensor(kvr[:, slot, :, DC:2 * DC], kr, kvt[:], ALU.add))
                own.step(g.tensor_tensor(kr, kr, kvt[:], ALU.add))
                g.sem_inc(c_rp, 1)

            def rotate_queries(h, hf):
                g.wait_ge(k_p, 2 * h + (hf + 1))
                if not isinstance(h, int) or h >= 1:
                    g.wait_ge(k_a, 2 * h + (hf - 1))
                for r in range(2):
                    ins = g.tensor_tensor(rot[:, hf, r, :], rp4[:, 2 * r, :], rp4[:, 2 * r + 1, :], ALU.add)
                ins.then_inc(k_r, 1)

            for hf in range(2):
                rotate_queries(0, hf)
            with g.Fori(1, LH) as h:
                for hf in range(2):
                    rotate_queries(h, hf)
            rope_context(0, 0, 1)
            rope_context(1, 1, 1)
            with g.Fori(0, B // 2 - 1) as j:
                own.enter(j, 10)
                for d in range(2):
                    rope_context(2 * j + (2 + d), d, j + 2)
            own.leave(B // 2 - 1)
            g.wait_ge(s_xr, 11)
            g.memset(one6[:], 1.0).then_inc(s_c6, 1)
            g.tensor_copy(identb[:], ident[:]).then_inc(s_c6, 1)

        @block.tensor
        def _(pe):
            pe.wait_ge(s_const, 6)
            ln_pe(pe, 0)
            pe.wait_ge(s_w1, 32)
            for hf in range(2):
                pe.wait_ge(s_xn, hf + 1)
                for m in range(4):
                    if hf == 1:
                        pe.wait_ge(s_pact, m + 1)
                    for c in range(KC):
                        mm = pe.matmul(bank(4 + m), w0[:, c, m * P:(m + 1) * P], half(xn, c, hf),
                                       start=c == 0, stop=c == KC - 1)
                    mm.then_inc(s_par, 1)
            ln_pe(pe, 1)
            pe.wait_ge(s_w2, 16 * 6)
            pe.wait_ge(s_xn, 4)
            with pe.Fori(0, PAIRS) as i:
                for m in range(4):
                    for c in range(KC):
                        mm = pe.matmul(PS[:, 0, m * P:(m + 1) * P], wxq[:, c, m * P:(m + 1) * P],
                                       xn[:, c, bass.ds(2 * i, 2), :], start=c == 0, stop=c == KC - 1)
                mm.then_inc(x_qm, 1)
                for m in range(4):
                    mm = pe.matmul(PS[:, 1, m * P:(m + 1) * P], wxk[:, m * P:(m + 1) * P],
                                   ctxs[:, bass.ds(2 * i, 2), :], start=True, stop=True)
                mm.then_inc(x_km, 1)
                pe.wait_ge(x_cp, i + 1)
                pe.wait_ge(x_oc, i + 1)
                for b in range(2):
                    mm = pe.matmul(PS[:, 2, b * C:(b + 1) * C], ctxp[:, b, :, :], wxv[:],
                                   start=True, stop=True)
                mm.then_inc(x_vm, 1)
                pe.wait_ge(x_qc, i + 1)
                pe.wait_ge(x_kc, i + 1)
                for c in range(4):
                    for r in range(4):
                        rows = slice(32 * r, 32 * r + 32)
                        for b in range(2):
                            mm = pe.matmul(PS[64 * b:64 * b + 64, 4 + r, TP * c:TP * c + T],
                                           qp[rows, c, b, :], kp[rows, c, b, 0:T], start=True, stop=True)
                mm.then_inc(x_sm, 1)
                pe.wait_ge(x_pr, i + 1)
                for m in range(8):
                    mm = pe.transpose(PS[:, m // 4, (m % 4) * P:(m % 4) * P + P],
                                      pr[:, 2 * m:2 * m + 2, :], ident[:])
                mm.then_inc(x_tm, 1)
                pe.wait_ge(x_vc, i + 1)
                pe.wait_ge(x_tc, i + 1)
                pe.sem_inc(s_gate, 1)
                for m in range(8):
                    for e in range(2):
                        r, c = m // 2, 2 * (m % 2) + e
                        for b in range(2):
                            rows = slice(64 * e, 64 * e + T)
                            at = (c // 2 * 2 + b) * T
                            mm = pe.matmul(PS[32 * r:32 * r + 32, 2 + e, at:at + T], vp[rows, b, 4 * c + r, :],
                                           pt[rows, m, 64 * b:64 * b + T], start=True, stop=True)
                mm.then_inc(x_om, 1)
            for hf in range(2):
                pe.wait_ge(x_oc, PAIRS + 1)
                for m in range(KC):
                    for c in range(4):
                        mm = pe.matmul(bank(4 + 2 * hf + m), wxo[:, c, m * P:(m + 1) * P], half(oT, c, hf),
                                       start=c == 0, stop=c == 3)
                    mm.then_inc(x_wm, 1)
            ln_pe(pe, 2)
            pe.wait_ge(s_w3, 16 * 9)
            pe.wait_ge(s_xn, 6)
            for i in range(PAIRS):
                for c in range(KC):
                    mm = pe.matmul(PS[:, 4 + i // 4, (i % 4) * E:(i % 4) * E + E],
                                   xn[:, c, 2 * i:2 * i + 2, :], wr[:, c, :], start=c == 0, stop=c == KC - 1)
            mm.then_inc(e_lm, 1)
            pe.wait_ge(e_co, 1)
            for i in range(PAIRS):
                mm = pe.transpose(PS[:, 6 + i // 4, (i % 4) * P:(i % 4) * P + P], expo[:, i, :], ident[:])
            mm.then_inc(e_tm, 1)
            pe.wait_ge(e_tc, 1)
            pe.wait_ge(e_mix, 1)
            for hf in range(2):
                for k in range(KB + 2):
                    n = hf * (KB + 2) + k
                    gb = 3 * (n % 2)
                    if n >= 2:
                        pe.wait_ge(e_pd, n - 1)
                    w, u, j = (wg, wu, k) if k < KB else (wsg, wsu, k - KB)
                    for c in range(KC):
                        mm = pe.matmul(bank(gb), w[:, c, j * P:(j + 1) * P], half(xn, c, hf),
                                       start=c == 0, stop=c == KC - 1)
                    mm.then_inc(e_gm, 1)
                    for c in range(KC):
                        mm = pe.matmul(bank(gb + 1), u[:, c, j * P:(j + 1) * P], half(xn, c, hf),
                                       start=c == 0, stop=c == KC - 1)
                    if k < KB:
                        mm = pe.matmul(bank(gb + 2), mixb[:, k, :], coT[:, HB * hf:HB * hf + HB, 0:T],
                                       start=True, stop=True)
                    mm.then_inc(e_um, 1)
            for hf in range(2):
                pe.wait_ge(e_ac, hf + 1)
                if hf == 1:
                    pe.wait_ge(s_xr, 7)
                for m in range(KC):
                    pe.matmul(bank(6 + m), wd[:, m * P:(m + 1) * P], cols(acc[:, hf, :]), start=True, stop=False)
                    for c in range(KC):
                        mm = pe.matmul(bank(6 + m), wsd[:, c, m * P:(m + 1) * P], cols(shr[:, hf, c, :]),
                                       start=False, stop=c == KC - 1)
                    mm.then_inc(e_dm, 1)
            ln_pe(pe, 3)
            pe.wait_ge(s_w4, 16 * 13)
            pe.wait_ge(s_xn, 8)
            for hf in range(2):
                for c in range(KC):
                    mm = pe.matmul(bank(6 + hf, rows=slice(0, NH)), wdt[:, c, :], half(xn, c, hf),
                                   start=c == 0, stop=c == KC - 1)
                mm.then_inc(d_mm, 1)
            for n in range(4):
                hf, x, bb = n // 2, n % 2, 3 * (n % 2)
                if n >= 2:
                    pe.wait_ge(b_n, n - 1)
                for s in range(2):
                    for c in range(KC):
                        mm = pe.matmul(bank(bb + s), wbc[:, c, 2 * x + s, :], half(xn, c, hf),
                                       start=c == 0, stop=c == KC - 1)
                mm.then_inc(b_mm, 1)
                pe.wait_ge(b_sq, n + 1)
                pe.matmul(bank(bb + 2), avg[:], cols(bsq), start=True, stop=True).then_inc(b_ms, 1)
            pe.wait_ge(s_c4, 9)
            pe.wait_ge(d_dt, 2)
            for i in range(PAIRS):
                mm = pe.transpose(PS[:, 6, i * NH:(i + 1) * NH], dtc[:, 2 * i:2 * i + 2, :], ident[0:NH, 0:NH])
            mm.then_inc(d_tm, 1)
            pe.wait_ge(b_n, 4)
            for i in range(PAIRS):
                zb = 2 * (i % 2)
                if i >= 2:
                    pe.wait_ge(z_si, i - 1)
                    pe.wait_ge(z_u, i - 1)
                for s in range(2):
                    for c in range(KC):
                        mm = pe.matmul(PS[:, zb + s, :], xn[:, c, 2 * i:2 * i + 2, :], wzx[:, c, s * DI:(s + 1) * DI],
                                       start=c == 0, stop=c == KC - 1)
                mm.then_inc(z_mm, 1)
            pe.wait_ge(z_u, PAIRS)
            pe.wait_ge(z_si, PAIRS)

            def ssm_angle(hp, slot):
                if not isinstance(hp, int) or hp >= 1:
                    pe.wait_ge(m_fr, hp)
                pe.wait_ge(m_f2, hp + 1)
                for hf in range(2):
                    mm = pe.matmul(PS[:, hf, 0:NT], f2[:, slot, :], cum[:, hf * NT:(hf + 1) * NT], start=True, stop=True)
                mm.then_inc(m_phi, 1)

            def ssm_mix(hp, slot):
                if not isinstance(hp, int) or hp >= 1:
                    pe.wait_ge(m_mt, hp)
                pe.wait_ge(m_rb, hp + 1)
                pe.wait_ge(m_rc, hp + 1)
                pe.sem_inc(s_gate, 1)
                for b in range(B):
                    for h2 in range(2):
                        rows = slice(64 * h2, 64 * h2 + 64)
                        mm = pe.matmul(PS[64 * (b % 2):64 * (b % 2) + 64, 2 + h2, b // 2 * T:b // 2 * T + T],
                                       rb[rows, slot, b * T:b * T + TP], rc[rows, slot, b * T:b * T + T],
                                       start=True, stop=True)
                mm.then_inc(m_g, 1)
                if not isinstance(hp, int) or hp >= 1:
                    pe.wait_ge(m_yc, hp)
                pe.wait_ge(m_u, hp + 1)
                pe.wait_ge(m_mt, hp + 1)
                pe.sem_inc(s_gate, 1)
                for i in range(PAIRS):
                    for b2 in range(2):
                        rows = slice(64 * b2, 64 * b2 + 64)
                        for h2 in range(2):
                            at = (2 * i + h2) * HD
                            mm = pe.matmul(PS[rows, 4 + b2, at:at + HD],
                                           mt[rows, slot, (2 * i + h2) * T:(2 * i + h2) * T + TP],
                                           uh[rows, slot, i, h2 * HD:(h2 + 1) * HD], start=True, stop=True)
                mm.then_inc(m_y, 1)

            pe.wait_ge(d_cum, 2)
            ssm_angle(0, 0)
            for hp in range(2):
                ssm_angle(hp + 1, (hp + 1) % 2)
                ssm_mix(hp, hp % 2)
            with pe.Fori(0, SSM_TRIPS) as j:
                for d in range(2):
                    ssm_angle(2 * j + 3 + d, (1 + d) % 2)
                    ssm_mix(2 * j + 2 + d, d % 2)
            ssm_angle(NH // 2 - 1, 1)
            ssm_mix(NH // 2 - 2, 0)
            ssm_mix(NH // 2 - 1, 1)
            for i in range(PAIRS):
                pe.wait_ge(g_n, i + 1)
                if i >= 2:
                    pe.wait_ge(g_tc, i - 1)
                for c in range(DI // P):
                    mm = pe.transpose(PS[:, i % 2, c * P:(c + 1) * P], ya[:, i, c * P:(c + 1) * P], ident[:])
                mm.then_inc(g_tm, 1)
            pe.wait_ge(g_tc, PAIRS)
            for hf in range(2):
                for m in range(KC):
                    for c in range(DI // P):
                        mm = pe.matmul(PS[:, 4 + 2 * hf + m, 0:NT], wmo[:, c, m * P:(m + 1) * P],
                                       gT[:, c, hf * NT:(hf + 1) * NT], start=c == 0, stop=c == DI // P - 1)
                    mm.then_inc(g_wm, 1)
            ln_pe(pe, 4)
            pe.wait_ge(s_c5, 3)
            pe.wait_ge(s_xn, 10)

            def latent_project(h, slot, nth):
                pe.wait_ge(k_ld[slot], 96 * nth)
                if not isinstance(h, int) or h >= 1:
                    pe.wait_ge(k_lo, 2 * h - 1)
                for r in range(2):
                    pe.matmul(PS[0:RQ, 6, r * P:(r + 1) * P], lwr[:, slot, r * RQ:(r + 1) * RQ], lwk[:, slot, :],
                              start=True, stop=True)
                pe.matmul(PS[0:DC, 6, 256:512], lwv[:, slot, :], lwo[:, slot, :], start=True, stop=True).then_inc(k_w, 1)
                if not isinstance(h, int) or h >= 1:
                    pe.wait_ge(k_qc, 2 * h)
                for hf in range(2):
                    for c in range(KC):
                        mm = pe.matmul(bank(hf), lwq[:, slot, c, :], half(xn, c, hf), start=c == 0, stop=c == KC - 1)
                    mm.then_inc(k_q, 1)

            def latent_big(h, slot):
                for hf in range(2):
                    pe.wait_ge(k_qc, 2 * h + (hf + 1))
                    if not isinstance(h, int) or h >= 1:
                        pe.wait_ge(k_p, 2 * h + (hf - 1))
                    for r in range(2):
                        mm = pe.matmul(PS[0:RQ, 2 + 2 * hf + r, 0:NT], lwc[:, slot, r * RQ:(r + 1) * RQ], qh[:, hf, :],
                                       start=True, stop=True)
                    mm.then_inc(k_b, 1)

            def latent_absorb(h, slot, h_w):
                for hf in range(2):
                    pe.wait_ge(k_r, 2 * h + (hf + 1))
                    if hf == 0 and (not isinstance(h, int) or h >= 1):
                        pe.wait_ge(k_lo, 2 * h)
                    if hf == 1:
                        pe.wait_ge(k_wc, h_w)
                    for r in range(2):
                        mm = pe.matmul(PS[:, 7 - hf, 0:NT], wab[:, slot, r, :], rot[:, hf, r, :], start=r == 0, stop=r == 1)
                    mm.then_inc(k_a, 1)

            latent_project(0, 0, 1)
            latent_big(0, 0)
            with pe.Fori(0, LH // 2 - 1) as j:
                for d in range(2):
                    h = 2 * j + (1 + d)
                    latent_project(h, (1 + d) % 2, j + (1 + d))
                    latent_absorb(2 * j + d, d, 2 * j + (2 + d))
                    latent_big(h, (1 + d) % 2)
            latent_project(LH - 1, 1, LH // 2)
            latent_absorb(LH - 2, 0, LH)
            latent_big(LH - 1, 1)
            latent_absorb(LH - 1, 1, LH)

            def keys_t(b, slot):
                pe.wait_ge(c_rp, b + 1)
                if not isinstance(b, int) or b >= 1:
                    pe.wait_ge(c_xu, b)
                for j in range(KT):
                    mm = pe.transpose(PS[:, j // 4, (j % 4) * KP:(j % 4) * KP + KP],
                                      kvr[:, slot, j, 0:2 * DC], ident[0:KP, 0:KP])
                mm.then_inc(c_tm, 1)

            def row_scores(b, slot, k):
                if k == 0:
                    pe.wait_ge(c_khi, b + 1)
                    pe.wait_ge(c_klo, b + 1)
                    pe.wait_ge(c_qb, b + 1)
                else:
                    pe.wait_ge(c_mr, (LH // 2) * b + k)
                for j in range(3):
                    mm = pe.matmul(PS[0:2 * T, j, 0:S // 3], qb2[0:DC, slot, 2 * T * k:2 * T * (k + 1)],
                                   khi[0:DC, slot, j * (S // 3):(j + 1) * (S // 3)], start=True, stop=True)
                mm.then_inc(c_mm, 1)

            def max_t(b):
                pe.wait_ge(c_mr, (LH // 2) * b + LH // 2)
                pe.transpose(PS[0:LH // 2, 2, 0:2 * T], rmx[:], ident[0:2 * T, 0:2 * T]).then_inc(c_mt, 1)

            def scores(b, slot, n):
                j, hf = n // 2, n % 2
                pe.wait_ge(c_ex, LS * b + (n + 1))
                keys = slice(j * KP, (j + 1) * KP)
                cut = slice(hf * NT, (hf + 1) * NT)
                pe.matmul(PS[0:KP, 3 + n % 3, 0:NT], khi[:, slot, keys], qb1[:, slot, cut], start=True, stop=False)
                pe.matmul(PS[0:KP, 3 + n % 3, 0:NT], klo[:, slot, keys], qb2[:, slot, cut],
                          start=False, stop=True).then_inc(c_sm, 1)

            def values(b, slot, n):
                j, hf = n // 2, n % 2
                pe.wait_ge(c_ex, LS * b + (n + 4))
                if n == 0:
                    pe.wait_ge(c_cx, b + 1)
                pe.matmul(PS[0:DC + 1, 6 + hf, 0:NT], kvr[:, slot, j, DC:2 * DC + 1], pe3[:, n % 3, :],
                          start=j == 0, stop=j == KT - 1).then_inc(c_pv, 1)

            def spread_recip(b, b_mn):
                pe.wait_ge(c_rd, b + 1)
                pe.wait_ge(c_mn, b_mn)
                for hf in range(2):
                    mm = pe.matmul(PS[0:DC, hf, 0:NT], ones[DC:DC + 1, 0:DC], rden[DC:DC + 1, hf, :], start=True, stop=True)
                mm.then_inc(c_bc, 1)

            def latent_out(b):
                pe.wait_ge(c_cn, b + 1)
                for m in range(KC):
                    for h in range(LH):
                        mm = pe.matmul(PS[:, 2, m * T:(m + 1) * T], wvo[:, h, m * P:(m + 1) * P], cn[:, h, :],
                                       start=h == 0, stop=h == LH - 1)
                mm.then_inc(c_om, 1)

            def latent_batch(b, slot, nth, last, prepare):
                pe.wait_ge(c_row[slot], 16 * nth)
                for n in range(LS + 2):
                    if n < LS:
                        scores(b, slot, n)
                    if n >= 2:
                        values(b, slot, n - 2)
                    if last is not None and n == 3:
                        spread_recip(last, b + 1)
                    if last is not None and n == 5:
                        latent_out(last)
                    if prepare is not None and n == 6:
                        keys_t(prepare, 1 - slot)
                    if prepare is not None and n >= 8 and n % 2 == 0 and (n - 8) // 2 < LH // 2:
                        row_scores(prepare, 1 - slot, (n - 8) // 2)
                if prepare is not None:
                    max_t(prepare)

            keys_t(0, 0)
            for k in range(LH // 2):
                row_scores(0, 0, k)
            max_t(0)
            latent_batch(0, 0, 1, None, 1)
            with pe.Fori(0, B // 2 - 1) as j:
                for d in range(2):
                    b = 2 * j + (1 + d)
                    latent_batch(b, 1 - d, j + (1 + d), 2 * j + d, 2 * j + (2 + d))
            latent_batch(B - 1, 1, B // 2, B - 2, None)
            spread_recip(B - 1, B)
            latent_out(B - 1)
            pe.wait_ge(s_xr, 11)
            for i in range(PAIRS):
                for c in range(KC):
                    mm = pe.transpose(PS[:, i // 2, (i % 2) * C + c * P:(i % 2) * C + (c + 1) * P],
                                      xT[:, c, 2 * i:2 * i + 2, :], ident[:])
                mm.then_inc(f_xm, 1)
            pb = PS[:].rearrange("p k n -> p (k n)").bitcast(BF16).rearrange("p (k n) -> p k n", k=8)
            pe.wait_ge(s_c6, 2)
            pe.wait_ge(f_ki, 1)
            for fc in range(KC):
                for dc in range(KC):
                    pe.transpose(pb[:, 6, (dc * KC + fc) * P:(dc * KC + fc + 1) * P], kwi[:, fc, dc * P:(dc + 1) * P], identb[:])
            for fc in range(KC):
                mm = pe.matmul(PS[:, 7, fc * P:(fc + 1) * P], one6[:], kdg[:, fc, :], start=True, stop=True)
            mm.then_inc(f_km, 1)
            for i in range(PAIRS):
                pe.wait_ge(f_xi, i + 1)
                pe.wait_ge(f_xc, PAIRS)
                if i >= 2:
                    pe.wait_ge(f_tc, i - 1)
                for c in range(KC):
                    mm = pe.transpose(pb[:, 4 + i % 2, c * P:(c + 1) * P], xi[:, i, c * P:(c + 1) * P], identb[:])
                mm.then_inc(f_tm, 1)
            pe.wait_ge(f_kc, 1)
            for i in range(PAIRS):
                pe.wait_ge(f_tc, i + 1)
                if i >= 4:
                    pe.wait_ge(f_o, i - 3)
                for c in range(KC):
                    mm = pe.matmul(PS[:, i % 4, 0:C], xiT[:, c, i * P:(i + 1) * P], kwT[:, c, :],
                                   start=c == 0, stop=c == KC - 1)
                mm.then_inc(f_ym, 1)

        @block.scalar
        def _(act):
            act.wait_ge(s_const, 6)
            ln_act(act, 0)
            act.wait_ge(s_w1, 32)
            for hf in range(2):
                if hf == 1:
                    act.wait_ge(s_xr, 3)
                for m in range(4):
                    act.wait_ge(s_par, 4 * hf + m + 1)
                    o = (gate_s, val_s)[m // 2][:, m % 2, :]
                    act.activation(o, PS[:, 4 + m, 0:NT], (ACT.Sigmoid, ACT.Tanh)[m // 2],
                                   bias=b0[:, m:m + 1]).then_inc(s_pact, 1)
            ln_act(act, 1)
            with act.Fori(0, PAIRS) as i:
                act.wait_ge(x_qm, i + 1)
                act.copy(qp[:].rearrange("p m b t -> p (m b t)"), PS[:, 0, :]).then_inc(x_qc, 1)
                act.wait_ge(x_vm, i + 1)
                act.copy(vp[:, :, :, 0:XD], PS[:, 2, :].rearrange("p (b h d) -> p b h d", b=2, h=XH)).then_inc(x_vc, 1)
                act.wait_ge(x_sh, i + 1)
                act.activation(pr[:, :, 0:T], sc[:], ACT.Exp).then_inc(x_ex, 1)
                act.wait_ge(x_tm, i + 1)
                act.copy(pt[:], PS[:, 0:2, :].rearrange("p k (m n) -> p (k m) n", n=P)).then_inc(x_tc, 1)
            ln_act(act, 2)
            act.wait_ge(e_lm, 1)
            act.copy(logit[:].rearrange("p i e -> p (i e)"), PS[:, 4:6, :].rearrange("p k n -> p (k n)")).then_inc(e_lc, 1)
            act.wait_ge(e_sh, 1)
            act.activation(expo[:], expo[:], ACT.Exp).then_inc(e_ex, 1)
            act.wait_ge(e_tm, 1)
            act.copy(coT[:].rearrange("p b t -> p (b t)"), PS[:, 6:8, :].rearrange("p k n -> p (k n)")).then_inc(e_tc, 1)
            for n in range(2 * (KB + 2)):
                act.wait_ge(e_gm, n + 1)
                if n >= 2:
                    act.wait_ge(e_pd, n - 1)
                act.activation(sgl[:, n % 2, :], PS[:, 3 * (n % 2), 0:NT], ACT.Silu).then_inc(e_si, 1)
            ln_act(act, 3)
            act.wait_ge(s_w4, 16 * 13)
            act.wait_ge(s_c4, 9)
            own = Own(act, own_a)
            act.wait_ge(d_ng, 1)
            own.step(act.activation(alog[:], alog[:], ACT.Exp))
            own.step(act.mul(alog[:], alog[:], -1.0))
            for hf in range(2):
                act.wait_ge(d_mm, hf + 1)
                raw = PS[0:NH, 6 + hf, 0:NT]
                act.activation(dts[:, 2 + hf, :], raw, ACT.Relu, bias=dtb[:])
                own.step(act.activation(dts[:, hf, :], raw, ACT.Abs, bias=dtb[:]))
                own.step(act.activation(dts[:, hf, :], dts[:, hf, :], ACT.Tanh, scale=0.5))
            for hf in range(2):
                act.activation(dts[:, hf, :], dts[:, hf, :], ACT.Ln, scale=0.5, bias=cst[0:NH, 0:1]).then_inc(d_ln, 1)
            for hf in range(2):
                act.wait_ge(d_dt, hf + 1)
                act.activation(aT[:, HB * hf:HB * hf + HB, :], dtc[:, HB * hf:HB * hf + HB, 0:T], ACT.Exp,
                               scale=alog[:]).then_inc(d_ex, 1)
            for n in range(4):
                bb = 3 * (n % 2)
                act.wait_ge(b_mm, n + 1)
                if n >= 1:
                    act.wait_ge(b_ms, n)
                act.activation(bsq, PS[:, bb, 0:NT], ACT.Square).then_inc(b_sq, 1)
                act.wait_ge(b_ms, n + 1)
                if n >= 1:
                    act.wait_ge(b_n, n)
                act.activation(bst, PS[:, bb + 2, 0:NT], ACT.Sqrt, scale=2.0 * P / 128, bias=cst[:, 1:2]).then_inc(b_sd, 1)
            act.wait_ge(d_tm, 1)
            act.copy(dtt[:].rearrange("p i h -> p (i h)"), PS[:, 6, :]).then_inc(d_tc, 1)
            for i in range(PAIRS):
                act.wait_ge(z_mm, i + 1)
                act.activation(siz[:, i, :], PS[:, 2 * (i % 2), :], ACT.Silu).then_inc(z_si, 1)

            def ssm_sines(hp, slot):
                act.wait_ge(m_fr, hp + 1)
                own.step(act.activation(absf[:], frac[:, slot, :], ACT.Abs))
                if not isinstance(hp, int) or hp >= 2:
                    act.wait_ge(m_tc, hp - 1)
                act.activation(sn[:, slot, :], frac[:, slot, :], ACT.Sin, scale=-TWO_PI)
                own.step(act.activation(cs[:, slot, :], absf[:], ACT.Sin, scale=-TWO_PI, bias=cst[:, 2:3]))
                act.sem_inc(m_sin, 1)

            def ssm_copy_y(hp):
                act.wait_ge(m_y, hp + 1)
                at = slice(hp * 2 * HD, (hp + 1) * 2 * HD) if isinstance(hp, int) else bass.ds(hp * (2 * HD), 2 * HD)
                for b2 in range(2):
                    rows = slice(64 * b2, 64 * b2 + 64)
                    ins = act.copy(ya[rows, :, at], PS[rows, 4 + b2, 0:2 * HD * PAIRS].rearrange("p (i n) -> p i n", n=2 * HD))
                ins.then_inc(m_yc, 1)

            ssm_sines(0, 0)
            for hp in range(2):
                ssm_sines(hp + 1, (hp + 1) % 2)
                ssm_copy_y(hp)
            with act.Fori(0, SSM_TRIPS) as j:
                own.enter(j, 4)
                for d in range(2):
                    ssm_sines(2 * j + 3 + d, (1 + d) % 2)
                    ssm_copy_y(2 * j + 2 + d)
            own.leave(SSM_TRIPS)
            ssm_sines(NH // 2 - 1, 1)
            ssm_copy_y(NH // 2 - 2)
            ssm_copy_y(NH // 2 - 1)
            for i in range(PAIRS):
                act.wait_ge(g_g, i + 1)
                act.activation(ysq[:, 0, 0:DI], ya[:, i, :], ACT.Square, accum_out=yss[:, i:i + 1]).then_inc(g_sq, 1)
                act.wait_ge(g_sq, i + 1)
            act.activation(yss[:], yss[:], ACT.Sqrt, scale=1.0 / DI, bias=cst[:, 1:2]).then_inc(g_sd, 1)
            ln_act(act, 4)

            def latent_copies(h, slot, absorb):
                act.wait_ge(k_w, h + 1)
                if not isinstance(h, int) or h >= 2:
                    act.wait_ge(k_a, 2 * h - 2)
                act.copy(wab[:, slot, :, :].rearrange("p r n -> p (r n)"), PS[0:RQ, 6, 0:256])
                w = wvo[:, h, :] if isinstance(h, int) else wvo[:, bass.ds(h, 1), :].rearrange("p o n -> p (o n)")
                act.copy(w, PS[0:DC, 6, 256:512]).then_inc(k_wc, 1)
                for hf in range(2):
                    act.wait_ge(k_q, 2 * h + (hf + 1))
                    if not isinstance(h, int) or h >= 1:
                        act.wait_ge(k_b, 2 * h + (hf - 1))
                    act.copy(qh[:, hf, :], PS[:, hf, 0:NT]).then_inc(k_qc, 1)
                if absorb is not None:
                    latent_high(absorb)

            def latent_high(h):
                for hf in range(2):
                    act.wait_ge(k_a, 2 * h + (hf + 1))
                    hs = slice(h, h + 1) if isinstance(h, int) else bass.ds(h, 1)
                    act.copy(qa[:, HB * hf:HB * hf + HB, hs, :].rearrange("p b o t -> p b (o t)"), bank(7 - hf)).then_inc(k_hi, 1)

            act.sem_inc(c_ex, 3)
            act.wait_ge(s_xn, 10)
            latent_copies(0, 0, None)
            with act.Fori(0, LH // 2 - 1) as j:
                for d in range(2):
                    latent_copies(2 * j + (1 + d), (1 + d) % 2, 2 * j + d)
            latent_copies(LH - 1, 1, LH - 2)
            latent_high(LH - 1)

            def keys_high(b, slot):
                act.wait_ge(c_tm, b + 1)
                act.copy(khi[:, slot, :].rearrange("p (k n) -> p k n", k=3), PS[:, 0:3, 0:S // 3]).then_inc(c_khi, 1)

            def max_row(b, slot):
                act.wait_ge(c_mt, b + 1)
                act.mul(rmn[:], PS[0:LH // 2, 2, 0:2 * T], -1.0).then_inc(c_mn, 1)
                act.wait_ge(c_mn, b + 1)
                act.dma_start(qb2[DC:DC + 1, slot, :].rearrange("o (k n) -> o k n", k=LH // 2), rmn[:]).then_inc(c_row[slot], 16)

            def latent_exp(b, slot, nth, prepare):
                for n in range(LS):
                    act.wait_ge(c_sm, LS * b + (n + 1))
                    act.wait_ge(c_pv, LS * b + (n + 1))
                    act.activation(pe3[:, n % 3, :], PS[0:KP, 3 + n % 3, 0:NT], ACT.Exp).then_inc(c_ex, 1)
                    if prepare is not None and n == 7:
                        keys_high(prepare, 1 - slot)
                if prepare is not None:
                    max_row(prepare, 1 - slot)

            keys_high(0, 0)
            max_row(0, 0)
            latent_exp(0, 0, 1, 1)
            with act.Fori(0, B // 2 - 1) as j:
                for d in range(2):
                    latent_exp(2 * j + (1 + d), 1 - d, None, 2 * j + (2 + d))
            latent_exp(B - 1, 1, None, None)
            pb = PS[:].rearrange("p k n -> p (k n)").bitcast(BF16).rearrange("p (k n) -> p k n", k=8)
            for i in range(PAIRS):
                act.wait_ge(f_xm, 2 * (i // 2) + 2)
                act.copy(xt[:, i, :], PS[:, i // 2, (i % 2) * C:(i % 2 + 1) * C]).then_inc(f_xc, 1)
            act.wait_ge(f_va, 1)
            act.activation(sx[:, 0, :], mv6[:, :, 1], ACT.Sqrt, bias=epsc[:]).then_inc(f_sd, 1)
            act.wait_ge(f_km, 1)
            act.copy(kwT[:].rearrange("p c f -> p (c f)"), pb[:, 6, 0:KC * C])
            act.copy(skb[:], PS[:, 7, 0:C]).then_inc(f_kc, 1)
            for i in range(PAIRS):
                act.wait_ge(f_tm, i + 1)
                act.copy(xiT[:, :, i * P:(i + 1) * P], pb[:, 4 + i % 2, 0:C].rearrange("p (c n) -> p c n", n=P)).then_inc(f_tc, 1)

        @block.vector
        def _(v):
            own = Own(v, own_v)
            v.wait_ge(s_const, 6)
            v.wait_ge(s_x, 16)
            for hf in range(2):
                v.nop().then_inc(s_xr, 1)
            ln_dve(v, own, 0)
            for hf in range(2):
                v.wait_ge(s_pact, 4 * hf + 4)
                own.step(v.memset(cols(gate_s[:].rearrange("p c n -> p (c n)"))[:, :, 0:1], 0.0))
                for c in range(KC):
                    own.done(v.tensor_tensor_scan(hid[:, c, :], gate_s[:, c, :], val_s[:, c, :], 0.0, ALU.mult, ALU.add))
                own.wait()
                for c in range(KC):
                    ins = v.tensor_tensor(half(xT, c, hf), half(xT, c, hf), cols(hid[:, c, :]), ALU.add)
                ins.then_inc(s_xr, 1)
                v.wait_ge(s_xr, 3 + hf)
            v.nop().then_inc(x_oc, 1)
            ln_dve(v, own, 1)
            with v.Fori(0, PAIRS) as i:
                own.enter(i, 4)
                v.wait_ge(x_km, i + 1)
                v.tensor_copy(kp[:].rearrange("p m b t -> p (m b t)"), PS[:, 1, :]).then_inc(x_kc, 1)
                v.wait_ge(x_sm, i + 1)
                mask = maskc[:].unsqueeze(1).broadcast_to((P, 4, T))
                for r in range(4):
                    s_r = PS[:, 4 + r, 0:4 * TP].rearrange("p (c t) -> p c t", t=TP)[:, :, 0:T]
                    ins = v.scalar_tensor_tensor(sc[:, 4 * r:4 * r + 4, :], s_r, XD ** -0.5, mask,
                                                 ALU.mult, ALU.add)
                own.step(ins)
                own.step(v.tensor_reduce(mxs[:], sc[:], AX, ALU.max))
                v.tensor_tensor(sc[:], sc[:], mxs[:].unsqueeze(2).broadcast_to((P, XH, T)),
                                ALU.subtract).then_inc(x_sh, 1)
                v.wait_ge(x_ex, i + 1)
                own.step(v.tensor_reduce(sms[:], pr[:, :, 0:T], AX, ALU.add))
                own.step(v.reciprocal(sms[:], sms[:]))
                v.tensor_tensor(pr[:, :, 0:T], pr[:, :, 0:T], sms[:].unsqueeze(2).broadcast_to((P, XH, T)),
                                ALU.mult).then_inc(x_pr, 1)
                v.wait_ge(x_om, i + 1)
                for e in range(2):
                    ins = v.tensor_copy(oT[:, e::2, bass.ds(2 * i, 2), 0:T],
                                        PS[:, 2 + e, 0:4 * T].rearrange("p (c b t) -> p c b t", c=2, b=2))
                ins.then_inc(x_oc, 1)
            own.leave(PAIRS)
            for hf in range(2):
                for m in range(KC):
                    v.wait_ge(x_wm, 2 * hf + m + 1)
                    ins = v.tensor_tensor(half(xT, m, hf), half(xT, m, hf), bank(4 + 2 * hf + m), ALU.add)
                ins.then_inc(s_xr, 1)
            v.wait_ge(s_xr, 6)
            v.wait_ge(s_w3, 16 * 9)
            own.step(v.tensor_tensor(amps[:], amps[:], amps[:], ALU.mult))
            own.step(v.tensor_tensor(mix[:], amps[:, 0, :], amps[:, 1, :], ALU.add))
            own.step(v.tensor_reduce(msum[:], mix[:], AX, ALU.add))
            own.step(v.tensor_scalar(msum[:], msum[:], 1e-8, None, ALU.add))
            own.step(v.reciprocal(msum[:], msum[:]))
            own.step(v.tensor_scalar(mix[:], mix[:], msum[:], escale[:], ALU.mult, ALU.mult))
            v.tensor_copy(mixb[:], mix[:].unsqueeze(2).broadcast_to((P, KB, P))).then_inc(e_mix, 1)
            ln_dve(v, own, 2)
            v.wait_ge(e_lc, 1)
            v.wait_ge(s_keep, 1)
            for i in range(PAIRS):
                ins = v.max(top8[:, i, :], logit[:, i, :])
            own.step(ins)
            shape = (P, PAIRS, E)
            v.tensor_tensor(expo[:], logit[:], top8[:, :, 0:1].broadcast_to(shape), ALU.subtract).then_inc(e_sh, 1)
            own.done(v.tensor_tensor(above[:], logit[:], top8[:, :, TOPK - 1:TOPK].broadcast_to(shape), ALU.is_gt))
            own.step(v.tensor_tensor(level[:], logit[:], top8[:, :, TOPK - 1:TOPK].broadcast_to(shape), ALU.is_equal))
            own.done(v.tensor_reduce(room[:], above[:], AX, ALU.add))
            own.step(v.tensor_tensor_scan(place[:].rearrange("p i e -> p (i e)"), keep[:],
                                          level[:].rearrange("p i e -> p (i e)"), 0.0, ALU.mult, ALU.add))
            own.step(v.tensor_scalar(room[:], room[:], -1.0, float(TOPK), ALU.mult, ALU.add))
            own.step(v.tensor_tensor(place[:], place[:], room[:].unsqueeze(2).broadcast_to(shape), ALU.is_le))
            own.step(v.tensor_tensor(level[:], level[:], place[:], ALU.mult))
            own.step(v.tensor_tensor(level[:], level[:], above[:], ALU.add))
            v.wait_ge(e_ex, 1)
            own.step(v.tensor_reduce(zsum[:], expo[:], AX, ALU.add))
            own.step(v.tensor_tensor(expo[:], expo[:], level[:], ALU.mult))
            own.step(v.tensor_reduce(tsum[:], expo[:], AX, ALU.add))
            own.step(v.scalar_tensor_tensor(tsum[:], zsum[:], 1e-8, tsum[:], ALU.mult, ALU.add))
            own.step(v.reciprocal(tsum[:], tsum[:]))
            v.tensor_tensor(expo[:], expo[:], tsum[:].unsqueeze(2).broadcast_to(shape), ALU.mult).then_inc(e_co, 1)
            for hf in range(2):
                for k in range(KB + 2):
                    n = hf * (KB + 2) + k
                    gb = 3 * (n % 2)
                    v.wait_ge(e_si, n + 1)
                    v.wait_ge(e_um, n + 1)
                    if k < KB:
                        own.step(v.tensor_tensor(gu[:, n % 2, :], sgl[:, n % 2, :], PS[:, gb + 1, 0:NT], ALU.mult))
                        if k == 0:
                            v.tensor_tensor(acc[:, hf, :], gu[:, n % 2, :], PS[:, gb + 2, 0:NT], ALU.mult).then_inc(e_pd, 1)
                            v.wait_ge(e_pd, n + 1)
                        else:
                            v.tensor_tensor(wgu[:], gu[:, n % 2, :], PS[:, gb + 2, 0:NT], ALU.mult).then_inc(e_pd, 1)
                            v.wait_ge(e_pd, n + 1)
                            own.step(v.tensor_tensor(acc[:, hf, :], acc[:, hf, :], wgu[:], ALU.add))
                    else:
                        v.tensor_tensor(shr[:, hf, k - KB, :], sgl[:, n % 2, :], PS[:, gb + 1, 0:NT],
                                        ALU.mult).then_inc(e_pd, 1)
                v.wait_ge(e_pd, (hf + 1) * (KB + 2))
                v.sem_inc(e_ac, 1)
            for hf in range(2):
                for m in range(KC):
                    v.wait_ge(e_dm, 2 * hf + m + 1)
                    ins = v.tensor_tensor(half(xT, m, hf), half(xT, m, hf), bank(6 + m), ALU.add)
                ins.then_inc(s_xr, 1)
            v.wait_ge(s_xr, 8)
            v.wait_ge(s_w4, 16 * 13)
            v.wait_ge(s_c4, 9)
            v.tensor_scalar(alog[:], alog[:], 80.0, None, ALU.min).then_inc(d_ng, 1)
            ln_dve(v, own, 3)
            for hf in range(2):
                v.wait_ge(d_ln, hf + 1)
                v.tensor_tensor(dtc[:, HB * hf:HB * hf + HB, 0:T], cols(dts[:, 2 + hf, :]), cols(dts[:, hf, :]),
                                ALU.subtract).then_inc(d_dt, 1)
            for hf in range(2):
                v.wait_ge(d_dt, hf + 1)
                own.step(v.tensor_copy(dts[:, hf, :].rearrange("p (b t) -> p b t", t=T), dtc[:, HB * hf:HB * hf + HB, 0:T]))
                v.tensor_tensor_scan(cum[:, hf * NT:(hf + 1) * NT], keept[:], dts[:, hf, :], 0.0,
                                     ALU.mult, ALU.add).then_inc(d_cum, 1)
            for hf in range(2):
                v.wait_ge(d_ex, hf + 1)
                v.memset(aT[:, HB * hf:HB * hf + HB, 0:1], 0.0).then_inc(d_a, 1)
            for n in range(4):
                hf, x, bb = n // 2, n % 2, 3 * (n % 2)
                v.wait_ge(b_sd, n + 1)
                own.step(v.reciprocal(bst, bst))
                for s in range(2):
                    ins = v.tensor_tensor(bcn[:, 2 * x + s, hf * NT:(hf + 1) * NT], PS[:, bb + s, 0:NT], bst, ALU.mult)
                ins.then_inc(b_n, 1)
                v.wait_ge(b_n, n + 1)
            v.wait_ge(d_tc, 1)
            for i in range(PAIRS):
                v.wait_ge(z_mm, i + 1)
                xs = PS[:, 2 * (i % 2) + 1, :].rearrange("p (h q) -> p h q", q=HD)
                v.tensor_tensor(dx[:, i, :].rearrange("p (h q) -> p h q", q=HD), xs,
                                dbc[:].unsqueeze(2).broadcast_to((P, NH, HD)), ALU.mult)
                v.tensor_tensor(ua[:, i, :].rearrange("p (h q) -> p h q", q=HD), xs,
                                dtt[:, i, :].unsqueeze(2).broadcast_to((P, NH, HD)), ALU.mult).then_inc(z_u, 1)

            def ssm_rotation(hp, slot):
                v.wait_ge(m_phi, hp + 1)
                phi = PS[:, 0:2, 0:NT]
                own.step(v.tensor_scalar(turn[:].rearrange("p (k n) -> p k n", k=2), phi, ROUND, -ROUND, ALU.add, ALU.add))
                if not isinstance(hp, int) or hp >= 2:
                    v.wait_ge(m_sin, hp - 1)
                v.tensor_tensor(frac[:, slot, :].rearrange("p (k n) -> p k n", k=2),
                                turn[:].rearrange("p (k n) -> p k n", k=2), phi, ALU.subtract).then_inc(m_fr, 1)

            def ssm_products(hp, slot):
                v.wait_ge(m_sin, hp + 1)
                for x, s in ((0, m_tb), (1, m_tc)):
                    if not isinstance(hp, int) or hp >= 1:
                        v.wait_ge((m_rb, m_rc)[x], hp)
                    for k, tab in ((2 * x, cs), (2 * x + 1, sn)):
                        bk = bias[:, k, hp:hp + 1] if isinstance(hp, int) else bias[:, k, bass.ds(hp, 1)]
                        ins = v.scalar_tensor_tensor(rt[:, k, :], bcn[:, k, :], bk, tab[:, slot, :], ALU.add, ALU.mult)
                    ins.then_inc(s, 1)

            def ssm_decay(hp, slot, nth):
                v.wait_ge(m_abc[slot], 32 * nth)
                v.tensor_tensor_scan(dec[:], ab[:, slot, :], eye[:], 0.0, ALU.mult, ALU.add).then_inc(m_sc, 1)
                v.wait_ge(m_sc, hp + 1)
                if not isinstance(hp, int) or hp >= 2:
                    v.wait_ge(m_y, hp - 1)
                v.wait_ge(m_g, hp + 1)
                m3 = mt[:, slot, 0:BT].rearrange("p (i h t) -> p i h t", h=2, t=T)
                d3 = dec[:].rearrange("p (i h t) -> p i h t", h=2, t=T)
                for h2 in range(2):
                    ins = v.tensor_tensor(m3[:, :, h2, :], bank(2 + h2), d3[:, :, h2, :], ALU.mult)
                ins.then_inc(m_mt, 1)
                v.wait_ge(m_mt, hp + 1)

            ssm_rotation(0, 0)
            ssm_products(0, 0)
            for hp in range(2):
                ssm_rotation(hp + 1, (hp + 1) % 2)
                ssm_decay(hp, hp % 2, 1)
                ssm_products(hp + 1, (hp + 1) % 2)
            with v.Fori(0, SSM_TRIPS) as j:
                own.enter(j, 2)
                for d in range(2):
                    ssm_rotation(2 * j + 3 + d, (1 + d) % 2)
                    ssm_decay(2 * j + 2 + d, d, j + 2)
                    ssm_products(2 * j + 3 + d, (1 + d) % 2)
            own.leave(SSM_TRIPS)
            ssm_rotation(NH // 2 - 1, 1)
            ssm_decay(NH // 2 - 2, 0, NH // 4)
            ssm_products(NH // 2 - 1, 1)
            ssm_decay(NH // 2 - 1, 1, NH // 4)
            v.wait_ge(m_yc, NH // 2)
            for i in range(PAIRS):
                own.step(v.scalar_tensor_tensor(ya[:, i, :], ya[:, i, :], DS ** -0.5, dx[:, i, :], ALU.mult, ALU.add))
                v.tensor_tensor(ya[:, i, :], ya[:, i, :], siz[:, i, :], ALU.mult).then_inc(g_g, 1)
            v.wait_ge(g_sd, 1)
            own.step(v.reciprocal(yss[:], yss[:]))
            for i in range(PAIRS):
                v.tensor_scalar(ya[:, i, :], ya[:, i, :], yss[:, i:i + 1], None, ALU.mult).then_inc(g_n, 1)
            for i in range(PAIRS):
                v.wait_ge(g_tm, i + 1)
                for b2 in range(2):
                    o = gT[:, :, (2 * i + b2) * T:(2 * i + b2 + 1) * T]
                    s = PS[:, i % 2, :].rearrange("p (c n) -> p c n", n=P)[:, :, 64 * b2:64 * b2 + T]
                    ins = v.tensor_tensor(o, s, nw[:].unsqueeze(2).broadcast_to((P, DI // P, T)), ALU.mult)
                ins.then_inc(g_tc, 1)
            for hf in range(2):
                for m in range(KC):
                    v.wait_ge(g_wm, 2 * hf + m + 1)
                    ins = v.tensor_tensor(half(xT, m, hf), half(xT, m, hf), bank(4 + 2 * hf + m), ALU.add)
                ins.then_inc(s_xr, 1)
            v.wait_ge(s_xr, 10)
            ln_dve(v, own, 4)
            v.sem_inc(k_lo, 1)
            v.sem_inc(c_pv, 3)
            v.sem_inc(c_cx, 1)
            v.wait_ge(s_w5, 48)

            def latent_products(h, hf):
                v.wait_ge(k_b, 2 * h + (hf + 1))
                if not isinstance(h, int) or h + hf >= 1:
                    v.wait_ge(k_r, 2 * h + hf)
                for n, (r, k) in enumerate(((0, 0), (1, 1), (1, 2), (0, 3))):
                    ins = v.tensor_tensor(cols(rp4[:, n, :]), bank(2 + 2 * hf + r, rows=slice(0, RQ)),
                                          rqt[:, k:k + 1, :].broadcast_to((RQ, HB, T)), ALU.mult)
                ins.then_inc(k_p, 1)

            def latent_low(h):
                for hf in range(2):
                    v.wait_ge(k_hi, 2 * h + (hf + 1))
                    hs = slice(h, h + 1) if isinstance(h, int) else bass.ds(h, 1)
                    q = qa[DC:P, HB * hf:HB * hf + HB, hs, :].rearrange("p b o t -> p b (o t)")
                    v.tensor_tensor(q, bank(7 - hf, rows=slice(DC, P)), q, ALU.subtract).then_inc(k_lo, 1)

            for hf in range(2):
                latent_products(0, hf)
            with v.Fori(1, LH) as h:
                latent_low(h - 1)
                for hf in range(2):
                    latent_products(h, hf)
            latent_low(LH - 1)
            v.wait_ge(k_lo, 2 * LH + 1)

            def keys_low(b, slot):
                v.wait_ge(c_khi, b + 1)
                v.tensor_tensor(klo[0:DC, slot, :].rearrange("p (k n) -> p k n", k=3), PS[0:DC, 0:3, 0:S // 3],
                                khi[0:DC, slot, :].rearrange("p (k n) -> p k n", k=3), ALU.subtract).then_inc(c_klo, 1)
                src = qa[:, b:b + 1] if isinstance(b, int) else qa[:, bass.ds(b, 1)]
                src = src.rearrange("p o h t -> p (o h t)")
                v.tensor_copy(qb1[:, slot, :], src)
                v.tensor_copy(qb2[0:DC, slot, :], src[0:DC]).then_inc(c_qb, 1)

            def row_max(b, k):
                v.wait_ge(c_mm, (LH // 2) * b + (k + 1))
                if k == 0 and (not isinstance(b, int) or b >= 1):
                    v.wait_ge(c_mt, b)
                v.tensor_reduce(rmx[:, k:k + 1], PS[0:2 * T, 0:3, 0:S // 3], XY, ALU.max).then_inc(c_mr, 1)

            def latent_sums(b):
                v.wait_ge(c_pv, LS * b + (LS + 3))
                v.tensor_copy(cx[:], PS[0:DC + 1, 6:8, 0:NT]).then_inc(c_cx, 1)
                v.wait_ge(c_cx, b + 2)
                v.reciprocal(rden[DC:DC + 1, :, :], cx[DC:DC + 1, :, :]).then_inc(c_rd, 1)

            def latent_update(b):
                v.wait_ge(c_bc, b + 1)
                v.tensor_tensor(cn[:].rearrange("p h t -> p (h t)").rearrange("p (k n) -> p k n", k=2),
                                cx[0:DC, :, :], PS[0:DC, 0:2, 0:NT], ALU.mult).then_inc(c_cn, 1)
                v.wait_ge(c_om, b + 1)
                xb = xT[:, :, b:b + 1, 0:T] if isinstance(b, int) else xT[:, :, bass.ds(b, 1), 0:T]
                xb = xb.rearrange("p c o t -> p c (o t)")
                v.tensor_tensor(xb, xb, PS[:, 2, 0:KC * T].rearrange("p (c t) -> p c t", t=T), ALU.add).then_inc(c_xu, 1)

            keys_low(0, 0)
            for k in range(LH // 2):
                row_max(0, k)

            def latent_vector(b, slot, last, prepare):
                if last is not None:
                    latent_sums(last)
                    latent_update(last)
                if prepare is not None:
                    keys_low(prepare, 1 - slot)
                    for k in range(LH // 2):
                        row_max(prepare, k)

            v.sem_inc(c_xu, 1)
            latent_vector(0, 0, None, 1)
            with v.Fori(0, B // 2 - 1) as j:
                for d in range(2):
                    latent_vector(2 * j + (1 + d), 1 - d, 2 * j + d, 2 * j + (2 + d))
            latent_vector(B - 1, 1, B - 2, None)
            latent_sums(B - 1)
            latent_update(B - 1)
            v.wait_ge(c_xu, B + 1)
            v.sem_inc(s_xr, 1)

            def quant_scale(s):
                own.step(v.tensor_scalar(s[:, 3], s[:, 0], 0.0, None, ALU.is_equal))
                own.step(v.scalar_tensor_tensor(s[:, 1], s[:, 0], 1.0 / 127.0, s[:, 3], ALU.mult, ALU.add))
                own.step(v.reciprocal(s[:, 2], s[:, 1]))

            def whole(o, a, inv):
                own.step(v.tensor_scalar(o, a, inv, ROUND, ALU.mult, ALU.add))
                own.step(v.tensor_scalar(o, o, -ROUND, 127.0, ALU.add, ALU.min))
                return v.tensor_scalar(o, o, -127.0, None, ALU.max)

            v.wait_ge(s_w6, 32)
            own.step(v.tensor_reduce(sk[:, 0, :], kw[:], AX, ALU.max, apply_absolute_value=True))
            own.step(v.tensor_reduce(sbq[:, 0:1], bq[:], AX, ALU.max, apply_absolute_value=True))
            quant_scale(sk)
            quant_scale(sbq[:].unsqueeze(2))
            for c in range(KC):
                own.step(v.tensor_scalar(kdg[:, c, :], ident[:], sk[:, 1, c:c + 1], None, ALU.mult))
                whole(kw[:, c, :], kw[:, c, :], sk[:, 2, c:c + 1]).then_inc(own_v, 1)
                own.n += 1
            own.wait()
            v.tensor_copy(kwi[:], kw[:]).then_inc(f_ki, 1)
            own.step(whole(bqi[:], bq[:], sbq[:, 2:3]))
            own.step(v.tensor_scalar(bq[:], bqi[:], sbq[:, 1:2], None, ALU.mult))
            for i in range(PAIRS):
                v.wait_ge(f_xc, i + 1)
                own.done(v.bn_stats(st6[:, i, :], xt[:, i, :]))
            own.wait()
            for i in range(PAIRS):
                ins = v.bn_aggr(mv6[:, i, :], st6[:, i, :])
            ins.then_inc(f_va, 1)
            v.wait_ge(f_sd, 1)
            own.step(v.reciprocal(sx[:, 0, :], sx[:, 0, :]))
            for i in range(PAIRS):
                own.done(v.tensor_scalar(xq[:, i, :], xt[:, i, :], mv6[:, i, 0:1], sx[:, 0, i:i + 1], ALU.subtract, ALU.mult))
            own.wait()
            own.step(v.tensor_reduce(sx[:, 0, :], xq[:], AX, ALU.max, apply_absolute_value=True))
            quant_scale(sx)
            for i in range(PAIRS):
                own.step(whole(xq[:, i, :], xq[:, i, :], sx[:, 2, i:i + 1]))
                v.tensor_copy(xi[:, i, :], xq[:, i, :]).then_inc(f_xi, 1)
            v.wait_ge(f_kc, 1)
            for i in range(PAIRS):
                v.wait_ge(f_ym, i + 1)
                own.step(v.scalar_tensor_tensor(y6[:, i, :], PS[:, i % 4, 0:C], sx[:, 1, i:i + 1], skb[:], ALU.mult, ALU.mult))
                own.step(v.tensor_tensor(y6[:, i, :], y6[:, i, :], bq[:], ALU.add))
                own.step(v.tensor_scalar(y6[:, i, :], y6[:, i, :], 0.0, None, ALU.max))
                own.step(v.tensor_reduce(sy[:, 0, i:i + 1], y6[:, i, :], AX, ALU.max))
                quant_scale(sy[:, :, i:i + 1])
                own.step(whole(y6[:, i, :], y6[:, i, :], sy[:, 2, i:i + 1]))
                v.scalar_tensor_tensor(y6[:, i, :], y6[:, i, :], sy[:, 1, i:i + 1], xt[:, i, :], ALU.mult, ALU.add).then_inc(f_o, 1)


def pad_time(a):
    import numpy as np
    o = np.zeros(a.shape[:-1] + (TP,), a.dtype)
    o[..., :T] = a
    return o


def layouts(inp):
    import numpy as np
    f = np.float32
    L = {}
    L["xT"] = pad_time(inp["x"].transpose(2, 0, 1))
    L["W0"] = inp["L0_attn_W"].T
    L["b0"] = inp["L0_attn_b"].reshape(4, P).T
    wq = inp["L0_xattn_Wq"].reshape(XH, XD, C)
    pq = np.zeros((C, XH, XDP), f)
    pq[:, :, :XD] = wq.transpose(2, 0, 1)
    L["Wxq"] = pq.reshape(C, XH * XDP)
    wkv = inp["L0_xattn_Wkv_expand"]
    pk = np.zeros((64, XH, XDP), f)
    pk[:, :, :XD] = wkv[:C].reshape(XH, XD, 64).transpose(2, 0, 1)
    L["Wxk"] = pk.reshape(64, XH * XDP)
    L["Wxv"] = wkv[C:].T
    po = np.zeros((XH, XDP, C), f)
    po[:, :XD, :] = inp["L0_xattn_Wout"].T.reshape(XH, XD, C)
    L["Wxo"] = po.reshape(XH * XDP, C)
    L["ctx56"] = pad_time(inp["ctx_512"][:, :T, :].transpose(2, 0, 1))
    q = np.arange(P) % TP
    L["causal"] = np.where(np.arange(T)[None, :] <= q[:, None], f(0), f(NEG)).astype(f)
    L["Wr"], L["Wg"], L["Wu"], L["Wd"] = (inp["L0_ffn_" + n] for n in ("w_router", "w_gate", "w_up", "w_down"))
    L["Wsg"], L["Wsu"], L["Wsd"] = (inp["L0_ffn_shared_w_" + n] for n in ("gate", "up", "down"))
    L["amps"] = inp["L0_ffn_amplitudes"].transpose(0, 2, 1)
    L["escale"] = inp["L0_ffn_expert_scale"].reshape(P, 1)
    win = inp["L1_attn_W_in"]
    L["Wzx"] = win[:, :2 * DI]
    up = np.r_[0:DS:2, 1:DS:2]
    sw = np.r_[1:DS:2, 0:DS:2]
    wb, wc = win[:, 2 * DI:2 * DI + DS], win[:, 2 * DI + DS:2 * DI + 2 * DS]
    L["Wbc"] = np.stack([np.tile(w[:, o], (1, 2)) for w in (wb, wc) for o in (up, sw)], 1)
    L["Wdt"] = win[:, 2 * DI + 2 * DS:]
    L["Wmo"] = inp["L1_attn_W_out"]
    L["frow"] = np.tile(inp["L1_attn_rope_freqs"], (1, 4))
    bb, cb = inp["L1_attn_B_bias"], inp["L1_attn_C_bias"]
    L["bcbias"] = np.stack([w[:, o].reshape(NH // 2, P).T for w in (bb, cb) for o in (up, sw)], 1)
    L["dtb"] = inp["L1_attn_dt_bias"].reshape(NH, 1)
    L["alog"] = inp["L1_attn_A_log"].reshape(NH, 1)
    L["Dp"] = inp["L1_attn_D_param"].reshape(1, NH)
    L["nw"] = inp["L1_attn_norm_w"].reshape(DI // P, P).T
    L["sgn"] = np.tile((np.where(np.arange(P) % DS < DS // 2, -1.0, 1.0) / (2 * np.pi)).astype(f), (NH, 1))
    L["sel"] = (np.arange(NH)[:, None, None] == np.arange(NH).reshape(1, NH // 2, 2)).astype(f)
    L["eye"] = np.tile((np.arange(P)[:, None] % TP == np.arange(T)[None, :]).astype(f), (1, 2 * PAIRS))
    L["ctx"] = inp["ctx_512"]
    L["Lwq"] = inp["L1_xattn_Wq"].reshape(LH, P, KC, P).transpose(0, 3, 2, 1)
    L["Lwc"] = inp["L1_xattn_w_kc_q"]
    L["Lwr"] = inp["L1_xattn_W_qr"].transpose(0, 2, 1)
    L["Lwk"] = np.tile(inp["L1_xattn_W_kr"].transpose(0, 2, 1), (1, 1, 2))
    L["Lwv"] = inp["L1_xattn_w_kc_kv"]
    L["Lwo"] = inp["L1_xattn_Wo"].reshape(C, LH, P).transpose(1, 2, 0)

    def rope(length, dim):
        inv = (1.0 / f(10000.0) ** (np.arange(0, dim, 2, dtype=f) / f(dim))).astype(f)
        a = np.arange(length, dtype=f)[:, None] * inv[None, :]
        sin, cos = np.repeat(np.sin(a), 2, -1), np.repeat(np.cos(a), 2, -1)
        sin[:, :dim // 2] *= -1
        return sin, cos

    sin, cos = rope(T, 2 * RQ)
    L["rqt"] = np.stack([cos[:, :RQ].T, sin[:, :RQ].T, cos[:, RQ:].T, sin[:, RQ:].T], 1)
    sin, cos = rope(S, DC)
    L["rkc"], L["rks"] = cos.reshape(KP, KT, DC), sin.reshape(KP, KT, DC)
    L["kT"] = inp["L1_ffn_kernel"].T
    L["fb"] = inp["L1_ffn_bias"].reshape(1, C)
    return {k: np.ascontiguousarray(a) for k, a in L.items()}


def kernel(**inputs):
    import numpy as _np
    import concourse.bacc as _bacc
    from concourse import mybir as _mybir
    from concourse.bass_utils import run_bass_kernel_spmd as _run

    nc = _bacc.Bacc("TRN2", target_bir_lowering=False, num_devices=1)
    arrays, aps = {}, {}
    for name, a in layouts({k: _np.asarray(v) for k, v in inputs.items()}).items():
        arrays[f"in_{name}_dram"] = a
        aps[name] = nc.dram_tensor(f"in_{name}_dram", a.shape, _mybir.dt.from_np(a.dtype), kind="ExternalInput").ap()
    out = nc.dram_tensor("out_dram", (B, T, C), F32, kind="ExternalOutput").ap()
    decoder(nc, aps, out)
    r = _run(nc, [arrays], core_ids=[0])
    return r.results[0]["out_dram"]
```

```python
from contextlib import ExitStack

import concourse.bass as bass
from concourse import mybir

F32 = mybir.dt.float32
F16 = mybir.dt.float16
BF16 = mybir.dt.bfloat16
ALU = mybir.AluOpType
ACT = mybir.ActivationFunctionType
AX = mybir.AxisListType.X
XY = mybir.AxisListType.XY

P = 128
B, T, TP = 16, 56, 64
PAIRS = B // 2
HB = B // 2
NT = HB * T
BT = B * T
C = 256
KC = C // P
XH, XD, XDP = 16, 16, 32
E, TOPK, KB = 128, 4, 8
NEG = -1e30
LN_EPS = 1e-5
NH, HD, DS = 64, 8, 64
DI = NH * HD
NP2 = NH // 2
SSM_TRIPS = (NP2 - 6) // 2
LH, DC, RQ = 16, 64, 96
S, KT = 1500, 12
KP = S // KT
LR = LH * T
LS = 2 * KT
KEYS_AT = 3
TWO_PI = 6.2831845
HALF_PI = 1.5707963
ROUND = 12582912.0


class Own:

    def __init__(self, eng, sem):
        self.eng, self.sem, self.n, self.i, self.per = eng, sem, 0, None, 0

    def enter(self, i, per):
        self.i, self.per, self.base = i, per, self.n
        self.n = 0

    def leave(self, trips):
        assert self.n == self.per, (self.n, self.per)
        self.n, self.i = self.base + trips * self.per, None

    def done(self, ins):
        ins.then_inc(self.sem, 1)
        self.n += 1

    def wait(self):
        if self.i is None:
            self.eng.wait_ge(self.sem, self.n)
        else:
            self.eng.wait_ge(self.sem, self.i * self.per + (self.base + self.n))

    def step(self, ins):
        self.done(ins)
        self.wait()


def decoder(nc, A, out):
    with ExitStack() as ctx:
        def sb(name, shape, dt=F32, where=ctx):
            return where.enter_context(nc.sbuf_tensor(name, shape, dt))

        def sem(name):
            return ctx.enter_context(nc.semaphore(name))

        PS = ctx.enter_context(nc.psum_tensor("PS", [P, 8, 512], F32))

        def bank(k, b=HB, t=T, rows=slice(0, P)):
            return PS[rows, k, 0:b * t].rearrange("p (b t) -> p b t", t=t)

        xT = sb("xT", [P, KC, B, TP])
        xn = sb("xn", [P, KC, B, TP])
        xc = sb("xc", [P, KC, NT])
        sq = sb("sq", [P, KC, NT])
        std = sb("std", [P, NT])
        avg = sb("avg", [P, P])
        ident = sb("ident", [P, P])
        epsc = sb("epsc", [P, 1])

        def half(t, c, hf):
            return t[:, c, HB * hf:HB * hf + HB, 0:T]

        def cols(t):
            return t.rearrange("p (b t) -> p b t", t=T)

        wzx = sb("wzx", [P, KC, 2 * DI])
        wbc = sb("wbc", [P, KC, 4, P])
        wdt = sb("wdt", [P, KC, NH])
        wmo = sb("wmo", [P, DI // P, C])
        sel = sb("sel", [NH, NH // 2, 2])
        sgn = sb("sgn", [NH, P])
        eye = sb("eye", [P, 2 * PAIRS * T])
        frow = sb("frow", [NH, P])
        bias = sb("bias", [P, 4, NH // 2])
        dtb = sb("dtb", [NH, 1])
        alog = sb("alog", [NH, 1])
        dbc = sb("dbc", [P, NH])
        nw = sb("nw", [P, DI // P])
        keept = sb("keept", [NH, NT])
        cst = sb("cst", [P, 4])
        rqt = sb("rqt", [RQ, 4, T])
        p2 = ExitStack()
        w0 = sb("w0", [P, KC, 2 * C], where=p2)
        b0 = sb("b0", [P, 4], where=p2)
        gate_s = sb("gate_s", [P, KC, NT], where=p2)
        val_s = sb("val_s", [P, KC, NT], where=p2)
        hid = sb("hid", [P, KC, NT], where=p2)

        wxq = sb("wxq", [P, KC, XH * XDP], where=p2)
        wxk = sb("wxk", [64, XH * XDP], where=p2)
        wxv = sb("wxv", [64, C], where=p2)
        wxo = sb("wxo", [P, 4, C], where=p2)
        ctxs = sb("ctxs", [64, B, TP], where=p2)
        ctxp = sb("ctxp", [64, 2, 2, TP], where=p2)
        maskc = sb("maskc", [P, T], where=p2)
        qp = sb("qp", [P, 4, 2, TP], where=p2)
        kp = sb("kp", [P, 4, 2, TP], where=p2)
        vp = sb("vp", [P, 2, XH, XDP], where=p2)
        sc = sb("sc", [P, XH, T], where=p2)
        pr = sb("pr", [P, XH, TP], where=p2)
        mxs = sb("mxs", [P, XH], where=p2)
        sms = sb("sms", [P, XH], where=p2)
        pt = sb("pt", [P, 8, P], where=p2)
        oT = sb("oT", [P, 4, B, TP], where=p2)

        wr = sb("wr", [P, KC, E], where=p2)
        wg = sb("wg", [P, KC, KB * P], where=p2)
        wu = sb("wu", [P, KC, KB * P], where=p2)
        wd = sb("wd", [P, C], where=p2)
        wsg = sb("wsg", [P, KC, C], where=p2)
        wsu = sb("wsu", [P, KC, C], where=p2)
        wsd = sb("wsd", [P, KC, C], where=p2)
        amps = sb("amps", [P, 2, KB], where=p2)
        escale = sb("escale", [P, 1], where=p2)
        mix = sb("mix", [P, KB], where=p2)
        mixb = sb("mixb", [P, KB, P], where=p2)
        msum = sb("msum", [P, 1], where=p2)
        keep = sb("keep", [P, PAIRS * E], where=p2)
        logit = sb("logit", [P, PAIRS, E], where=p2)
        top8 = sb("top8", [P, PAIRS, 8], where=p2)
        above = sb("above", [P, PAIRS, E], where=p2)
        level = sb("level", [P, PAIRS, E], where=p2)
        place = sb("place", [P, PAIRS, E], where=p2)
        expo = sb("expo", [P, PAIRS, E], where=p2)
        room = sb("room", [P, PAIRS], where=p2)
        zsum = sb("zsum", [P, PAIRS], where=p2)
        tsum = sb("tsum", [P, PAIRS], where=p2)
        coT = sb("coT", [P, B, TP], where=p2)
        sgl = sb("sgl", [P, 2, NT], where=p2)
        gu = sb("gu", [P, 2, NT], where=p2)
        wgu = sb("wgu", [P, NT], where=p2)
        acc = sb("acc", [P, 2, NT], where=p2)
        shr = sb("shr", [P, 2, 2, NT], where=p2)
        p2.close()
        p4 = ExitStack()
        dtc = sb("dtc", [NH, B, TP], where=p4)
        cum = sb("cum", [NH, B * T], where=p4)
        aT = sb("aT", [NH, B, T], where=p4)
        dtt = sb("dtt", [P, PAIRS, NH], where=p4)
        bcn = sb("bcn", [P, 4, BT], where=p4)
        siz = sb("siz", [P, PAIRS, DI], where=p4)
        dx = sb("dx", [P, PAIRS, DI], where=p4)
        ua = sb("ua", [P, PAIRS, DI], where=p4)
        ya = ua
        f2 = sb("f2", [NH, 2, P], where=p4)
        uh = sb("uh", [P, 2, PAIRS, 2, 2 * HD], where=p4)
        turn = sb("turn", [P, BT], where=p4)
        frac = sb("frac", [P, 2, BT], where=p4)
        sn = sb("sn", [P, 2, BT], where=p4)
        cs = sb("cs", [P, 2, BT], where=p4)
        rt = sb("rt", [P, 4, BT], where=p4)
        rb = sb("rb", [P, 2, BT + 8], where=p4)
        rc = sb("rc", [P, 2, B, 2, T], where=p4)
        ab = sb("ab", [P, 2, BT], where=p4)
        dec = sb("dec", [P, BT], where=p4)
        mt = sb("mt", [P, 2, 2 * PAIRS, TP], where=p4)
        yss = sb("yss", [P, PAIRS], where=p4)
        bsq, bst = frac[:, 0, 0:NT], frac[:, 1, 0:NT]
        dts = cs[0:NH].rearrange("p s (k n) -> p (s k) n", k=2)
        gT = rt
        ysq = frac
        p4.close()
        p5 = ExitStack()
        rkc = sb("rkc", [KP, KT, DC], where=p5)
        rks = sb("rks", [KP, KT, DC], where=p5)
        lwq = sb("lwq", [P, 2, KC, P], where=p5)
        lwc = sb("lwc", [P, 2, 2 * RQ], where=p5)
        lwr = sb("lwr", [DC, 2, 2 * RQ], where=p5)
        lwk = sb("lwk", [DC, 2, P], where=p5)
        lwv = sb("lwv", [P, 2, DC], where=p5)
        lwo = sb("lwo", [P, 2, C], where=p5)
        wab = sb("wab", [RQ, 2, 2, P], where=p5)
        wvo = sb("wvo", [P, LH // 2, C], where=p5)
        cn = sb("cn", [P, LH // 2, B, T], where=p5)
        qbuf = cn[:].rearrange("p k b t -> p (k b t)").rearrange("p (n t) -> p n t", t=NT)
        qh = qbuf[:, 0:2, :]
        rp4 = qbuf[0:RQ, 2:10, :].rearrange("p (k n) t -> p k n t", k=2)
        rot = qbuf[0:RQ, 10:14, :].rearrange("p (k n) t -> p k n t", k=2)
        qa = sb("qa", [P, B, LH, T], F16, where=p5)
        kvx = sb("kvx", [KP, 2, KT, DC], where=p5)
        kvr = sb("kvr", [KP, 2, KT, 2 * DC + 1], where=p5)
        kvt = sb("kvt", [KP, KT, DC], where=p5)
        kvp = sb("kvp", [KP, KT, DC], where=p5)
        khi = sb("khi", [P, 2, S], F16, where=p5)
        klo = sb("klo", [DC + 1, 2, S], F16, where=p5)
        qb1 = sb("qb1", [P, 2, LR], F16, where=p5)
        qb2 = sb("qb2", [DC + 1, 2, LR], F16, where=p5)
        rmx = sb("rmx", [2 * T, LH // 2], where=p5)
        rmn = sb("rmn", [LH // 2, 2 * T], F16, where=p5)
        pe3 = sb("pe3", [KP, 3, NT], where=p5)
        cx = sb("cx", [DC + 1, 2, NT], where=p5)
        rden = sb("rden", [DC + 1, 2, NT], where=p5)
        ones = sb("ones", [P, P], where=p5)
        p5.close()
        p6 = ExitStack()
        xt = sb("xt", [P, PAIRS, C], where=p6)
        xq = sb("xq", [P, PAIRS, C], where=p6)
        xi = sb("xi", [P, PAIRS, C], BF16, where=p6)
        xiT = sb("xiT", [P, KC, PAIRS * P], BF16, where=p6)
        kw = sb("kw", [P, KC, C], where=p6)
        kwi = sb("kwi", [P, KC, C], BF16, where=p6)
        kwT = sb("kwT", [P, KC, C], BF16, where=p6)
        kdg = sb("kdg", [P, KC, P], where=p6)
        skb = sb("skb", [P, C], where=p6)
        bq = sb("bq", [P, C], where=p6)
        bqi = sb("bqi", [P, C], where=p6)
        one6 = sb("one6", [P, P], where=p6)
        identb = sb("identb", [P, P], BF16, where=p6)
        st6 = sb("st6", [P, PAIRS, 6], where=p6)
        mv6 = sb("mv6", [P, PAIRS, 2], where=p6)
        sx = sb("sx", [P, 4, PAIRS], where=p6)
        sk = sb("sk", [P, 4, KC], where=p6)
        sbq = sb("sbq", [P, 4], where=p6)
        sy = sb("sy", [P, 4, PAIRS], where=p6)
        y6 = sb("y6", [P, PAIRS, C], where=p6)
        p6.close()
        s_x = sem("x_loaded")
        s_w1 = sem("w1_loaded")
        s_w2 = sem("w2_loaded")
        s_const = sem("const_ready")
        s_xr = sem("x_ready")
        s_mean = sem("ln_mean")
        s_cen = sem("ln_centred")
        s_sq = sem("ln_squared")
        s_var = sem("ln_var")
        s_std = sem("ln_std")
        s_xn = sem("ln_out")
        own_v = sem("vector_own")
        own_a = sem("scalar_own")
        own_g = sem("gpsimd_own")
        s_par = sem("l0_params")
        s_pact = sem("l0_activated")
        x_cp = sem("xa_ctx_copied")
        x_qm, x_km, x_vm = sem("xa_q_mm"), sem("xa_k_mm"), sem("xa_v_mm")
        x_qc, x_kc, x_vc = sem("xa_q_copied"), sem("xa_k_copied"), sem("xa_v_copied")
        x_sm, x_sh, x_ex, x_pr = sem("xa_scores"), sem("xa_shifted"), sem("xa_exp"), sem("xa_probs")
        x_tm, x_tc = sem("xa_pt_mm"), sem("xa_pt_copied")
        x_om, x_oc, x_wm = sem("xa_o_mm"), sem("xa_o_copied"), sem("xa_out_mm")
        s_gate = sem("tensor_gate")
        s_out = sem("stored")
        s_w3 = sem("w3_loaded")
        s_keep = sem("moe_keep")
        e_mix = sem("moe_mix")
        e_lm, e_lc, e_sh, e_ex, e_co = sem("moe_logits"), sem("moe_logits_copied"), sem("moe_shifted"), sem("moe_exp"), sem("moe_coeff")
        e_tm, e_tc = sem("moe_coT_mm"), sem("moe_coT")
        e_gm, e_um, e_si, e_pd = sem("moe_gate_mm"), sem("moe_up_mm"), sem("moe_silu"), sem("moe_product")
        e_ac, e_dm = sem("moe_acc"), sem("moe_down_mm")
        a_scr = nc.dram_tensor("decay_scratch", (NH // 2, 2, PAIRS, 2, T), F32, kind="Internal").ap()
        s_w4 = sem("w4_loaded")
        s_c4 = sem("ssm_const")
        d_mm, d_abs, d_th, d_ln, d_dt, d_cum = (sem("ssm_" + n) for n in ("dt_mm", "dt_abs", "dt_tanh", "dt_ln", "dt", "cum"))
        d_ng, d_ex, d_a, d_st = (sem("ssm_" + n) for n in ("neg_a", "decay_exp", "decay", "decay_stored"))
        d_tm, d_tc = sem("ssm_dtt_mm"), sem("ssm_dtt")
        b_mm, b_sq, b_ms, b_sd, b_n = (sem("ssm_bc_" + n) for n in ("mm", "squared", "mean", "std", "normed"))
        z_mm, z_si, z_u = sem("ssm_zx_mm"), sem("ssm_silu"), sem("ssm_u")
        m_f2, m_u, m_phi, m_fr, m_ab, m_sin = (sem("ssm_" + n) for n in ("f2", "uh", "phi", "frac", "absf", "sin"))
        m_tb, m_tc, m_rb, m_rc, m_sc = (sem("ssm_" + n) for n in ("tb", "tc", "rotB", "rotC", "scan"))
        m_abc = [sem(f"ssm_a_bcast_{n}") for n in range(2)]
        m_g, m_mt, m_y, m_yc = (sem("ssm_" + n) for n in ("g", "mt", "y", "y_copied"))
        g_g, g_sq, g_sd, g_n, g_tm, g_tc, g_wm = (sem("ssm_out_" + n) for n in ("gated", "squared", "std", "normed", "t_mm", "t", "mm"))
        s_w5, s_c5 = sem("w5_loaded"), sem("latent_const")
        k_ld = [sem(f"lq_weights_{n}") for n in range(2)]
        k_w, k_wc, k_q, k_qc, k_b, k_p, k_r, k_a, k_hi, k_lo = (sem("lq_" + n) for n in (
            "w_mm", "w_copied", "proj", "proj_copied", "big", "products", "rotated", "abs_mm", "high", "low"))
        c_ld = [sem(f"kv_loaded_{n}") for n in range(2)]
        c_row = [sem(f"max_row_{n}") for n in range(2)]
        c_rp, c_tm, c_khi, c_klo, c_qb, c_mm, c_mr, c_mt, c_mn = (sem("la_" + n) for n in (
            "roped", "kT_mm", "k_high", "k_low", "q_slot", "max_mm", "max", "max_t", "max_neg"))
        c_sm, c_ex, c_pv, c_cx, c_rd, c_bc, c_cn, c_om, c_xu = (sem("la_" + n) for n in (
            "scores", "exp", "pv", "ctx_copied", "recip", "recip_bcast", "ctx_normed", "out_mm", "x_updated"))
        s_w6, s_c6 = sem("w6_loaded"), sem("ffn_const")
        f_xm, f_xc, f_va, f_sd, f_xi = (sem("ffn_" + n) for n in ("x_mm", "x_copied", "variance", "std", "x_int"))
        f_tm, f_tc, f_ki, f_km, f_kc, f_ym = (sem("ffn_" + n) for n in ("xT_mm", "xT", "k_int", "k_mm", "k_ready", "y_mm"))
        f_o = sem("ffn_out")
        block = ctx.enter_context(nc.Block())

        @block.sync
        def _(sp):
            sp.dma_start(xT[:], A["xT"].rearrange("(c p) b t -> p c b t", p=P)).then_inc(s_x, 16)
            sp.dma_start(w0[:], A["W0"].rearrange("(c p) n -> p c n", p=P)).then_inc(s_w1, 16)
            sp.dma_start(b0[:], A["b0"]).then_inc(s_w1, 16)
            sp.dma_start(wxq[:], A["Wxq"].rearrange("(c p) n -> p c n", p=P)).then_inc(s_w2, 16)
            sp.dma_start(wxk[:], A["Wxk"]).then_inc(s_w2, 16)
            sp.dma_start(wxv[:], A["Wxv"]).then_inc(s_w2, 16)
            sp.dma_start(wxo[:], A["Wxo"].rearrange("(c p) n -> p c n", p=P)).then_inc(s_w2, 16)
            sp.dma_start(ctxs[:], A["ctx56"]).then_inc(s_w2, 16)
            sp.dma_start(maskc[:], A["causal"]).then_inc(s_w2, 16)
            sp.dma_start(wr[:], A["Wr"].rearrange("(c p) n -> p c n", p=P)).then_inc(s_w3, 16)
            sp.dma_start(wg[:], A["Wg"].rearrange("(c p) n -> p c n", p=P)).then_inc(s_w3, 16)
            sp.dma_start(wu[:], A["Wu"].rearrange("(c p) n -> p c n", p=P)).then_inc(s_w3, 16)
            sp.dma_start(wd[:], A["Wd"]).then_inc(s_w3, 16)
            sp.dma_start(wsg[:], A["Wsg"].rearrange("(c p) n -> p c n", p=P)).then_inc(s_w3, 16)
            sp.dma_start(wsu[:], A["Wsu"].rearrange("(c p) n -> p c n", p=P)).then_inc(s_w3, 16)
            sp.dma_start(wsd[:], A["Wsd"].rearrange("(c p) n -> p c n", p=P)).then_inc(s_w3, 16)
            sp.dma_start(amps[:], A["amps"]).then_inc(s_w3, 16)
            sp.dma_start(escale[:], A["escale"]).then_inc(s_w3, 16)
            for t, src in ((wzx, A["Wzx"].rearrange("(c p) n -> p c n", p=P)), (wbc, A["Wbc"].rearrange("(c p) k n -> p c k n", p=P)),
                           (wdt, A["Wdt"].rearrange("(c p) n -> p c n", p=P)),
                           (wmo, A["Wmo"].rearrange("(c p) n -> p c n", p=P)), (sel, A["sel"]), (eye, A["eye"]),
                           (frow, A["frow"]), (sgn, A["sgn"]), (bias, A["bcbias"]), (dtb, A["dtb"]), (alog, A["alog"]),
                           (dbc, A["Dp"].broadcast_to((P, NH))), (nw, A["nw"])):
                sp.dma_start(t[:], src).then_inc(s_w4, 16)
            sp.wait_ge(d_a, 2)
            for h2 in range(2):
                for b2 in range(2):
                    sp.dma_start(a_scr[:, b2, :, h2, :], aT[h2::2, b2::2, :]).then_inc(d_st, 16)
            sp.wait_ge(d_st, 64)

            def ssm_load(hp, slot):
                for b2 in range(2):
                    src = a_scr[hp, b2] if isinstance(hp, int) else a_scr[bass.ds(hp, 1), b2]
                    src = src.rearrange("i h t -> (i h t)") if isinstance(hp, int) else src.rearrange("o i h t -> o (i h t)")
                    if isinstance(hp, int):
                        src = src.unsqueeze(0)
                    sp.dma_start(ab[64 * b2:64 * b2 + 64, slot, :], src.broadcast_to((64, BT))).then_inc(m_abc[slot], 16)

            ssm_load(0, 0)
            ssm_load(1, 1)
            with sp.Fori(0, NH // 4 - 1) as j:
                for d in range(2):
                    sp.wait_ge(m_sc, 2 * j + (1 + d))
                    ssm_load(2 * j + (2 + d), d)
            sp.dma_start(rqt[:], A["rqt"]).then_inc(s_w5, 16)
            sp.wait_ge(s_xr, 10)
            sp.dma_start(rkc[:], A["rkc"]).then_inc(s_w5, 16)
            sp.dma_start(rks[:], A["rks"]).then_inc(s_w5, 16)

            def latent_weights(h, slot):
                hs = slice(h, h + 1) if isinstance(h, int) else bass.ds(h, 1)
                for t, a in ((lwq[:, slot, :, :], A["Lwq"][hs].rearrange("o p c n -> p (o c) n")),
                             (lwc[:, slot, :], A["Lwc"][hs].rearrange("o p n -> p (o n)")),
                             (lwr[:, slot, :], A["Lwr"][hs].rearrange("o p n -> p (o n)")),
                             (lwk[:, slot, :], A["Lwk"][hs].rearrange("o p n -> p (o n)")),
                             (lwv[:, slot, :], A["Lwv"][hs].rearrange("o p n -> p (o n)")),
                             (lwo[:, slot, :], A["Lwo"][hs].rearrange("o p n -> p (o n)"))):
                    sp.dma_start(t, a).then_inc(k_ld[slot], 16)

            def latent_context(b, slot):
                bs = slice(b, b + 1) if isinstance(b, int) else bass.ds(b, 1)
                sp.dma_start(kvx[:, slot, :, :].rearrange("p j d -> p (j d)"),
                             A["ctx"][bs].rearrange("o (p j) d -> (o p) (j d)", j=KT)).then_inc(c_ld[slot], 16)

            latent_weights(0, 0)
            latent_weights(1, 1)
            latent_context(0, 0)
            latent_context(1, 1)
            with sp.Fori(0, LH // 2 - 1) as j:
                for d in range(2):
                    sp.wait_ge(k_b, 4 * j + (2 + 2 * d))
                    latent_weights(2 * j + (2 + d), d)
            with sp.Fori(0, B // 2 - 1) as j:
                for d in range(2):
                    sp.wait_ge(c_rp, 2 * j + (1 + d))
                    latent_context(2 * j + (2 + d), d)
            sp.wait_ge(s_xr, 11)
            sp.dma_start(kw[:], A["kT"].rearrange("(c p) d -> p c d", p=P)).then_inc(s_w6, 16)
            sp.dma_start(bq[:], A["fb"].broadcast_to((P, C))).then_inc(s_w6, 16)
            for i in range(PAIRS):
                sp.wait_ge(f_o, i + 1)
                for b2 in range(2):
                    sp.dma_start(out[2 * i + b2], y6[64 * b2:64 * b2 + T, i, :]).then_inc(s_out, 16)
            sp.wait_ge(s_out, 16 * B)

        def ln_pe(pe, k):
            for hf in range(2):
                pe.wait_ge(s_xr, 2 * k + hf + 1)
                for c in range(KC):
                    mm = pe.matmul(bank(hf), avg[:], half(xT, c, hf), start=c == 0, stop=c == KC - 1)
                mm.then_inc(s_mean, 1)
            for hf in range(2):
                pe.wait_ge(s_sq, 2 * k + hf + 1)
                for c in range(KC):
                    mm = pe.matmul(bank(2 + hf), avg[:], cols(sq[:, c, :]), start=c == 0, stop=c == KC - 1)
                mm.then_inc(s_var, 1)

        def ln_act(act, k):
            for hf in range(2):
                act.wait_ge(s_cen, 2 * k + hf + 1)
                if hf == 1:
                    act.wait_ge(s_var, 2 * k + 1)
                act.activation(sq[:], xc[:], ACT.Square).then_inc(s_sq, 1)
                act.wait_ge(s_var, 2 * k + hf + 1)
                act.activation(std[:], PS[:, 2 + hf, 0:NT], ACT.Sqrt, bias=epsc[:]).then_inc(s_std, 1)

        def ln_dve(v, own, k):
            for hf in range(2):
                v.wait_ge(s_mean, 2 * k + hf + 1)
                for c in range(KC):
                    ins = v.tensor_tensor(cols(xc[:, c, :]), half(xT, c, hf), bank(hf), ALU.subtract)
                ins.then_inc(s_cen, 1)
                v.wait_ge(s_std, 2 * k + hf + 1)
                own.step(v.reciprocal(std[:], std[:]))
                for c in range(KC):
                    ins = v.tensor_tensor(half(xn, c, hf), cols(xc[:, c, :]), cols(std[:]), ALU.mult)
                ins.then_inc(s_xn, 1)
                v.wait_ge(s_xn, 2 * k + hf + 1)

        @block.gpsimd
        def _(g):
            own = Own(g, own_g)
            g.memset(avg[:], 1.0 / C).then_inc(s_const, 1)
            g.memset(epsc[:], LN_EPS).then_inc(s_const, 1)
            g.memset(xn[:], 0.0).then_inc(s_const, 1)
            own.step(g.memset(ident[:], 0.0))
            g.affine_select(out=ident[:], in_=ident[:], compare_op=ALU.not_equal, fill=1.0, base=0,
                            pattern=[[-1, P]], channel_multiplier=1).then_inc(s_const, 1)
            g.memset(vp[:], 0.0).then_inc(s_const, 1)
            g.memset(pr[:], 0.0).then_inc(s_const, 1)
            g.wait_ge(s_w2, 16 * 6)
            for b in range(2):
                ins = g.tensor_copy(ctxp[:, :, b, :], ctxs[:, 0:2, :])
            ins.then_inc(x_cp, 1)
            with g.Fori(0, PAIRS - 1) as i:
                g.wait_ge(x_vm, i + 1)
                for b in range(2):
                    ins = g.tensor_copy(ctxp[:, :, b, :], ctxs[:, bass.ds(2 * i + 2, 2), :])
                ins.then_inc(x_cp, 1)
            own.step(g.memset(keep[:], 1.0))
            g.memset(keep[:].rearrange("p (i e) -> p i e", e=E)[:, :, 0:1], 0.0).then_inc(s_keep, 1)
            own.step(g.memset(keept[:], 1.0))
            g.memset(cols(keept[:])[:, :, 0:1], 0.0).then_inc(s_c4, 1)
            for n, c in enumerate((0.5, 1e-6, HALF_PI, 0.0)):
                g.memset(cst[:, n:n + 1], c).then_inc(s_c4, 1)
            g.wait_ge(s_xr, 8)
            g.memset(dtc[:], 0.0).then_inc(s_c4, 1)
            g.memset(rb[:], 0.0).then_inc(s_c4, 1)
            g.memset(rc[:], 0.0).then_inc(s_c4, 1)
            g.memset(mt[:], 0.0).then_inc(s_c4, 1)
            g.memset(uh[:], 0.0).then_inc(s_c4, 1)
            g.wait_ge(s_c4, 10)
            g.wait_ge(s_w4, 16 * 13)
            own.step(g.tensor_tensor(frow[:], frow[:], sgn[:], ALU.mult))
            g.wait_ge(z_u, PAIRS)

            def ssm_freq(hp, slot):
                if not isinstance(hp, int) or hp >= 2:
                    g.wait_ge(m_phi, hp - 1)
                s = sel[:, hp, :] if isinstance(hp, int) else sel[:, bass.ds(hp, 1), :].rearrange("p o h -> p (o h)")
                g.tensor_tensor(f2[:, slot, :].rearrange("p (h n) -> p h n", h=2), frow[:].rearrange("p (h n) -> p h n", h=2),
                                s.unsqueeze(2).broadcast_to((NH, 2, DS)), ALU.mult).then_inc(m_f2, 1)

            def ssm_rotate(hp, slot):
                g.wait_ge(m_tb, hp + 1)
                if not isinstance(hp, int) or hp >= 2:
                    g.wait_ge(m_g, hp - 1)
                g.tensor_tensor(rb[:, slot, 0:BT], rt[:, 0, :], rt[:, 1, :], ALU.add).then_inc(m_rb, 1)
                g.wait_ge(m_tc, hp + 1)
                for h2 in range(2):
                    rows = slice(64 * h2, 64 * h2 + 64)
                    g.tensor_tensor(rc[rows, slot, :, h2, :], rt[rows, 2, :].rearrange("p (b t) -> p b t", t=T),
                                    rt[rows, 3, :].rearrange("p (b t) -> p b t", t=T), ALU.add).then_inc(m_rc, 1)
                    g.wait_ge(m_rc, 2 * hp + (1 + h2))

            def ssm_inputs(hp, slot):
                if not isinstance(hp, int) or hp >= 2:
                    g.wait_ge(m_y, hp - 1)
                at = slice(hp * 2 * HD, (hp + 1) * 2 * HD) if isinstance(hp, int) else bass.ds(hp * (2 * HD), 2 * HD)
                for b2 in range(2):
                    rows = slice(64 * b2, 64 * b2 + 64)
                    g.tensor_copy(uh[rows, slot, :, b2, :], ua[rows, :, at]).then_inc(m_u, 1)
                    g.wait_ge(m_u, 2 * hp + (1 + b2))

            def ssm_pool(k, p):
                if not isinstance(k, int) or k + 4 < NP2:
                    ssm_freq(k + 4, p)
                if not isinstance(k, int) or 0 <= k + 1 < NP2:
                    ssm_rotate(k + 1, 1 - p)
                if not isinstance(k, int) or 0 <= k < NP2:
                    ssm_inputs(k, p)

            for k in range(-4, 2):
                ssm_pool(k, k % 2)
            with g.Fori(0, SSM_TRIPS) as j:
                for d in range(2):
                    ssm_pool(2 * j + (2 + d), d)
            for k in range(NP2 - 4, NP2):
                ssm_pool(k, k % 2)
            g.wait_ge(s_xr, 10)
            g.memset(kvr[:, :, :, 2 * DC:2 * DC + 1], 1.0).then_inc(s_c5, 1)
            g.wait_ge(s_c5, 1)
            g.memset(klo[DC:DC + 1, :, :], 1.0).then_inc(s_c5, 1)
            g.wait_ge(s_c5, 2)
            g.memset(ones[:], 1.0).then_inc(s_c5, 1)
            g.wait_ge(s_c5, 3)
            g.wait_ge(s_w5, 48)

            def rope_context(b, slot, nth):
                g.wait_ge(c_ld[slot], 16 * nth)
                kx = kvx[:, slot, :, :]
                own.done(g.tensor_tensor(kvt[:, :, 0:DC // 2], kx[:, :, DC // 2:DC], rks[:, :, 0:DC // 2], ALU.mult))
                own.done(g.tensor_tensor(kvt[:, :, DC // 2:DC], kx[:, :, 0:DC // 2], rks[:, :, DC // 2:DC], ALU.mult))
                own.step(g.tensor_tensor(kvp[:], kx, rkc[:], ALU.mult))
                if not isinstance(b, int) or b >= 2:
                    g.wait_ge(c_pv, LS * b - (LS - 3))
                own.done(g.tensor_tensor(kvr[:, slot, :, 0:DC], kvp[:], kvt[:], ALU.add))
                own.step(g.tensor_tensor(kvr[:, slot, :, DC:2 * DC], kvp[:], kvt[:], ALU.add))
                g.sem_inc(c_rp, 1)

            def rotate_queries(h, hf):
                g.wait_ge(k_p, 2 * h + (hf + 1))
                if not isinstance(h, int) or h >= 1:
                    g.wait_ge(k_a, 2 * h + (hf - 1))
                for r in range(2):
                    ins = g.tensor_tensor(rot[:, hf, r, :], rp4[:, hf, 2 * r, :], rp4[:, hf, 2 * r + 1, :], ALU.add)
                ins.then_inc(k_r, 1)

            for hf in range(2):
                rotate_queries(0, hf)
            with g.Fori(1, LH) as h:
                for hf in range(2):
                    rotate_queries(h, hf)
            rope_context(0, 0, 1)
            rope_context(1, 1, 1)
            with g.Fori(0, B // 2 - 1) as j:
                own.enter(j, 10)
                for d in range(2):
                    rope_context(2 * j + (2 + d), d, j + 2)
            own.leave(B // 2 - 1)
            g.wait_ge(s_xr, 11)
            g.memset(one6[:], 1.0).then_inc(s_c6, 1)
            g.tensor_copy(identb[:], ident[:]).then_inc(s_c6, 1)

        @block.tensor
        def _(pe):
            pe.wait_ge(s_const, 6)
            ln_pe(pe, 0)
            pe.wait_ge(s_w1, 32)
            for hf in range(2):
                pe.wait_ge(s_xn, hf + 1)
                for m in range(4):
                    if hf == 1:
                        pe.wait_ge(s_pact, m + 1)
                    for c in range(KC):
                        mm = pe.matmul(bank(4 + m), w0[:, c, m * P:(m + 1) * P], half(xn, c, hf),
                                       start=c == 0, stop=c == KC - 1)
                    mm.then_inc(s_par, 1)
            ln_pe(pe, 1)
            pe.wait_ge(s_w2, 16 * 6)
            pe.wait_ge(s_xn, 4)
            with pe.Fori(0, PAIRS) as i:
                for m in range(4):
                    for c in range(KC):
                        mm = pe.matmul(PS[:, 0, m * P:(m + 1) * P], wxq[:, c, m * P:(m + 1) * P],
                                       xn[:, c, bass.ds(2 * i, 2), :], start=c == 0, stop=c == KC - 1)
                mm.then_inc(x_qm, 1)
                for m in range(4):
                    mm = pe.matmul(PS[:, 1, m * P:(m + 1) * P], wxk[:, m * P:(m + 1) * P],
                                   ctxs[:, bass.ds(2 * i, 2), :], start=True, stop=True)
                mm.then_inc(x_km, 1)
                pe.wait_ge(x_cp, i + 1)
                pe.wait_ge(x_oc, i + 1)
                for b in range(2):
                    mm = pe.matmul(PS[:, 2, b * C:(b + 1) * C], ctxp[:, b, :, :], wxv[:],
                                   start=True, stop=True)
                mm.then_inc(x_vm, 1)
                pe.wait_ge(x_qc, i + 1)
                pe.wait_ge(x_kc, i + 1)
                for c in range(4):
                    for r in range(4):
                        rows = slice(32 * r, 32 * r + 32)
                        for b in range(2):
                            mm = pe.matmul(PS[64 * b:64 * b + 64, 4 + r, TP * c:TP * c + T],
                                           qp[rows, c, b, :], kp[rows, c, b, 0:T], start=True, stop=True)
                mm.then_inc(x_sm, 1)
                pe.wait_ge(x_pr, i + 1)
                for m in range(8):
                    mm = pe.transpose(PS[:, m // 4, (m % 4) * P:(m % 4) * P + P],
                                      pr[:, 2 * m:2 * m + 2, :], ident[:])
                mm.then_inc(x_tm, 1)
                pe.wait_ge(x_vc, i + 1)
                pe.wait_ge(x_tc, i + 1)
                pe.sem_inc(s_gate, 1)
                for m in range(8):
                    for e in range(2):
                        r, c = m // 2, 2 * (m % 2) + e
                        for b in range(2):
                            rows = slice(64 * e, 64 * e + T)
                            at = (c // 2 * 2 + b) * T
                            mm = pe.matmul(PS[32 * r:32 * r + 32, 2 + e, at:at + T], vp[rows, b, 4 * c + r, :],
                                           pt[rows, m, 64 * b:64 * b + T], start=True, stop=True)
                mm.then_inc(x_om, 1)
            for hf in range(2):
                pe.wait_ge(x_oc, PAIRS + 1)
                for m in range(KC):
                    for c in range(4):
                        mm = pe.matmul(bank(4 + 2 * hf + m), wxo[:, c, m * P:(m + 1) * P], half(oT, c, hf),
                                       start=c == 0, stop=c == 3)
                    mm.then_inc(x_wm, 1)
            ln_pe(pe, 2)
            pe.wait_ge(s_w3, 16 * 9)
            pe.wait_ge(s_xn, 6)
            for i in range(PAIRS):
                for c in range(KC):
                    mm = pe.matmul(PS[:, 4 + i // 4, (i % 4) * E:(i % 4) * E + E],
                                   xn[:, c, 2 * i:2 * i + 2, :], wr[:, c, :], start=c == 0, stop=c == KC - 1)
            mm.then_inc(e_lm, 1)
            pe.wait_ge(e_co, 1)
            for i in range(PAIRS):
                mm = pe.transpose(PS[:, 6 + i // 4, (i % 4) * P:(i % 4) * P + P], expo[:, i, :], ident[:])
            mm.then_inc(e_tm, 1)
            pe.wait_ge(e_tc, 1)
            pe.wait_ge(e_mix, 1)
            for hf in range(2):
                for k in range(KB + 2):
                    n = hf * (KB + 2) + k
                    gb = 3 * (n % 2)
                    if n >= 2:
                        pe.wait_ge(e_pd, n - 1)
                    w, u, j = (wg, wu, k) if k < KB else (wsg, wsu, k - KB)
                    for c in range(KC):
                        mm = pe.matmul(bank(gb), w[:, c, j * P:(j + 1) * P], half(xn, c, hf),
                                       start=c == 0, stop=c == KC - 1)
                    mm.then_inc(e_gm, 1)
                    for c in range(KC):
                        mm = pe.matmul(bank(gb + 1), u[:, c, j * P:(j + 1) * P], half(xn, c, hf),
                                       start=c == 0, stop=c == KC - 1)
                    if k < KB:
                        mm = pe.matmul(bank(gb + 2), mixb[:, k, :], coT[:, HB * hf:HB * hf + HB, 0:T],
                                       start=True, stop=True)
                    mm.then_inc(e_um, 1)
            for hf in range(2):
                pe.wait_ge(e_ac, hf + 1)
                if hf == 1:
                    pe.wait_ge(s_xr, 7)
                for m in range(KC):
                    pe.matmul(bank(6 + m), wd[:, m * P:(m + 1) * P], cols(acc[:, hf, :]), start=True, stop=False)
                    for c in range(KC):
                        mm = pe.matmul(bank(6 + m), wsd[:, c, m * P:(m + 1) * P], cols(shr[:, hf, c, :]),
                                       start=False, stop=c == KC - 1)
                    mm.then_inc(e_dm, 1)
            ln_pe(pe, 3)
            pe.wait_ge(s_w4, 16 * 13)
            pe.wait_ge(s_xn, 8)
            for hf in range(2):
                for c in range(KC):
                    mm = pe.matmul(bank(6 + hf, rows=slice(0, NH)), wdt[:, c, :], half(xn, c, hf),
                                   start=c == 0, stop=c == KC - 1)
                mm.then_inc(d_mm, 1)
            for n in range(4):
                hf, x, bb = n // 2, n % 2, 3 * (n % 2)
                if n >= 2:
                    pe.wait_ge(b_n, n - 1)
                for s in range(2):
                    for c in range(KC):
                        mm = pe.matmul(bank(bb + s), wbc[:, c, 2 * x + s, :], half(xn, c, hf),
                                       start=c == 0, stop=c == KC - 1)
                mm.then_inc(b_mm, 1)
                pe.wait_ge(b_sq, n + 1)
                pe.matmul(bank(bb + 2), avg[:], cols(bsq), start=True, stop=True).then_inc(b_ms, 1)
            pe.wait_ge(s_c4, 10)
            pe.wait_ge(d_dt, 2)
            for i in range(PAIRS):
                mm = pe.transpose(PS[:, 6, i * NH:(i + 1) * NH], dtc[:, 2 * i:2 * i + 2, :], ident[0:NH, 0:NH])
            mm.then_inc(d_tm, 1)
            pe.wait_ge(b_n, 4)
            for i in range(PAIRS):
                zb = 2 * (i % 2)
                if i >= 2:
                    pe.wait_ge(z_si, i - 1)
                    pe.wait_ge(z_u, i - 1)
                for s in range(2):
                    for c in range(KC):
                        mm = pe.matmul(PS[:, zb + s, :], xn[:, c, 2 * i:2 * i + 2, :], wzx[:, c, s * DI:(s + 1) * DI],
                                       start=c == 0, stop=c == KC - 1)
                mm.then_inc(z_mm, 1)
            pe.wait_ge(z_u, PAIRS)
            pe.wait_ge(z_si, PAIRS)

            def ssm_angle(hp, slot):
                if not isinstance(hp, int) or hp >= 1:
                    pe.wait_ge(m_fr, hp)
                pe.wait_ge(m_f2, hp + 1)
                for hf in range(2):
                    mm = pe.matmul(PS[:, hf, 0:NT], f2[:, slot, :], cum[:, hf * NT:(hf + 1) * NT], start=True, stop=True)
                mm.then_inc(m_phi, 1)

            def ssm_mix(hp, slot):
                if not isinstance(hp, int) or hp >= 1:
                    pe.wait_ge(m_mt, hp)
                pe.wait_ge(m_rb, hp + 1)
                pe.wait_ge(m_rc, 2 * hp + 2)
                for b in range(B):
                    i, half_pairs = b // 2, PAIRS // 2
                    mm = pe.matmul(PS[64 * (b % 2):64 * (b % 2) + 64, 2 + i // half_pairs,
                                      i % half_pairs * 2 * T:(i % half_pairs + 1) * 2 * T],
                                   rb[:, slot, b * T:b * T + TP], rc[:, slot, b, :, :].rearrange("p h t -> p (h t)"),
                                   start=True, stop=True)
                mm.then_inc(m_g, 1)

            def ssm_y(hp, slot):
                if not isinstance(hp, int) or hp >= 2:
                    pe.wait_ge(m_yc, hp - 1)
                pe.wait_ge(m_u, 2 * hp + 2)
                pe.wait_ge(m_mt, hp + 1)
                for i in range(PAIRS):
                    mm = pe.matmul(PS[:, 4 + slot, i * 4 * HD:(i + 1) * 4 * HD],
                                   mt[:, slot, 2 * i:2 * i + 2, :].rearrange("p h t -> p (h t)"),
                                   uh[:, slot, i, :, :].rearrange("p b n -> p (b n)"), start=True, stop=True)
                mm.then_inc(m_y, 1)

            pe.wait_ge(d_cum, 2)

            def ssm_tensor(k, p):
                if not isinstance(k, int) or 0 <= k < NP2:
                    ssm_mix(k, p)
                if not isinstance(k, int) or k + 3 < NP2:
                    ssm_angle(k + 3, 1 - p)
                if not isinstance(k, int) or 1 <= k:
                    ssm_y(k - 1, 1 - p)

            for k in range(-3, 2):
                ssm_tensor(k, k % 2)
            with pe.Fori(0, SSM_TRIPS) as j:
                for d in range(2):
                    ssm_tensor(2 * j + (2 + d), d)
            for k in range(NP2 - 4, NP2 + 1):
                ssm_tensor(k, k % 2)
            for i in range(PAIRS):
                pe.wait_ge(g_n, i + 1)
                if i >= 2:
                    pe.wait_ge(g_tc, i - 1)
                for c in range(DI // P):
                    mm = pe.transpose(PS[:, i % 2, c * P:(c + 1) * P], ya[:, i, c * P:(c + 1) * P], ident[:])
                mm.then_inc(g_tm, 1)
            pe.wait_ge(g_tc, PAIRS)
            for hf in range(2):
                for m in range(KC):
                    for c in range(DI // P):
                        mm = pe.matmul(PS[:, 4 + 2 * hf + m, 0:NT], wmo[:, c, m * P:(m + 1) * P],
                                       gT[:, c, hf * NT:(hf + 1) * NT], start=c == 0, stop=c == DI // P - 1)
                    mm.then_inc(g_wm, 1)
            ln_pe(pe, 4)
            pe.wait_ge(s_c5, 3)
            pe.wait_ge(s_xn, 10)

            def latent_project(h, slot, nth):
                pe.wait_ge(k_ld[slot], 96 * nth)
                if not isinstance(h, int) or h >= 1:
                    pe.wait_ge(k_lo, 2 * h - 1)
                for r in range(2):
                    pe.matmul(PS[0:RQ, 6, r * P:(r + 1) * P], lwr[:, slot, r * RQ:(r + 1) * RQ], lwk[:, slot, :],
                              start=True, stop=True)
                pe.matmul(PS[0:DC, 6, 256:512], lwv[:, slot, :], lwo[:, slot, :], start=True, stop=True).then_inc(k_w, 1)
                if not isinstance(h, int) or h >= 1:
                    pe.wait_ge(k_qc, 2 * h)
                for hf in range(2):
                    for c in range(KC):
                        mm = pe.matmul(bank(hf), lwq[:, slot, c, :], half(xn, c, hf), start=c == 0, stop=c == KC - 1)
                    mm.then_inc(k_q, 1)

            def latent_big(h, slot):
                for hf in range(2):
                    pe.wait_ge(k_qc, 2 * h + (hf + 1))
                    if not isinstance(h, int) or h >= 1:
                        pe.wait_ge(k_p, 2 * h + (hf - 1))
                    for r in range(2):
                        mm = pe.matmul(PS[0:RQ, 2 + 2 * hf + r, 0:NT], lwc[:, slot, r * RQ:(r + 1) * RQ], qh[:, hf, :],
                                       start=True, stop=True)
                    mm.then_inc(k_b, 1)

            def latent_absorb(h, slot, h_w):
                for hf in range(2):
                    pe.wait_ge(k_r, 2 * h + (hf + 1))
                    if hf == 0 and (not isinstance(h, int) or h >= 1):
                        pe.wait_ge(k_lo, 2 * h)
                    if hf == 1:
                        pe.wait_ge(k_wc, h_w)
                    for r in range(2):
                        mm = pe.matmul(PS[:, 7 - hf, 0:NT], wab[:, slot, r, :], rot[:, hf, r, :], start=r == 0, stop=r == 1)
                    mm.then_inc(k_a, 1)

            latent_project(0, 0, 1)
            latent_big(0, 0)
            with pe.Fori(0, LH // 2 - 1) as j:
                for d in range(2):
                    h = 2 * j + (1 + d)
                    latent_project(h, (1 + d) % 2, j + (1 + d))
                    latent_absorb(2 * j + d, d, 2 * j + (2 + d))
                    latent_big(h, (1 + d) % 2)
            latent_project(LH - 1, 1, LH // 2)
            latent_absorb(LH - 2, 0, LH)
            latent_big(LH - 1, 1)
            latent_absorb(LH - 1, 1, LH)

            def keys_t(b, slot):
                pe.wait_ge(c_rp, b + 1)
                if not isinstance(b, int) or b >= 1:
                    pe.wait_ge(c_mn, b)
                if not isinstance(b, int) or b >= 2:
                    pe.wait_ge(c_cn, b - 1)
                for j in range(KT):
                    mm = pe.transpose(PS[:, j // 4, (j % 4) * KP:(j % 4) * KP + KP],
                                      kvr[:, slot, j, 0:2 * DC], ident[0:KP, 0:KP])
                mm.then_inc(c_tm, 1)

            def row_scores(b, slot, k):
                if k == 0:
                    pe.wait_ge(c_khi, 3 * b + 3)
                    pe.wait_ge(c_klo, b + 1)
                    pe.wait_ge(c_qb, b + 1)
                else:
                    pe.wait_ge(c_mr, (LH // 2) * b + k)
                for j in range(3):
                    mm = pe.matmul(PS[0:2 * T, j, 0:S // 3], qb2[0:DC, slot, 2 * T * k:2 * T * (k + 1)],
                                   khi[0:DC, slot, j * (S // 3):(j + 1) * (S // 3)], start=True, stop=True)
                mm.then_inc(c_mm, 1)

            def max_t(b):
                pe.wait_ge(c_mr, (LH // 2) * b + LH // 2)
                pe.transpose(PS[0:LH // 2, 2, 0:2 * T], rmx[:], ident[0:2 * T, 0:2 * T]).then_inc(c_mt, 1)

            def scores(b, slot, n):
                j, hf = n // 2, n % 2
                pe.wait_ge(c_ex, LS * b + (n + 1))
                keys = slice(j * KP, (j + 1) * KP)
                cut = slice(hf * NT, (hf + 1) * NT)
                pe.matmul(PS[0:KP, 3 + n % 3, 0:NT], khi[:, slot, keys], qb1[:, slot, cut], start=True, stop=False)
                pe.matmul(PS[0:KP, 3 + n % 3, 0:NT], klo[:, slot, keys], qb2[:, slot, cut],
                          start=False, stop=True).then_inc(c_sm, 1)

            def values(b, slot, n):
                j, hf = n // 2, n % 2
                pe.wait_ge(c_ex, LS * b + (n + 4))
                if n == 0:
                    pe.wait_ge(c_cx, b + 1)
                pe.matmul(PS[0:DC + 1, 6 + hf, 0:NT], kvr[:, slot, j, DC:2 * DC + 1], pe3[:, n % 3, :],
                          start=j == 0, stop=j == KT - 1).then_inc(c_pv, 1)

            def spread_recip(b, rows):
                pe.wait_ge(c_rd, b + 1)
                pe.wait_ge(c_mr, (LH // 2) * rows)
                for hf in range(2):
                    mm = pe.matmul(PS[0:DC, hf, 0:NT], ones[DC:DC + 1, 0:DC], rden[DC:DC + 1, hf, :], start=True, stop=True)
                mm.then_inc(c_bc, 1)

            def latent_out(hf):
                for m in range(KC):
                    for k in range(LH // 2):
                        mm = pe.matmul(bank(m), wvo[:, k, m * P:(m + 1) * P], cn[:, k, hf * HB:(hf + 1) * HB, :],
                                       start=k == 0, stop=k == LH // 2 - 1)
                mm.then_inc(c_om, 1)

            def latent_batch(b, slot, nth, last, prepare):
                rows = b + 1 if prepare is None else b + 2
                pe.wait_ge(c_row[slot], 16 * nth)
                for n in range(LS + 2):
                    if n < LS:
                        scores(b, slot, n)
                    if n >= 2:
                        values(b, slot, n - 2)
                    if prepare is not None and n == KEYS_AT:
                        keys_t(prepare, 1 - slot)
                    k, odd = divmod(n - KEYS_AT - 4, 2)
                    if prepare is not None and not odd and 0 <= k < LH // 2:
                        row_scores(prepare, 1 - slot, k)
                    if n == KEYS_AT + 4 + LH:
                        if prepare is not None:
                            max_t(prepare)
                    if last is not None and n == KEYS_AT + 5 + LH:
                        spread_recip(last, rows)

            keys_t(0, 0)
            for k in range(LH // 2):
                row_scores(0, 0, k)
            max_t(0)
            latent_batch(0, 0, 1, None, 1)
            with pe.Fori(0, B // 2 - 1) as j:
                for d in range(2):
                    b = 2 * j + (1 + d)
                    latent_batch(b, 1 - d, j + (1 + d), 2 * j + d, 2 * j + (2 + d))
            latent_batch(B - 1, 1, B // 2, B - 2, None)
            spread_recip(B - 1, B)
            pe.wait_ge(c_cn, B + 1)
            for hf in range(2):
                if hf == 1:
                    pe.wait_ge(c_xu, 1)
                latent_out(hf)
            pe.wait_ge(s_xr, 11)
            for i in range(PAIRS):
                for c in range(KC):
                    mm = pe.transpose(PS[:, i // 2, (i % 2) * C + c * P:(i % 2) * C + (c + 1) * P],
                                      xT[:, c, 2 * i:2 * i + 2, :], ident[:])
                mm.then_inc(f_xm, 1)
            pb = PS[:].rearrange("p k n -> p (k n)").bitcast(BF16).rearrange("p (k n) -> p k n", k=8)
            pe.wait_ge(s_c6, 2)
            pe.wait_ge(f_ki, 1)
            for fc in range(KC):
                for dc in range(KC):
                    pe.transpose(pb[:, 6, (dc * KC + fc) * P:(dc * KC + fc + 1) * P], kwi[:, fc, dc * P:(dc + 1) * P], identb[:])
            for fc in range(KC):
                mm = pe.matmul(PS[:, 7, fc * P:(fc + 1) * P], one6[:], kdg[:, fc, :], start=True, stop=True)
            mm.then_inc(f_km, 1)
            for i in range(PAIRS):
                pe.wait_ge(f_xi, i + 1)
                pe.wait_ge(f_xc, PAIRS)
                if i >= 2:
                    pe.wait_ge(f_tc, i - 1)
                for c in range(KC):
                    mm = pe.transpose(pb[:, 4 + i % 2, c * P:(c + 1) * P], xi[:, i, c * P:(c + 1) * P], identb[:])
                mm.then_inc(f_tm, 1)
            pe.wait_ge(f_kc, 1)
            for i in range(PAIRS):
                pe.wait_ge(f_tc, i + 1)
                if i >= 4:
                    pe.wait_ge(f_o, i - 3)
                for c in range(KC):
                    mm = pe.matmul(PS[:, i % 4, 0:C], xiT[:, c, i * P:(i + 1) * P], kwT[:, c, :],
                                   start=c == 0, stop=c == KC - 1)
                mm.then_inc(f_ym, 1)

        @block.scalar
        def _(act):
            act.wait_ge(s_const, 6)
            ln_act(act, 0)
            act.wait_ge(s_w1, 32)
            for hf in range(2):
                if hf == 1:
                    act.wait_ge(s_xr, 3)
                for m in range(4):
                    act.wait_ge(s_par, 4 * hf + m + 1)
                    o = (gate_s, val_s)[m // 2][:, m % 2, :]
                    act.activation(o, PS[:, 4 + m, 0:NT], (ACT.Sigmoid, ACT.Tanh)[m // 2],
                                   bias=b0[:, m:m + 1]).then_inc(s_pact, 1)
            ln_act(act, 1)
            with act.Fori(0, PAIRS) as i:
                act.wait_ge(x_qm, i + 1)
                act.copy(qp[:].rearrange("p m b t -> p (m b t)"), PS[:, 0, :]).then_inc(x_qc, 1)
                act.wait_ge(x_vm, i + 1)
                act.copy(vp[:, :, :, 0:XD], PS[:, 2, :].rearrange("p (b h d) -> p b h d", b=2, h=XH)).then_inc(x_vc, 1)
                act.wait_ge(x_sh, i + 1)
                act.activation(pr[:, :, 0:T], sc[:], ACT.Exp).then_inc(x_ex, 1)
                act.wait_ge(x_tm, i + 1)
                act.copy(pt[:], PS[:, 0:2, :].rearrange("p k (m n) -> p (k m) n", n=P)).then_inc(x_tc, 1)
            ln_act(act, 2)
            act.wait_ge(e_lm, 1)
            act.copy(logit[:].rearrange("p i e -> p (i e)"), PS[:, 4:6, :].rearrange("p k n -> p (k n)")).then_inc(e_lc, 1)
            act.wait_ge(e_sh, 1)
            act.activation(expo[:], expo[:], ACT.Exp).then_inc(e_ex, 1)
            act.wait_ge(e_tm, 1)
            act.copy(coT[:].rearrange("p b t -> p (b t)"), PS[:, 6:8, :].rearrange("p k n -> p (k n)")).then_inc(e_tc, 1)
            for n in range(2 * (KB + 2)):
                act.wait_ge(e_gm, n + 1)
                if n >= 2:
                    act.wait_ge(e_pd, n - 1)
                act.activation(sgl[:, n % 2, :], PS[:, 3 * (n % 2), 0:NT], ACT.Silu).then_inc(e_si, 1)
            ln_act(act, 3)
            act.wait_ge(s_w4, 16 * 13)
            act.wait_ge(s_c4, 10)
            own = Own(act, own_a)
            act.wait_ge(d_ng, 1)
            own.step(act.activation(alog[:], alog[:], ACT.Exp))
            own.step(act.mul(alog[:], alog[:], -1.0))
            for hf in range(2):
                act.wait_ge(d_mm, hf + 1)
                raw = PS[0:NH, 6 + hf, 0:NT]
                act.activation(dts[:, 2 + hf, :], raw, ACT.Relu, bias=dtb[:])
                own.step(act.activation(dts[:, hf, :], raw, ACT.Abs, bias=dtb[:]))
                own.step(act.activation(dts[:, hf, :], dts[:, hf, :], ACT.Tanh, scale=0.5))
            for hf in range(2):
                act.activation(dts[:, hf, :], dts[:, hf, :], ACT.Ln, scale=0.5, bias=cst[0:NH, 0:1]).then_inc(d_ln, 1)
            for hf in range(2):
                act.wait_ge(d_dt, hf + 1)
                act.activation(aT[:, HB * hf:HB * hf + HB, :], dtc[:, HB * hf:HB * hf + HB, 0:T], ACT.Exp,
                               scale=alog[:]).then_inc(d_ex, 1)
            for n in range(4):
                bb = 3 * (n % 2)
                act.wait_ge(b_mm, n + 1)
                if n >= 1:
                    act.wait_ge(b_ms, n)
                act.activation(bsq, PS[:, bb, 0:NT], ACT.Square).then_inc(b_sq, 1)
                act.wait_ge(b_ms, n + 1)
                if n >= 1:
                    act.wait_ge(b_n, n)
                act.activation(bst, PS[:, bb + 2, 0:NT], ACT.Sqrt, scale=2.0 * P / 128, bias=cst[:, 1:2]).then_inc(b_sd, 1)
            act.wait_ge(d_tm, 1)
            act.copy(dtt[:].rearrange("p i h -> p (i h)"), PS[:, 6, :]).then_inc(d_tc, 1)
            for i in range(PAIRS):
                act.wait_ge(z_mm, i + 1)
                act.activation(siz[:, i, :], PS[:, 2 * (i % 2), :], ACT.Silu).then_inc(z_si, 1)

            def ssm_sines(hp, slot):
                act.wait_ge(m_fr, hp + 1)
                if not isinstance(hp, int) or hp >= 2:
                    act.wait_ge(m_tc, hp - 1)
                own.step(act.activation(cs[:, slot, :], frac[:, slot, :], ACT.Abs))
                act.activation(sn[:, slot, :], frac[:, slot, :], ACT.Sin, scale=-TWO_PI)
                own.step(act.activation(cs[:, slot, :], cs[:, slot, :], ACT.Sin, scale=-TWO_PI, bias=cst[:, 2:3]))
                act.sem_inc(m_sin, 1)

            def ssm_copy_y(hp, slot):
                act.wait_ge(m_y, hp + 1)
                for h2 in range(2):
                    at = hp * 2 * HD + h2 * HD
                    at = slice(at, at + HD) if isinstance(hp, int) else bass.ds(at, HD)
                    y = PS[64 * h2:64 * h2 + 64, 4 + slot, 0:4 * HD * PAIRS].rearrange("p (i b n) -> p i b n", b=2, n=2 * HD)
                    for b2 in range(2):
                        ins = act.copy(ya[64 * b2:64 * b2 + 64, :, at], y[:, :, b2, h2 * HD:(h2 + 1) * HD])
                ins.then_inc(m_yc, 1)

            def ssm_scalar(k, p):
                if not isinstance(k, int) or 1 <= k:
                    ssm_copy_y(k - 1, 1 - p)
                if not isinstance(k, int) or k + 3 < NP2:
                    ssm_sines(k + 3, 1 - p)

            for k in range(-3, 2):
                ssm_scalar(k, k % 2)
            with act.Fori(0, SSM_TRIPS) as j:
                own.enter(j, 4)
                for d in range(2):
                    ssm_scalar(2 * j + (2 + d), d)
            own.leave(SSM_TRIPS)
            for k in range(NP2 - 4, NP2 + 1):
                ssm_scalar(k, k % 2)
            for i in range(PAIRS):
                act.wait_ge(g_g, i + 1)
                act.activation(ysq[:, 0, 0:DI], ya[:, i, :], ACT.Square, accum_out=yss[:, i:i + 1]).then_inc(g_sq, 1)
                act.wait_ge(g_sq, i + 1)
            act.activation(yss[:], yss[:], ACT.Sqrt, scale=1.0 / DI, bias=cst[:, 1:2]).then_inc(g_sd, 1)
            ln_act(act, 4)

            def latent_copies(h, pair, slot, absorb):
                act.wait_ge(k_w, h + 1)
                if not isinstance(h, int) or h >= 2:
                    act.wait_ge(k_a, 2 * h - 2)
                act.copy(wab[:, slot, :, :].rearrange("p r n -> p (r n)"), PS[0:RQ, 6, 0:256])
                rows = slice(DC * slot, DC * slot + DC)
                w = wvo[rows, pair, :] if isinstance(h, int) else wvo[rows, bass.ds(pair, 1), :].rearrange("p o n -> p (o n)")
                act.copy(w, PS[0:DC, 6, 256:512]).then_inc(k_wc, 1)
                for hf in range(2):
                    act.wait_ge(k_q, 2 * h + (hf + 1))
                    if not isinstance(h, int) or h >= 1:
                        act.wait_ge(k_b, 2 * h + (hf - 1))
                    act.copy(qh[:, hf, :], PS[:, hf, 0:NT]).then_inc(k_qc, 1)
                if absorb is not None:
                    latent_high(absorb)

            def latent_high(h):
                for hf in range(2):
                    act.wait_ge(k_a, 2 * h + (hf + 1))
                    hs = slice(h, h + 1) if isinstance(h, int) else bass.ds(h, 1)
                    act.copy(qa[:, HB * hf:HB * hf + HB, hs, :].rearrange("p b o t -> p b (o t)"), bank(7 - hf)).then_inc(k_hi, 1)

            act.sem_inc(c_ex, 3)
            act.wait_ge(s_xn, 10)
            latent_copies(0, 0, 0, None)
            with act.Fori(0, LH // 2 - 1) as j:
                for d in range(2):
                    latent_copies(2 * j + (1 + d), j + d, (1 + d) % 2, 2 * j + d)
            latent_copies(LH - 1, LH // 2 - 1, 1, LH - 2)
            latent_high(LH - 1)

            def keys_high(b, slot, k):
                act.wait_ge(c_tm, b + 1)
                act.copy(khi[:, slot, k * (S // 3):(k + 1) * (S // 3)], PS[:, k, 0:S // 3]).then_inc(c_khi, 1)

            def max_row(b, slot):
                act.wait_ge(c_mt, b + 1)
                act.mul(rmn[:], PS[0:LH // 2, 2, 0:2 * T], -1.0).then_inc(c_mn, 1)
                act.wait_ge(c_mn, b + 1)
                act.dma_start(qb2[DC:DC + 1, slot, :].rearrange("o (k n) -> o k n", k=LH // 2), rmn[:]).then_inc(c_row[slot], 16)

            def latent_exp(b, slot, nth, prepare):
                for n in range(LS):
                    act.wait_ge(c_sm, LS * b + (n + 1))
                    act.wait_ge(c_pv, LS * b + (n + 1))
                    act.activation(pe3[:, n % 3, :], PS[0:KP, 3 + n % 3, 0:NT], ACT.Exp).then_inc(c_ex, 1)
                    if prepare is not None and 0 <= n - KEYS_AT < 3:
                        keys_high(prepare, 1 - slot, n - KEYS_AT)
                    if prepare is not None and n == KEYS_AT + 3 + LH:
                        max_row(prepare, 1 - slot)

            for k in range(3):
                keys_high(0, 0, k)
            max_row(0, 0)
            latent_exp(0, 0, 1, 1)
            with act.Fori(0, B // 2 - 1) as j:
                for d in range(2):
                    latent_exp(2 * j + (1 + d), 1 - d, None, 2 * j + (2 + d))
            latent_exp(B - 1, 1, None, None)
            pb = PS[:].rearrange("p k n -> p (k n)").bitcast(BF16).rearrange("p (k n) -> p k n", k=8)
            for i in range(PAIRS):
                act.wait_ge(f_xm, 2 * (i // 2) + 2)
                act.copy(xt[:, i, :], PS[:, i // 2, (i % 2) * C:(i % 2 + 1) * C]).then_inc(f_xc, 1)
            act.wait_ge(f_va, 1)
            act.activation(sx[:, 0, :], mv6[:, :, 1], ACT.Sqrt, bias=epsc[:]).then_inc(f_sd, 1)
            act.wait_ge(f_km, 1)
            act.copy(kwT[:].rearrange("p c f -> p (c f)"), pb[:, 6, 0:KC * C])
            act.copy(skb[:], PS[:, 7, 0:C]).then_inc(f_kc, 1)
            for i in range(PAIRS):
                act.wait_ge(f_tm, i + 1)
                act.copy(xiT[:, :, i * P:(i + 1) * P], pb[:, 4 + i % 2, 0:C].rearrange("p (c n) -> p c n", n=P)).then_inc(f_tc, 1)

        @block.vector
        def _(v):
            own = Own(v, own_v)
            v.wait_ge(s_const, 6)
            v.wait_ge(s_x, 16)
            for hf in range(2):
                v.nop().then_inc(s_xr, 1)
            ln_dve(v, own, 0)
            for hf in range(2):
                v.wait_ge(s_pact, 4 * hf + 4)
                own.step(v.memset(cols(gate_s[:].rearrange("p c n -> p (c n)"))[:, :, 0:1], 0.0))
                for c in range(KC):
                    own.done(v.tensor_tensor_scan(hid[:, c, :], gate_s[:, c, :], val_s[:, c, :], 0.0, ALU.mult, ALU.add))
                own.wait()
                for c in range(KC):
                    ins = v.tensor_tensor(half(xT, c, hf), half(xT, c, hf), cols(hid[:, c, :]), ALU.add)
                ins.then_inc(s_xr, 1)
                v.wait_ge(s_xr, 3 + hf)
            v.nop().then_inc(x_oc, 1)
            ln_dve(v, own, 1)
            with v.Fori(0, PAIRS) as i:
                own.enter(i, 4)
                v.wait_ge(x_km, i + 1)
                v.tensor_copy(kp[:].rearrange("p m b t -> p (m b t)"), PS[:, 1, :]).then_inc(x_kc, 1)
                v.wait_ge(x_sm, i + 1)
                mask = maskc[:].unsqueeze(1).broadcast_to((P, 4, T))
                for r in range(4):
                    s_r = PS[:, 4 + r, 0:4 * TP].rearrange("p (c t) -> p c t", t=TP)[:, :, 0:T]
                    ins = v.scalar_tensor_tensor(sc[:, 4 * r:4 * r + 4, :], s_r, XD ** -0.5, mask,
                                                 ALU.mult, ALU.add)
                own.step(ins)
                own.step(v.tensor_reduce(mxs[:], sc[:], AX, ALU.max))
                v.tensor_tensor(sc[:], sc[:], mxs[:].unsqueeze(2).broadcast_to((P, XH, T)),
                                ALU.subtract).then_inc(x_sh, 1)
                v.wait_ge(x_ex, i + 1)
                own.step(v.tensor_reduce(sms[:], pr[:, :, 0:T], AX, ALU.add))
                own.step(v.reciprocal(sms[:], sms[:]))
                v.tensor_tensor(pr[:, :, 0:T], pr[:, :, 0:T], sms[:].unsqueeze(2).broadcast_to((P, XH, T)),
                                ALU.mult).then_inc(x_pr, 1)
                v.wait_ge(x_om, i + 1)
                for e in range(2):
                    ins = v.tensor_copy(oT[:, e::2, bass.ds(2 * i, 2), 0:T],
                                        PS[:, 2 + e, 0:4 * T].rearrange("p (c b t) -> p c b t", c=2, b=2))
                ins.then_inc(x_oc, 1)
            own.leave(PAIRS)
            for hf in range(2):
                for m in range(KC):
                    v.wait_ge(x_wm, 2 * hf + m + 1)
                    ins = v.tensor_tensor(half(xT, m, hf), half(xT, m, hf), bank(4 + 2 * hf + m), ALU.add)
                ins.then_inc(s_xr, 1)
            v.wait_ge(s_xr, 6)
            v.wait_ge(s_w3, 16 * 9)
            own.step(v.tensor_tensor(amps[:], amps[:], amps[:], ALU.mult))
            own.step(v.tensor_tensor(mix[:], amps[:, 0, :], amps[:, 1, :], ALU.add))
            own.step(v.tensor_reduce(msum[:], mix[:], AX, ALU.add))
            own.step(v.tensor_scalar(msum[:], msum[:], 1e-8, None, ALU.add))
            own.step(v.reciprocal(msum[:], msum[:]))
            own.step(v.tensor_scalar(mix[:], mix[:], msum[:], escale[:], ALU.mult, ALU.mult))
            v.tensor_copy(mixb[:], mix[:].unsqueeze(2).broadcast_to((P, KB, P))).then_inc(e_mix, 1)
            ln_dve(v, own, 2)
            v.wait_ge(e_lc, 1)
            v.wait_ge(s_keep, 1)
            for i in range(PAIRS):
                ins = v.max(top8[:, i, :], logit[:, i, :])
            own.step(ins)
            shape = (P, PAIRS, E)
            v.tensor_tensor(expo[:], logit[:], top8[:, :, 0:1].broadcast_to(shape), ALU.subtract).then_inc(e_sh, 1)
            own.done(v.tensor_tensor(above[:], logit[:], top8[:, :, TOPK - 1:TOPK].broadcast_to(shape), ALU.is_gt))
            own.step(v.tensor_tensor(level[:], logit[:], top8[:, :, TOPK - 1:TOPK].broadcast_to(shape), ALU.is_equal))
            own.done(v.tensor_reduce(room[:], above[:], AX, ALU.add))
            own.step(v.tensor_tensor_scan(place[:].rearrange("p i e -> p (i e)"), keep[:],
                                          level[:].rearrange("p i e -> p (i e)"), 0.0, ALU.mult, ALU.add))
            own.step(v.tensor_scalar(room[:], room[:], -1.0, float(TOPK), ALU.mult, ALU.add))
            own.step(v.tensor_tensor(place[:], place[:], room[:].unsqueeze(2).broadcast_to(shape), ALU.is_le))
            own.step(v.tensor_tensor(level[:], level[:], place[:], ALU.mult))
            own.step(v.tensor_tensor(level[:], level[:], above[:], ALU.add))
            v.wait_ge(e_ex, 1)
            own.step(v.tensor_reduce(zsum[:], expo[:], AX, ALU.add))
            own.step(v.tensor_tensor(expo[:], expo[:], level[:], ALU.mult))
            own.step(v.tensor_reduce(tsum[:], expo[:], AX, ALU.add))
            own.step(v.scalar_tensor_tensor(tsum[:], zsum[:], 1e-8, tsum[:], ALU.mult, ALU.add))
            own.step(v.reciprocal(tsum[:], tsum[:]))
            v.tensor_tensor(expo[:], expo[:], tsum[:].unsqueeze(2).broadcast_to(shape), ALU.mult).then_inc(e_co, 1)
            for hf in range(2):
                for k in range(KB + 2):
                    n = hf * (KB + 2) + k
                    gb = 3 * (n % 2)
                    v.wait_ge(e_si, n + 1)
                    v.wait_ge(e_um, n + 1)
                    if k < KB:
                        own.step(v.tensor_tensor(gu[:, n % 2, :], sgl[:, n % 2, :], PS[:, gb + 1, 0:NT], ALU.mult))
                        if k == 0:
                            v.tensor_tensor(acc[:, hf, :], gu[:, n % 2, :], PS[:, gb + 2, 0:NT], ALU.mult).then_inc(e_pd, 1)
                            v.wait_ge(e_pd, n + 1)
                        else:
                            v.tensor_tensor(wgu[:], gu[:, n % 2, :], PS[:, gb + 2, 0:NT], ALU.mult).then_inc(e_pd, 1)
                            v.wait_ge(e_pd, n + 1)
                            own.step(v.tensor_tensor(acc[:, hf, :], acc[:, hf, :], wgu[:], ALU.add))
                    else:
                        v.tensor_tensor(shr[:, hf, k - KB, :], sgl[:, n % 2, :], PS[:, gb + 1, 0:NT],
                                        ALU.mult).then_inc(e_pd, 1)
                v.wait_ge(e_pd, (hf + 1) * (KB + 2))
                v.sem_inc(e_ac, 1)
            for hf in range(2):
                for m in range(KC):
                    v.wait_ge(e_dm, 2 * hf + m + 1)
                    ins = v.tensor_tensor(half(xT, m, hf), half(xT, m, hf), bank(6 + m), ALU.add)
                ins.then_inc(s_xr, 1)
            v.wait_ge(s_xr, 8)
            v.wait_ge(s_w4, 16 * 13)
            v.wait_ge(s_c4, 10)
            v.tensor_scalar(alog[:], alog[:], 80.0, None, ALU.min).then_inc(d_ng, 1)
            ln_dve(v, own, 3)
            for hf in range(2):
                v.wait_ge(d_ln, hf + 1)
                v.tensor_tensor(dtc[:, HB * hf:HB * hf + HB, 0:T], cols(dts[:, 2 + hf, :]), cols(dts[:, hf, :]),
                                ALU.subtract).then_inc(d_dt, 1)
            for hf in range(2):
                v.wait_ge(d_dt, hf + 1)
                own.step(v.tensor_copy(dts[:, hf, :].rearrange("p (b t) -> p b t", t=T), dtc[:, HB * hf:HB * hf + HB, 0:T]))
                v.tensor_tensor_scan(cum[:, hf * NT:(hf + 1) * NT], keept[:], dts[:, hf, :], 0.0,
                                     ALU.mult, ALU.add).then_inc(d_cum, 1)
            for hf in range(2):
                v.wait_ge(d_ex, hf + 1)
                v.memset(aT[:, HB * hf:HB * hf + HB, 0:1], 0.0).then_inc(d_a, 1)
            for n in range(4):
                hf, x, bb = n // 2, n % 2, 3 * (n % 2)
                v.wait_ge(b_sd, n + 1)
                own.step(v.reciprocal(bst, bst))
                for s in range(2):
                    ins = v.tensor_tensor(bcn[:, 2 * x + s, hf * NT:(hf + 1) * NT], PS[:, bb + s, 0:NT], bst, ALU.mult)
                ins.then_inc(b_n, 1)
                v.wait_ge(b_n, n + 1)
            v.wait_ge(d_tc, 1)
            for i in range(PAIRS):
                v.wait_ge(z_mm, i + 1)
                xs = PS[:, 2 * (i % 2) + 1, :].rearrange("p (h q) -> p h q", q=HD)
                v.tensor_tensor(dx[:, i, :].rearrange("p (h q) -> p h q", q=HD), xs,
                                dbc[:].unsqueeze(2).broadcast_to((P, NH, HD)), ALU.mult)
                v.tensor_tensor(ua[:, i, :].rearrange("p (h q) -> p h q", q=HD), xs,
                                dtt[:, i, :].unsqueeze(2).broadcast_to((P, NH, HD)), ALU.mult).then_inc(z_u, 1)

            def ssm_rotation(hp, slot):
                v.wait_ge(m_phi, hp + 1)
                phi = PS[:, 0:2, 0:NT]
                own.step(v.tensor_scalar(turn[:].rearrange("p (k n) -> p k n", k=2), phi, ROUND, -ROUND, ALU.add, ALU.add))
                if not isinstance(hp, int) or hp >= 2:
                    v.wait_ge(m_sin, hp - 1)
                v.tensor_tensor(frac[:, slot, :].rearrange("p (k n) -> p k n", k=2),
                                turn[:].rearrange("p (k n) -> p k n", k=2), phi, ALU.subtract).then_inc(m_fr, 1)

            def ssm_products(hp, slot):
                v.wait_ge(m_sin, hp + 1)
                for x, s in ((0, m_tb), (1, m_tc)):
                    if not isinstance(hp, int) or hp >= 1:
                        v.wait_ge((m_rb, m_rc)[x], (1 + x) * hp)
                    for k, tab in ((2 * x, cs), (2 * x + 1, sn)):
                        bk = bias[:, k, hp:hp + 1] if isinstance(hp, int) else bias[:, k, bass.ds(hp, 1)]
                        ins = v.scalar_tensor_tensor(rt[:, k, :], bcn[:, k, :], bk, tab[:, slot, :], ALU.add, ALU.mult)
                    ins.then_inc(s, 1)

            def ssm_scan(hp, slot, nth):
                v.wait_ge(m_abc[slot], 32 * nth)
                v.tensor_tensor_scan(dec[:], ab[:, slot, :], eye[:], 0.0, ALU.mult, ALU.add).then_inc(m_sc, 1)

            def ssm_decay(hp, slot):
                v.wait_ge(m_sc, hp + 1)
                if not isinstance(hp, int) or hp >= 2:
                    v.wait_ge(m_y, hp - 1)
                v.wait_ge(m_g, hp + 1)
                for q in range(2):
                    blocks = slice(q * PAIRS, (q + 1) * PAIRS)
                    ins = v.tensor_tensor(mt[:, slot, blocks, 0:T], bank(2 + q),
                                          dec[:].rearrange("p (n t) -> p n t", t=T)[:, blocks, :], ALU.mult)
                ins.then_inc(m_mt, 1)
                v.wait_ge(m_mt, hp + 1)

            def ssm_vector(k, p, nth):
                if not isinstance(k, int) or 0 <= k < NP2:
                    ssm_scan(k, p, nth)
                if not isinstance(k, int) or 0 <= k + 1 < NP2:
                    ssm_products(k + 1, 1 - p)
                if not isinstance(k, int) or 0 <= k < NP2:
                    ssm_decay(k, p)
                if not isinstance(k, int) or k + 3 < NP2:
                    ssm_rotation(k + 3, 1 - p)

            for k in range(-3, 2):
                ssm_vector(k, k % 2, 1)
            with v.Fori(0, SSM_TRIPS) as j:
                own.enter(j, 2)
                for d in range(2):
                    ssm_vector(2 * j + (2 + d), d, j + 2)
            own.leave(SSM_TRIPS)
            for k in range(NP2 - 4, NP2):
                ssm_vector(k, k % 2, k // 2 + 1)
            v.wait_ge(m_yc, NH // 2)
            for i in range(PAIRS):
                own.step(v.scalar_tensor_tensor(ya[:, i, :], ya[:, i, :], DS ** -0.5, dx[:, i, :], ALU.mult, ALU.add))
                v.tensor_tensor(ya[:, i, :], ya[:, i, :], siz[:, i, :], ALU.mult).then_inc(g_g, 1)
            v.wait_ge(g_sd, 1)
            own.step(v.reciprocal(yss[:], yss[:]))
            for i in range(PAIRS):
                v.tensor_scalar(ya[:, i, :], ya[:, i, :], yss[:, i:i + 1], None, ALU.mult).then_inc(g_n, 1)
            for i in range(PAIRS):
                v.wait_ge(g_tm, i + 1)
                for b2 in range(2):
                    o = gT[:, :, (2 * i + b2) * T:(2 * i + b2 + 1) * T]
                    s = PS[:, i % 2, :].rearrange("p (c n) -> p c n", n=P)[:, :, 64 * b2:64 * b2 + T]
                    ins = v.tensor_tensor(o, s, nw[:].unsqueeze(2).broadcast_to((P, DI // P, T)), ALU.mult)
                ins.then_inc(g_tc, 1)
            for hf in range(2):
                for m in range(KC):
                    v.wait_ge(g_wm, 2 * hf + m + 1)
                    ins = v.tensor_tensor(half(xT, m, hf), half(xT, m, hf), bank(4 + 2 * hf + m), ALU.add)
                ins.then_inc(s_xr, 1)
            v.wait_ge(s_xr, 10)
            ln_dve(v, own, 4)
            v.sem_inc(k_lo, 1)
            v.sem_inc(c_pv, 3)
            v.sem_inc(c_cx, 1)
            v.sem_inc(c_cn, 1)
            v.wait_ge(s_w5, 48)

            def latent_products(h, hf):
                v.wait_ge(k_b, 2 * h + (hf + 1))
                if not isinstance(h, int) or h >= 1:
                    v.wait_ge(k_r, 2 * h + (hf - 1))
                for n, (r, k) in enumerate(((0, 0), (1, 1), (1, 2), (0, 3))):
                    ins = v.tensor_tensor(cols(rp4[:, hf, n, :]), bank(2 + 2 * hf + r, rows=slice(0, RQ)),
                                          rqt[:, k:k + 1, :].broadcast_to((RQ, HB, T)), ALU.mult)
                ins.then_inc(k_p, 1)

            def latent_low(h):
                for hf in range(2):
                    v.wait_ge(k_hi, 2 * h + (hf + 1))
                    hs = slice(h, h + 1) if isinstance(h, int) else bass.ds(h, 1)
                    q = qa[DC:P, HB * hf:HB * hf + HB, hs, :].rearrange("p b o t -> p b (o t)")
                    v.tensor_tensor(q, bank(7 - hf, rows=slice(DC, P)), q, ALU.subtract).then_inc(k_lo, 1)

            for hf in range(2):
                latent_products(0, hf)
            with v.Fori(1, LH) as h:
                latent_low(h - 1)
                for hf in range(2):
                    latent_products(h, hf)
            latent_low(LH - 1)
            v.wait_ge(k_lo, 2 * LH + 1)

            def keys_low(b, slot):
                v.wait_ge(c_khi, 3 * b + 3)
                v.tensor_tensor(klo[0:DC, slot, :].rearrange("p (k n) -> p k n", k=3), PS[0:DC, 0:3, 0:S // 3],
                                khi[0:DC, slot, :].rearrange("p (k n) -> p k n", k=3), ALU.subtract).then_inc(c_klo, 1)
                src = qa[:, b:b + 1] if isinstance(b, int) else qa[:, bass.ds(b, 1)]
                src = src.rearrange("p o h t -> p (o h t)")
                v.tensor_copy(qb1[:, slot, :], src)
                v.tensor_copy(qb2[0:DC, slot, :], src[0:DC]).then_inc(c_qb, 1)

            def row_max(b, k):
                v.wait_ge(c_mm, (LH // 2) * b + (k + 1))
                if k == 0 and (not isinstance(b, int) or b >= 1):
                    v.wait_ge(c_mt, b)
                v.tensor_reduce(rmx[:, k:k + 1], PS[0:2 * T, 0:3, 0:S // 3], XY, ALU.max).then_inc(c_mr, 1)

            def latent_sums(b):
                v.wait_ge(c_pv, LS * b + (LS + 3))
                v.wait_ge(c_cn, b + 1)
                v.tensor_copy(cx[:], PS[0:DC + 1, 6:8, 0:NT]).then_inc(c_cx, 1)

            def latent_recip(b, k):
                if k == 0:
                    v.wait_ge(c_cx, b + 2)
                part = slice(k % 4 * (NT // 4), (k % 4 + 1) * (NT // 4))
                ins = v.reciprocal(rden[DC:DC + 1, k // 4, part], cx[DC:DC + 1, k // 4, part])
                if k == 7:
                    ins.then_inc(c_rd, 1)

            def latent_update(b):
                v.wait_ge(c_bc, b + 1)
                for odd in range(2):
                    o = cn[DC * odd:DC * odd + DC, :, b:b + 1, :] if isinstance(b, int) else cn[DC * odd:DC * odd + DC, :, bass.ds(b, 1), :]
                    o = o.rearrange("p (k h) o t -> p k h (o t)", k=2)
                    x, r = (a.rearrange("p k (h t) -> p k h t", t=T)[:, :, odd::2, :] for a in (cx[0:DC, :, :], PS[0:DC, 0:2, 0:NT]))
                    ins = v.tensor_tensor(o, x, r, ALU.mult)
                ins.then_inc(c_cn, 1)

            keys_low(0, 0)
            for k in range(LH // 2):
                row_max(0, k)

            def latent_vector(b, slot, last, prepare):
                if last is not None:
                    latent_sums(last)
                if prepare is not None:
                    keys_low(prepare, 1 - slot)
                for k in range(8):
                    if prepare is not None:
                        row_max(prepare, k)
                    if last is not None:
                        latent_recip(last, k)
                if last is not None:
                    latent_update(last)

            latent_vector(0, 0, None, 1)
            with v.Fori(0, B // 2 - 1) as j:
                for d in range(2):
                    latent_vector(2 * j + (1 + d), 1 - d, 2 * j + d, 2 * j + (2 + d))
            latent_vector(B - 1, 1, B - 2, None)
            latent_sums(B - 1)
            for k in range(8):
                latent_recip(B - 1, k)
            latent_update(B - 1)
            for hf in range(2):
                v.wait_ge(c_om, hf + 1)
                for m in range(KC):
                    ins = v.tensor_tensor(half(xT, m, hf), half(xT, m, hf), bank(m), ALU.add)
                ins.then_inc(c_xu, 1)
            v.wait_ge(c_xu, 2)
            v.sem_inc(s_xr, 1)

            def quant_scale(s):
                own.step(v.tensor_scalar(s[:, 3], s[:, 0], 0.0, None, ALU.is_equal))
                own.step(v.scalar_tensor_tensor(s[:, 1], s[:, 0], 1.0 / 127.0, s[:, 3], ALU.mult, ALU.add))
                own.step(v.reciprocal(s[:, 2], s[:, 1]))

            def whole(o, a, inv):
                own.step(v.tensor_scalar(o, a, inv, ROUND, ALU.mult, ALU.add))
                own.step(v.tensor_scalar(o, o, -ROUND, 127.0, ALU.add, ALU.min))
                return v.tensor_scalar(o, o, -127.0, None, ALU.max)

            v.wait_ge(s_w6, 32)
            own.step(v.tensor_reduce(sk[:, 0, :], kw[:], AX, ALU.max, apply_absolute_value=True))
            own.step(v.tensor_reduce(sbq[:, 0:1], bq[:], AX, ALU.max, apply_absolute_value=True))
            quant_scale(sk)
            quant_scale(sbq[:].unsqueeze(2))
            for c in range(KC):
                own.step(v.tensor_scalar(kdg[:, c, :], ident[:], sk[:, 1, c:c + 1], None, ALU.mult))
                whole(kw[:, c, :], kw[:, c, :], sk[:, 2, c:c + 1]).then_inc(own_v, 1)
                own.n += 1
            own.wait()
            v.tensor_copy(kwi[:], kw[:]).then_inc(f_ki, 1)
            own.step(whole(bqi[:], bq[:], sbq[:, 2:3]))
            own.step(v.tensor_scalar(bq[:], bqi[:], sbq[:, 1:2], None, ALU.mult))
            for i in range(PAIRS):
                v.wait_ge(f_xc, i + 1)
                own.done(v.bn_stats(st6[:, i, :], xt[:, i, :]))
            own.wait()
            for i in range(PAIRS):
                ins = v.bn_aggr(mv6[:, i, :], st6[:, i, :])
            ins.then_inc(f_va, 1)
            v.wait_ge(f_sd, 1)
            own.step(v.reciprocal(sx[:, 0, :], sx[:, 0, :]))
            for i in range(PAIRS):
                own.done(v.tensor_scalar(xq[:, i, :], xt[:, i, :], mv6[:, i, 0:1], sx[:, 0, i:i + 1], ALU.subtract, ALU.mult))
            own.wait()
            own.step(v.tensor_reduce(sx[:, 0, :], xq[:], AX, ALU.max, apply_absolute_value=True))
            quant_scale(sx)
            for i in range(PAIRS):
                own.step(whole(xq[:, i, :], xq[:, i, :], sx[:, 2, i:i + 1]))
                v.tensor_copy(xi[:, i, :], xq[:, i, :]).then_inc(f_xi, 1)
            v.wait_ge(f_kc, 1)
            for i in range(PAIRS):
                v.wait_ge(f_ym, i + 1)
                own.step(v.scalar_tensor_tensor(y6[:, i, :], PS[:, i % 4, 0:C], sx[:, 1, i:i + 1], skb[:], ALU.mult, ALU.mult))
                own.step(v.tensor_tensor(y6[:, i, :], y6[:, i, :], bq[:], ALU.add))
                own.step(v.tensor_scalar(y6[:, i, :], y6[:, i, :], 0.0, None, ALU.max))
                own.step(v.tensor_reduce(sy[:, 0, i:i + 1], y6[:, i, :], AX, ALU.max))
                quant_scale(sy[:, :, i:i + 1])
                own.step(whole(y6[:, i, :], y6[:, i, :], sy[:, 2, i:i + 1]))
                v.scalar_tensor_tensor(y6[:, i, :], y6[:, i, :], sy[:, 1, i:i + 1], xt[:, i, :], ALU.mult, ALU.add).then_inc(f_o, 1)


def pad_time(a):
    import numpy as np
    o = np.zeros(a.shape[:-1] + (TP,), a.dtype)
    o[..., :T] = a
    return o


def layouts(inp):
    import numpy as np
    f = np.float32
    L = {}
    L["xT"] = pad_time(inp["x"].transpose(2, 0, 1))
    L["W0"] = inp["L0_attn_W"].T
    L["b0"] = inp["L0_attn_b"].reshape(4, P).T
    wq = inp["L0_xattn_Wq"].reshape(XH, XD, C)
    pq = np.zeros((C, XH, XDP), f)
    pq[:, :, :XD] = wq.transpose(2, 0, 1)
    L["Wxq"] = pq.reshape(C, XH * XDP)
    wkv = inp["L0_xattn_Wkv_expand"]
    pk = np.zeros((64, XH, XDP), f)
    pk[:, :, :XD] = wkv[:C].reshape(XH, XD, 64).transpose(2, 0, 1)
    L["Wxk"] = pk.reshape(64, XH * XDP)
    L["Wxv"] = wkv[C:].T
    po = np.zeros((XH, XDP, C), f)
    po[:, :XD, :] = inp["L0_xattn_Wout"].T.reshape(XH, XD, C)
    L["Wxo"] = po.reshape(XH * XDP, C)
    L["ctx56"] = pad_time(inp["ctx_512"][:, :T, :].transpose(2, 0, 1))
    q = np.arange(P) % TP
    L["causal"] = np.where(np.arange(T)[None, :] <= q[:, None], f(0), f(NEG)).astype(f)
    L["Wr"], L["Wg"], L["Wu"], L["Wd"] = (inp["L0_ffn_" + n] for n in ("w_router", "w_gate", "w_up", "w_down"))
    L["Wsg"], L["Wsu"], L["Wsd"] = (inp["L0_ffn_shared_w_" + n] for n in ("gate", "up", "down"))
    L["amps"] = inp["L0_ffn_amplitudes"].transpose(0, 2, 1)
    L["escale"] = inp["L0_ffn_expert_scale"].reshape(P, 1)
    win = inp["L1_attn_W_in"]
    L["Wzx"] = win[:, :2 * DI]
    up = np.r_[0:DS:2, 1:DS:2]
    sw = np.r_[1:DS:2, 0:DS:2]
    wb, wc = win[:, 2 * DI:2 * DI + DS], win[:, 2 * DI + DS:2 * DI + 2 * DS]
    L["Wbc"] = np.stack([np.tile(w[:, o], (1, 2)) for w in (wb, wc) for o in (up, sw)], 1)
    L["Wdt"] = win[:, 2 * DI + 2 * DS:]
    L["Wmo"] = inp["L1_attn_W_out"]
    L["frow"] = np.tile(inp["L1_attn_rope_freqs"], (1, 4))
    bb, cb = inp["L1_attn_B_bias"], inp["L1_attn_C_bias"]
    L["bcbias"] = np.stack([w[:, o].reshape(NH // 2, P).T for w in (bb, cb) for o in (up, sw)], 1)
    L["dtb"] = inp["L1_attn_dt_bias"].reshape(NH, 1)
    L["alog"] = inp["L1_attn_A_log"].reshape(NH, 1)
    L["Dp"] = inp["L1_attn_D_param"].reshape(1, NH)
    L["nw"] = inp["L1_attn_norm_w"].reshape(DI // P, P).T
    L["sgn"] = np.tile((np.where(np.arange(P) % DS < DS // 2, -1.0, 1.0) / (2 * np.pi)).astype(f), (NH, 1))
    L["sel"] = (np.arange(NH)[:, None, None] == np.arange(NH).reshape(1, NH // 2, 2)).astype(f)
    L["eye"] = np.tile((np.arange(P)[:, None] % TP == np.arange(T)[None, :]).astype(f), (1, 2 * PAIRS))
    L["ctx"] = inp["ctx_512"]
    L["Lwq"] = inp["L1_xattn_Wq"].reshape(LH, P, KC, P).transpose(0, 3, 2, 1)
    L["Lwc"] = inp["L1_xattn_w_kc_q"]
    L["Lwr"] = inp["L1_xattn_W_qr"].transpose(0, 2, 1)
    L["Lwk"] = np.tile(inp["L1_xattn_W_kr"].transpose(0, 2, 1), (1, 1, 2))
    L["Lwv"] = inp["L1_xattn_w_kc_kv"]
    L["Lwo"] = inp["L1_xattn_Wo"].reshape(C, LH, P).transpose(1, 2, 0)

    def rope(length, dim):
        inv = (1.0 / f(10000.0) ** (np.arange(0, dim, 2, dtype=f) / f(dim))).astype(f)
        a = np.arange(length, dtype=f)[:, None] * inv[None, :]
        sin, cos = np.repeat(np.sin(a), 2, -1), np.repeat(np.cos(a), 2, -1)
        sin[:, :dim // 2] *= -1
        return sin, cos

    sin, cos = rope(T, 2 * RQ)
    L["rqt"] = np.stack([cos[:, :RQ].T, sin[:, :RQ].T, cos[:, RQ:].T, sin[:, RQ:].T], 1)
    sin, cos = rope(S, DC)
    L["rkc"], L["rks"] = cos.reshape(KP, KT, DC), sin.reshape(KP, KT, DC)
    L["kT"] = inp["L1_ffn_kernel"].T
    L["fb"] = inp["L1_ffn_bias"].reshape(1, C)
    return {k: np.ascontiguousarray(a) for k, a in L.items()}


def kernel(**inputs):
    import numpy as _np
    import concourse.bacc as _bacc
    from concourse import mybir as _mybir
    from concourse.bass_utils import run_bass_kernel_spmd as _run

    nc = _bacc.Bacc("TRN2", target_bir_lowering=False, num_devices=1)
    arrays, aps = {}, {}
    for name, a in layouts({k: _np.asarray(v) for k, v in inputs.items()}).items():
        arrays[f"in_{name}_dram"] = a
        aps[name] = nc.dram_tensor(f"in_{name}_dram", a.shape, _mybir.dt.from_np(a.dtype), kind="ExternalInput").ap()
    out = nc.dram_tensor("out_dram", (B, T, C), F32, kind="ExternalOutput").ap()
    decoder(nc, aps, out)
    r = _run(nc, [arrays], core_ids=[0])
    return r.results[0]["out_dram"]
```

```python
from contextlib import ExitStack

import concourse.bass as bass
from concourse import mybir

F32 = mybir.dt.float32
F16 = mybir.dt.float16
BF16 = mybir.dt.bfloat16
ALU = mybir.AluOpType
ACT = mybir.ActivationFunctionType
AX = mybir.AxisListType.X
XY = mybir.AxisListType.XY

P = 128
B, T, TP = 16, 56, 64
PAIRS = B // 2
HB = B // 2
NT = HB * T
BT = B * T
C = 256
KC = C // P
XH, XD, XDP = 16, 16, 32
E, TOPK, KB = 128, 4, 8
NEG = -1e30
LN_EPS = 1e-5
NH, HD, DS = 64, 8, 64
DI = NH * HD
NP2 = NH // 2
SSM_TRIPS = (NP2 - 6) // 2
LH, DC, RQ = 16, 64, 96
S, KT = 1500, 12
KP = S // KT
LR = LH * T
LS = 2 * KT
PIECES = 3 * LH // 2
KEYS_AT, ROWS_AT, MAX_AT = 5, 9, 22
SUMS_AT = 14
TWO_PI = 6.2831845
HALF_PI = 1.5707963
ROUND = 12582912.0


class Own:

    def __init__(self, eng, sem):
        self.eng, self.sem, self.n, self.i, self.per = eng, sem, 0, None, 0

    def enter(self, i, per):
        self.i, self.per, self.base = i, per, self.n
        self.n = 0

    def leave(self, trips):
        assert self.n == self.per, (self.n, self.per)
        self.n, self.i = self.base + trips * self.per, None

    def done(self, ins):
        ins.then_inc(self.sem, 1)
        self.n += 1

    def wait(self):
        if self.i is None:
            self.eng.wait_ge(self.sem, self.n)
        else:
            self.eng.wait_ge(self.sem, self.i * self.per + (self.base + self.n))

    def step(self, ins):
        self.done(ins)
        self.wait()


def decoder(nc, A, out):
    with ExitStack() as ctx:
        def sb(name, shape, dt=F32, where=ctx):
            return where.enter_context(nc.sbuf_tensor(name, shape, dt))

        def sem(name):
            return ctx.enter_context(nc.semaphore(name))

        PS = ctx.enter_context(nc.psum_tensor("PS", [P, 8, 512], F32))

        def bank(k, b=HB, t=T, rows=slice(0, P)):
            return PS[rows, k, 0:b * t].rearrange("p (b t) -> p b t", t=t)

        xT = sb("xT", [P, KC, B, TP])
        xn = sb("xn", [P, KC, B, TP])
        sq = sb("sq", [P, 2, KC, NT])
        std = sb("std", [P, NT])
        stds = (std[:], sq[:, 0, 0, :])
        avg = sb("avg", [P, P])
        ident = sb("ident", [P, P])
        epsc = sb("epsc", [P, 1])

        def half(t, c, hf):
            return t[:, c, HB * hf:HB * hf + HB, 0:T]

        def cols(t):
            return t.rearrange("p (b t) -> p b t", t=T)

        wzx = sb("wzx", [P, KC, 2 * DI])
        wbc = sb("wbc", [P, KC, 4, P])
        wdt = sb("wdt", [P, KC, NH])
        wmo = sb("wmo", [P, DI // P, C])
        sgn = sb("sgn", [P, 1])
        eye = sb("eye", [P, 2 * PAIRS * T])
        fcol = sb("fcol", [P, NP2])
        bias = sb("bias", [P, 4, NH // 2])
        dtb = sb("dtb", [NH, 1])
        alog = sb("alog", [NH, 1])
        dbc = sb("dbc", [P, NH])
        nw = sb("nw", [P, DI // P])
        keept = sb("keept", [NH, NT])
        cst = sb("cst", [P, 4])
        rqt = sb("rqt", [RQ, 4, T])
        p2 = ExitStack()
        w0 = sb("w0", [P, KC, 2 * C], where=p2)
        b0 = sb("b0", [P, 4], where=p2)
        gate_s = sb("gate_s", [P, KC, NT], where=p2)
        val_s = sb("val_s", [P, KC, NT], where=p2)
        hid = sb("hid", [P, KC, NT], where=p2)

        wxq = sb("wxq", [P, KC, XH * XDP], where=p2)
        wxk = sb("wxk", [64, XH * XDP], where=p2)
        wxv = sb("wxv", [64, C], where=p2)
        wxo = sb("wxo", [P, 4, C], where=p2)
        ctxs = sb("ctxs", [64, B, TP], where=p2)
        ctxp = sb("ctxp", [64, 2, 2, TP], where=p2)
        maskc = sb("maskc", [P, T], where=p2)
        qp = sb("qp", [P, 4, 2, TP], where=p2)
        kp = sb("kp", [P, 4, 2, TP], where=p2)
        vp = sb("vp", [P, 2, 2, XH, XDP], where=p2)
        sc = sb("sc", [P, XH, T], where=p2)
        pr = sb("pr", [P, XH, TP], where=p2)
        mxs = sb("mxs", [P, XH], where=p2)
        sms = sb("sms", [P, XH], where=p2)
        pt = sb("pt", [P, 8, P], where=p2)
        oT = sb("oT", [P, 4, B, TP], where=p2)

        wr = sb("wr", [P, KC, E], where=p2)
        wg = sb("wg", [P, KC, KB * P], where=p2)
        wu = sb("wu", [P, KC, KB * P], where=p2)
        wd = sb("wd", [P, C], where=p2)
        wsg = sb("wsg", [P, KC, C], where=p2)
        wsu = sb("wsu", [P, KC, C], where=p2)
        wsd = sb("wsd", [P, KC, C], where=p2)
        amps = sb("amps", [P, 2, KB], where=p2)
        escale = sb("escale", [P, 1], where=p2)
        mix = sb("mix", [P, KB], where=p2)
        mixb = sb("mixb", [P, KB, P], where=p2)
        msum = sb("msum", [P, 1], where=p2)
        keep = sb("keep", [P, PAIRS * E], where=p2)
        logit = sb("logit", [P, PAIRS, E], where=p2)
        top8 = sb("top8", [P, PAIRS, 8], where=p2)
        above = sb("above", [P, PAIRS, E], where=p2)
        level = sb("level", [P, PAIRS, E], where=p2)
        place = sb("place", [P, PAIRS, E], where=p2)
        expo = sb("expo", [P, PAIRS, E], where=p2)
        room = sb("room", [P, PAIRS], where=p2)
        zsum = sb("zsum", [P, PAIRS], where=p2)
        tsum = sb("tsum", [P, PAIRS], where=p2)
        coT = sb("coT", [P, B, TP], where=p2)
        sgl = sb("sgl", [P, 2, NT], where=p2)
        gu = sb("gu", [P, 2, NT], where=p2)
        wgu = sb("wgu", [P, NT], where=p2)
        acc = sb("acc", [P, 2, NT], where=p2)
        shr = sb("shr", [P, 2, 2, NT], where=p2)
        p2.close()
        p4 = ExitStack()
        dtc = sb("dtc", [NH, B, TP], where=p4)
        cum = sb("cum", [NH, B * T], where=p4)
        aT = sb("aT", [NH, B, T], where=p4)
        dtt = sb("dtt", [P, PAIRS, NH], where=p4)
        bcn = sb("bcn", [P, 4, BT], where=p4)
        siz = sb("siz", [P, PAIRS, DI], where=p4)
        dx = sb("dx", [P, PAIRS, DI], where=p4)
        ua = sb("ua", [P, PAIRS, DI], where=p4)
        ya = ua
        uh = sb("uh", [P, 2, PAIRS, 2, 2 * HD], where=p4)
        turn = sb("turn", [P, BT], where=p4)
        frac = sb("frac", [P, 2, BT], where=p4)
        sn = sb("sn", [P, 2, BT], where=p4)
        cs = sb("cs", [P, 2, BT], where=p4)
        rt = sb("rt", [P, 4, BT], where=p4)
        rb = sb("rb", [P, 2, BT + 8], where=p4)
        rc = sb("rc", [P, 2, B, 2, T], where=p4)
        ab = sb("ab", [P, 2, BT], where=p4)
        dec = sb("dec", [P, BT], where=p4)
        mt = sb("mt", [P, 2, 2 * PAIRS, TP], where=p4)
        yss = sb("yss", [P, PAIRS], where=p4)
        bsq, bst = ([frac[:, k, n * NT:(n + 1) * NT] for n in range(2)] for k in range(2))
        zx_banks = ((6, 7),) * 4 + ((0, 1), (3, 4)) * 2
        dts = cs[0:NH].rearrange("p s (k n) -> p (s k) n", k=2)
        gT = rt
        ysq = frac
        p4.close()
        p5 = ExitStack()
        rkc = sb("rkc", [KP, KT, DC], where=p5)
        rks = sb("rks", [KP, KT, DC], where=p5)
        lwq = sb("lwq", [P, 2, KC, P], where=p5)
        lwc = sb("lwc", [P, 2, 2 * RQ], where=p5)
        lwr = sb("lwr", [DC, 2, 2 * RQ], where=p5)
        lwk = sb("lwk", [DC, 2, DC], where=p5)
        lwv = sb("lwv", [P, 2, DC], where=p5)
        lwo = sb("lwo", [P, 2, C], where=p5)
        wab = sb("wab", [RQ, 2, 2, DC], where=p5)
        qa = sb("qa", [P, B, LH, T], F16, where=p5)
        kvx = sb("kvx", [KP, 2, KT, DC], where=p5)
        kvr = sb("kvr", [KP, 2, KT, 2 * DC], where=p5)
        kvt = sb("kvt", [KP, KT, DC], where=p5)
        kvp = sb("kvp", [KP, KT, DC], where=p5)
        khi = sb("khi", [P, 2, S], F16, where=p5)
        klo = sb("klo", [DC + 1, 2, S], F16, where=p5)
        qb1 = sb("qb1", [P, 2, LR], F16, where=p5)
        qb2 = sb("qb2", [DC + 1, 2, LR], F16, where=p5)
        qb3 = sb("qb3", [P, 2, LR], F16, where=p5)
        rmp = sb("rmp", [2 * T, 3 * LH // 2], where=p5)
        rmx = sb("rmx", [2 * T, LH // 2], where=p5)
        rmn = sb("rmn", [LH // 2, 2 * T], F16, where=p5)
        pe3 = sb("pe3", [KP, 6, NT], where=p5)
        psm = sb("psm", [KP, 2, 2, NT], where=p5)
        cx = sb("cx", [P, NT], where=p5)
        dsum = sb("dsum", [P, NT], where=p5)
        rden = sb("rden", [P, NT], where=p5)
        ones = sb("ones", [KP, 32], where=p5)
        pick = sb("pick", [P, P], where=p5)
        wvo = sb("wvo", [P, LH // 2, C], where=p5)
        cn = sb("cn", [P, LH // 2, B, T], where=p5)
        qbuf = cn[:].rearrange("p k b t -> p (k b t)").rearrange("p (n t) -> p n t", t=NT)
        qh = qbuf[:, 0:2, :]
        rp4 = qbuf[0:RQ, 2:10, :].rearrange("p (k n) t -> p k n t", k=2)
        rot = qbuf[0:RQ, 10:14, :].rearrange("p (k n) t -> p k n t", k=2)
        p5.close()
        p6 = ExitStack()
        xt = sb("xt", [P, PAIRS, C], where=p6)
        xq = sb("xq", [P, PAIRS, C], where=p6)
        xi = sb("xi", [P, PAIRS, C], BF16, where=p6)
        xiT = sb("xiT", [P, KC, PAIRS * P], BF16, where=p6)
        kw = sb("kw", [P, KC, C], where=p6)
        kwi = sb("kwi", [P, KC, C], BF16, where=p6)
        kwT = sb("kwT", [P, KC, C], BF16, where=p6)
        kdg = sb("kdg", [P, KC, P], where=p6)
        skb = sb("skb", [P, C], where=p6)
        bq = sb("bq", [P, C], where=p6)
        bqi = sb("bqi", [P, C], where=p6)
        one6 = sb("one6", [P, P], where=p6)
        identb = sb("identb", [P, P], BF16, where=p6)
        st6 = sb("st6", [P, PAIRS, 6], where=p6)
        mv6 = sb("mv6", [P, PAIRS, 2], where=p6)
        sx = sb("sx", [P, 4, PAIRS], where=p6)
        sk = sb("sk", [P, 4, KC], where=p6)
        sbq = sb("sbq", [P, 4], where=p6)
        sy = sb("sy", [P, 4, PAIRS], where=p6)
        y6 = sb("y6", [P, PAIRS, C], where=p6)
        p6.close()
        s_x = sem("x_loaded")
        s_w1 = sem("w1_loaded")
        s_w2 = sem("w2_loaded")
        s_const = sem("const_ready")
        s_xr = sem("x_ready")
        s_mean = sem("ln_mean")
        s_cen = sem("ln_centred")
        s_sq = sem("ln_squared")
        s_var = sem("ln_var")
        s_std = sem("ln_std")
        s_xn = sem("ln_out")
        own_v = sem("vector_own")
        own_a = sem("scalar_own")
        own_g = sem("gpsimd_own")
        s_par = sem("l0_params")
        s_pact = sem("l0_activated")
        x_cp = sem("xa_ctx_copied")
        x_qm, x_km, x_vm = sem("xa_q_mm"), sem("xa_k_mm"), sem("xa_v_mm")
        x_qc, x_kc, x_vc = sem("xa_q_copied"), sem("xa_k_copied"), sem("xa_v_copied")
        x_sm, x_sh, x_ex, x_pr = sem("xa_scores"), sem("xa_shifted"), sem("xa_exp"), sem("xa_probs")
        x_sr = sem("xa_scores_read")
        x_tm, x_tc = sem("xa_pt_mm"), sem("xa_pt_copied")
        x_om, x_oc, x_wm = sem("xa_o_mm"), sem("xa_o_copied"), sem("xa_out_mm")
        s_gate = sem("tensor_gate")
        s_out = sem("stored")
        s_w3 = sem("w3_loaded")
        s_keep = sem("moe_keep")
        e_mix = sem("moe_mix")
        e_lm, e_lc, e_sh, e_ex, e_co = sem("moe_logits"), sem("moe_logits_copied"), sem("moe_shifted"), sem("moe_exp"), sem("moe_coeff")
        e_tm, e_tc = sem("moe_coT_mm"), sem("moe_coT")
        e_sg, e_ss, e_sp = sem("moe_shared_mm"), sem("moe_shared_silu"), sem("moe_shared_product")
        e_gm, e_um, e_si, e_pd = sem("moe_gate_mm"), sem("moe_up_mm"), sem("moe_silu"), sem("moe_product")
        e_ac, e_dm = sem("moe_acc"), sem("moe_down_mm")
        a_scr = nc.dram_tensor("decay_scratch", (NH // 2, 2, PAIRS, 2, T), F32, kind="Internal").ap()
        t_scr = nc.dram_tensor("time_scratch", (NH, BT), F32, kind="Internal").ap()
        s_w4 = sem("w4_loaded")
        s_c4 = sem("ssm_const")
        d_mm, d_ln, d_dt, d_cum = (sem("ssm_" + n) for n in ("dt_mm", "dt_ln", "dt", "cum"))
        d_ng, d_ex, d_a, d_st = (sem("ssm_" + n) for n in ("neg_a", "decay_exp", "decay", "decay_stored"))
        d_tm, d_tc = sem("ssm_dtt_mm"), sem("ssm_dtt")
        b_mm, b_sq, b_ms, b_sd, b_n = (sem("ssm_bc_" + n) for n in ("mm", "squared", "mean", "std", "normed"))
        z_mm, z_si, z_u = sem("ssm_zx_mm"), sem("ssm_silu"), sem("ssm_u")
        m_u, m_tu, m_fr, m_sin = (sem("ssm_" + n) for n in ("uh", "turns", "frac", "sin"))
        d_ts = sem("ssm_time_stored")
        m_tb, m_tc, m_rb, m_rc, m_sc = (sem("ssm_" + n) for n in ("tb", "tc", "rotB", "rotC", "scan"))
        m_abc = [sem(f"ssm_a_bcast_{n}") for n in range(2)]
        m_tbc = [sem(f"ssm_time_bcast_{n}") for n in range(2)]
        m_g, m_mt, m_y, m_yc = (sem("ssm_" + n) for n in ("g", "mt", "y", "y_copied"))
        g_g, g_sq, g_sd, g_n, g_tm, g_tc, g_wm = (sem("ssm_out_" + n) for n in ("gated", "squared", "std", "normed", "t_mm", "t", "mm"))
        s_w5, s_c5 = sem("w5_loaded"), sem("latent_const")
        k_ld = [sem(f"lq_weights_{n}") for n in range(2)]
        k_w, k_wc, k_q, k_qc, k_b, k_p, k_r, k_a, k_hi, k_lo = (sem("lq_" + n) for n in (
            "w_mm", "w_copied", "proj", "proj_copied", "big", "products", "rotated", "abs_mm", "high", "low"))
        c_ld = [sem(f"kv_loaded_{n}") for n in range(2)]
        c_row = [sem(f"max_row_{n}") for n in range(2)]
        c_rp, c_tm, c_khi, c_klo, c_qb, c_mm, c_mr, c_mx, c_mt, c_mn = (sem("la_" + n) for n in (
            "roped", "kT_mm", "k_high", "k_low", "q_slot", "max_mm", "part_max", "max", "max_t", "max_neg"))
        c_sm, c_ex, c_pv, c_pa, c_dn, c_cx, c_ds, c_bc, c_cn, c_om, c_xu = (sem("la_" + n) for n in (
            "scores", "exp", "pv", "added", "sums", "ctx_copied", "sums_copied", "sums_bcast", "ctx_normed", "out_mm", "x_updated"))
        s_w6, s_c6 = sem("w6_loaded"), sem("ffn_const")
        f_xm, f_xc, f_va, f_sd, f_xi = (sem("ffn_" + n) for n in ("x_mm", "x_copied", "variance", "std", "x_int"))
        f_tm, f_tc, f_ki, f_km, f_kc, f_ym = (sem("ffn_" + n) for n in ("xT_mm", "xT", "k_int", "k_mm", "k_ready", "y_mm"))
        f_yr = sem("ffn_y_read")
        f_o = sem("ffn_out")
        block = ctx.enter_context(nc.Block())

        @block.sync
        def _(sp):
            sp.dma_start(xT[:], A["xT"].rearrange("(c p) b t -> p c b t", p=P)).then_inc(s_x, 16)
            sp.dma_start(w0[:], A["W0"].rearrange("(c p) n -> p c n", p=P)).then_inc(s_w1, 16)
            sp.dma_start(b0[:], A["b0"]).then_inc(s_w1, 16)
            sp.dma_start(wxq[:], A["Wxq"].rearrange("(c p) n -> p c n", p=P)).then_inc(s_w2, 16)
            sp.dma_start(wxk[:], A["Wxk"]).then_inc(s_w2, 16)
            sp.dma_start(wxv[:], A["Wxv"]).then_inc(s_w2, 16)
            sp.dma_start(wxo[:], A["Wxo"].rearrange("(c p) n -> p c n", p=P)).then_inc(s_w2, 16)
            sp.dma_start(ctxs[:], A["ctx56"]).then_inc(s_w2, 16)
            sp.dma_start(maskc[:], A["causal"]).then_inc(s_w2, 16)
            sp.dma_start(wr[:], A["Wr"].rearrange("(c p) n -> p c n", p=P)).then_inc(s_w3, 16)
            sp.dma_start(wg[:], A["Wg"].rearrange("(c p) n -> p c n", p=P)).then_inc(s_w3, 16)
            sp.dma_start(wu[:], A["Wu"].rearrange("(c p) n -> p c n", p=P)).then_inc(s_w3, 16)
            sp.dma_start(wd[:], A["Wd"]).then_inc(s_w3, 16)
            sp.dma_start(wsg[:], A["Wsg"].rearrange("(c p) n -> p c n", p=P)).then_inc(s_w3, 16)
            sp.dma_start(wsu[:], A["Wsu"].rearrange("(c p) n -> p c n", p=P)).then_inc(s_w3, 16)
            sp.dma_start(wsd[:], A["Wsd"].rearrange("(c p) n -> p c n", p=P)).then_inc(s_w3, 16)
            sp.dma_start(amps[:], A["amps"]).then_inc(s_w3, 16)
            sp.dma_start(escale[:], A["escale"]).then_inc(s_w3, 16)
            for t, src in ((wzx, A["Wzx"].rearrange("(c p) n -> p c n", p=P)), (wbc, A["Wbc"].rearrange("(c p) k n -> p c k n", p=P)),
                           (wdt, A["Wdt"].rearrange("(c p) n -> p c n", p=P)),
                           (wmo, A["Wmo"].rearrange("(c p) n -> p c n", p=P)), (eye, A["eye"]),
                           (fcol, A["fcol"]), (sgn, A["sgn"]), (bias, A["bcbias"]), (dtb, A["dtb"]), (alog, A["alog"]),
                           (dbc, A["Dp"].broadcast_to((P, NH))), (nw, A["nw"])):
                sp.dma_start(t[:], src).then_inc(s_w4, 16)
            sp.wait_ge(d_cum, 2)
            sp.dma_start(t_scr[:], cum[:]).then_inc(d_ts, 16)
            sp.wait_ge(d_a, 2)
            for h2 in range(2):
                for b2 in range(2):
                    sp.dma_start(a_scr[:, b2, :, h2, :], aT[h2::2, b2::2, :]).then_inc(d_st, 16)
            sp.wait_ge(d_st, 64)
            sp.wait_ge(d_ts, 16)

            def ssm_load(hp, slot):
                for b2 in range(2):
                    src = a_scr[hp, b2] if isinstance(hp, int) else a_scr[bass.ds(hp, 1), b2]
                    src = src.rearrange("i h t -> (i h t)") if isinstance(hp, int) else src.rearrange("o i h t -> o (i h t)")
                    if isinstance(hp, int):
                        src = src.unsqueeze(0)
                    sp.dma_start(ab[64 * b2:64 * b2 + 64, slot, :], src.broadcast_to((64, BT))).then_inc(m_abc[slot], 16)

            def ssm_load_time(hp, slot):
                if not isinstance(hp, int) or hp >= 2:
                    sp.wait_ge(m_sin, hp - 1)
                for h2 in range(2):
                    h = 2 * hp + h2
                    src = t_scr[h:h + 1] if isinstance(hp, int) else t_scr[bass.ds(h, 1)]
                    sp.dma_start(frac[64 * h2:64 * h2 + 64, slot, :], src.broadcast_to((64, BT))).then_inc(m_tbc[slot], 16)

            sp.wait_ge(b_n, 4)
            ssm_load_time(0, 0)
            ssm_load_time(1, 1)
            ssm_load(0, 0)
            ssm_load(1, 1)
            for hp in (2, 3, 4):
                ssm_load_time(hp, hp % 2)
            with sp.Fori(0, SSM_TRIPS) as j:
                for d in range(2):
                    ssm_load_time(2 * j + (5 + d), 1 - d)
                    sp.wait_ge(m_sc, 2 * j + (1 + d))
                    ssm_load(2 * j + (2 + d), d)
            ssm_load_time(NP2 - 1, 1)
            for hp in range(NP2 - 4, NP2):
                sp.wait_ge(m_sc, hp - 1)
                ssm_load(hp, hp % 2)
            sp.dma_start(rqt[:], A["rqt"]).then_inc(s_w5, 16)
            sp.wait_ge(s_xr, 10)
            sp.dma_start(rkc[:], A["rkc"]).then_inc(s_w5, 16)
            sp.dma_start(rks[:], A["rks"]).then_inc(s_w5, 16)

            def latent_weights(h, slot):
                hs = slice(h, h + 1) if isinstance(h, int) else bass.ds(h, 1)
                for t, a in ((lwq[:, slot, :, :], A["Lwq"][hs].rearrange("o p c n -> p (o c) n")),
                             (lwc[:, slot, :], A["Lwc"][hs].rearrange("o p n -> p (o n)")),
                             (lwr[:, slot, :], A["Lwr"][hs].rearrange("o p n -> p (o n)")),
                             (lwk[:, slot, :], A["Lwk"][hs].rearrange("o p n -> p (o n)")),
                             (lwv[:, slot, :], A["Lwv"][hs].rearrange("o p n -> p (o n)")),
                             (lwo[:, slot, :], A["Lwo"][hs].rearrange("o p n -> p (o n)"))):
                    sp.dma_start(t, a).then_inc(k_ld[slot], 16)

            def latent_context(b, slot):
                bs = slice(b, b + 1) if isinstance(b, int) else bass.ds(b, 1)
                sp.dma_start(kvx[:, slot, :, :].rearrange("p j d -> p (j d)"),
                             A["ctx"][bs].rearrange("o (p j) d -> (o p) (j d)", j=KT)).then_inc(c_ld[slot], 16)

            latent_weights(0, 0)
            latent_weights(1, 1)
            latent_context(0, 0)
            latent_context(1, 1)
            with sp.Fori(0, LH // 2 - 1) as j:
                for d in range(2):
                    sp.wait_ge(k_b, 4 * j + (2 + 2 * d))
                    latent_weights(2 * j + (2 + d), d)
            with sp.Fori(0, B // 2 - 1) as j:
                for d in range(2):
                    sp.wait_ge(c_rp, 2 * j + (1 + d))
                    latent_context(2 * j + (2 + d), d)
            sp.wait_ge(c_cn, B + 1)
            sp.dma_start(kw[:], A["kT"].rearrange("(c p) d -> p c d", p=P)).then_inc(s_w6, 16)
            sp.dma_start(bq[:], A["fb"].broadcast_to((P, C))).then_inc(s_w6, 16)
            for i in range(PAIRS):
                sp.wait_ge(f_o, i + 1)
                for b2 in range(2):
                    sp.dma_start(out[2 * i + b2], y6[64 * b2:64 * b2 + T, i, :]).then_inc(s_out, 16)
            sp.wait_ge(s_out, 16 * B)

        def ln_pe(pe, k):
            for hf in range(2):
                pe.wait_ge(s_xr, 2 * k + hf + 1)
                for c in range(KC):
                    mm = pe.matmul(bank(hf), avg[:], half(xT, c, hf), start=c == 0, stop=c == KC - 1)
                mm.then_inc(s_mean, 1)
            for hf in range(2):
                pe.wait_ge(s_sq, 2 * k + hf + 1)
                for c in range(KC):
                    mm = pe.matmul(bank(2 + hf), avg[:], cols(sq[:, hf, c, :]), start=c == 0, stop=c == KC - 1)
                mm.then_inc(s_var, 1)

        def both(t, hf):
            return t[:, :, HB * hf:HB * hf + HB, 0:T]

        def ln_act(act, k):
            for hf in range(2):
                act.wait_ge(s_cen, 2 * k + hf + 1)
                act.activation(sq[:, hf, :, :].rearrange("p c (b t) -> p c b t", t=T), both(xn, hf), ACT.Square).then_inc(s_sq, 1)
            for hf in range(2):
                act.wait_ge(s_var, 2 * k + hf + 1)
                act.activation(stds[hf], PS[:, 2 + hf, 0:NT], ACT.Sqrt, bias=epsc[:]).then_inc(s_std, 1)

        def ln_dve(v, own, k):
            for hf in range(2):
                v.wait_ge(s_mean, 2 * k + hf + 1)
                v.tensor_tensor(both(xn, hf), both(xT, hf), bank(hf).unsqueeze(1).broadcast_to((P, KC, HB, T)),
                                ALU.subtract).then_inc(s_cen, 1)
            for hf in range(2):
                v.wait_ge(s_cen, 2 * k + hf + 1)
                v.wait_ge(s_std, 2 * k + hf + 1)
                own.step(v.reciprocal(stds[hf], stds[hf]))
                v.tensor_tensor(both(xn, hf), both(xn, hf), cols(stds[hf]).unsqueeze(1).broadcast_to((P, KC, HB, T)),
                                ALU.mult).then_inc(s_xn, 1)
            v.wait_ge(s_xn, 2 * k + 2)

        @block.gpsimd
        def _(g):
            own = Own(g, own_g)
            g.memset(avg[:], 1.0 / C).then_inc(s_const, 1)
            g.memset(epsc[:], LN_EPS).then_inc(s_const, 1)
            g.memset(xn[:], 0.0).then_inc(s_const, 1)
            own.step(g.memset(ident[:], 0.0))
            g.affine_select(out=ident[:], in_=ident[:], compare_op=ALU.not_equal, fill=1.0, base=0,
                            pattern=[[-1, P]], channel_multiplier=1).then_inc(s_const, 1)
            g.memset(vp[:], 0.0).then_inc(s_const, 1)
            g.memset(pr[:], 0.0).then_inc(s_const, 1)
            g.wait_ge(s_w2, 16 * 6)
            for b in range(2):
                ins = g.tensor_copy(ctxp[:, :, b, :], ctxs[:, 0:2, :])
            ins.then_inc(x_cp, 1)
            with g.Fori(0, PAIRS - 1) as i:
                g.wait_ge(x_vm, i + 1)
                for b in range(2):
                    ins = g.tensor_copy(ctxp[:, :, b, :], ctxs[:, bass.ds(2 * i + 2, 2), :])
                ins.then_inc(x_cp, 1)
            own.step(g.memset(keep[:], 1.0))
            g.memset(keep[:].rearrange("p (i e) -> p i e", e=E)[:, :, 0:1], 0.0).then_inc(s_keep, 1)
            own.step(g.memset(keept[:], 1.0))
            g.memset(cols(keept[:])[:, :, 0:1], 0.0).then_inc(s_c4, 1)
            for n, c in enumerate((0.5, 1e-6, HALF_PI, 0.0)):
                g.memset(cst[:, n:n + 1], c).then_inc(s_c4, 1)
            g.wait_ge(s_xr, 8)
            g.memset(dtc[:], 0.0).then_inc(s_c4, 1)
            g.memset(rb[:], 0.0).then_inc(s_c4, 1)
            g.memset(rc[:], 0.0).then_inc(s_c4, 1)
            g.memset(mt[:], 0.0).then_inc(s_c4, 1)
            g.memset(uh[:], 0.0).then_inc(s_c4, 1)
            g.wait_ge(s_c4, 10)
            g.wait_ge(s_w4, 16 * 12)
            g.tensor_scalar(fcol[:], fcol[:], sgn[:], None, ALU.mult).then_inc(s_c4, 1)

            def ssm_rotate(hp, slot):
                g.wait_ge(m_tb, hp + 1)
                if not isinstance(hp, int) or hp >= 2:
                    g.wait_ge(m_g, hp - 1)
                g.tensor_tensor(rb[:, slot, 0:BT], rt[:, 0, :], rt[:, 1, :], ALU.add).then_inc(m_rb, 1)
                g.wait_ge(m_tc, hp + 1)
                for h2 in range(2):
                    rows = slice(64 * h2, 64 * h2 + 64)
                    g.tensor_tensor(rc[rows, slot, :, h2, :], rt[rows, 2, :].rearrange("p (b t) -> p b t", t=T),
                                    rt[rows, 3, :].rearrange("p (b t) -> p b t", t=T), ALU.add).then_inc(m_rc, 1)
                    g.wait_ge(m_rc, 2 * hp + (1 + h2))

            def ssm_inputs(hp, slot):
                if isinstance(hp, int) and hp == 0:
                    g.wait_ge(z_u, PAIRS)
                if not isinstance(hp, int) or hp >= 2:
                    g.wait_ge(m_y, hp - 1)
                at = slice(hp * 2 * HD, (hp + 1) * 2 * HD) if isinstance(hp, int) else bass.ds(hp * (2 * HD), 2 * HD)
                for b2 in range(2):
                    rows = slice(64 * b2, 64 * b2 + 64)
                    g.tensor_copy(uh[rows, slot, :, b2, :], ua[rows, :, at]).then_inc(m_u, 1)
                    g.wait_ge(m_u, 2 * hp + (1 + b2))

            def ssm_pool(k, p):
                if not isinstance(k, int) or 0 <= k + 1 < NP2:
                    ssm_rotate(k + 1, 1 - p)
                if not isinstance(k, int) or 0 <= k < NP2:
                    ssm_inputs(k, p)

            for k in range(-1, 2):
                ssm_pool(k, k % 2)
            with g.Fori(0, SSM_TRIPS) as j:
                for d in range(2):
                    ssm_pool(2 * j + (2 + d), d)
            for k in range(NP2 - 4, NP2):
                ssm_pool(k, k % 2)
            g.wait_ge(s_xr, 10)
            g.memset(pick[:], 0.0).then_inc(s_c5, 1)
            for q in range(4):
                g.wait_ge(s_c5, 1 + q)
                g.memset(pick[32 * q:32 * q + 32, 64 * (q % 2):64 * (q % 2) + 64], 1.0 / 32).then_inc(s_c5, 1)
            g.wait_ge(s_c5, 5)
            g.memset(ones[:], 1.0).then_inc(s_c5, 1)
            g.wait_ge(s_c5, 6)
            g.memset(klo[DC:DC + 1, :, :], 1.0).then_inc(s_c5, 1)
            g.wait_ge(s_c5, 7)
            g.wait_ge(s_w5, 48)

            def rope_products(b, slot, nth):
                g.wait_ge(c_ld[slot], 16 * nth)
                kx = kvx[:, slot, :, :]
                own.done(g.tensor_tensor(kvt[:, :, 0:DC // 2], kx[:, :, DC // 2:DC], rks[:, :, 0:DC // 2], ALU.mult))
                own.done(g.tensor_tensor(kvt[:, :, DC // 2:DC], kx[:, :, 0:DC // 2], rks[:, :, DC // 2:DC], ALU.mult))
                own.step(g.tensor_tensor(kvp[:], kx, rkc[:], ALU.mult))

            def rope_context(b, slot):
                if not isinstance(b, int) or b >= 2:
                    g.wait_ge(c_pv, KT * b - KT)
                own.done(g.tensor_tensor(kvr[:, slot, :, 0:DC], kvp[:], kvt[:], ALU.add))
                own.step(g.tensor_tensor(kvr[:, slot, :, DC:2 * DC], kvp[:], kvt[:], ALU.add))
                g.sem_inc(c_rp, 1)

            def add_probs(b, k):
                if not isinstance(b, int) or b >= 1 or k >= 2:
                    g.wait_ge(c_dn, 2 * b + k // 2)
                tiles = [pe3[:, 2 * j:2 * j + 2, :] for j in range(3)]
                g.wait_ge(c_ex, LS * b + (6 * k + 7))
                g.tensor_tensor(psm[:, k % 2, :, :], tiles[0], tiles[1], ALU.add).then_inc(c_pa, 1)
                g.wait_ge(c_pa, 8 * b + (2 * k + 1))
                g.wait_ge(c_ex, LS * b + (6 * k + 9))
                g.tensor_tensor(psm[:, k % 2, :, :], psm[:, k % 2, :, :], tiles[2], ALU.add).then_inc(c_pa, 1)

            def latent_pool(b, slot, rope, products, nth):
                if rope is not None:
                    rope_context(rope, 1 - slot)
                for k in range(4):
                    add_probs(b, k)
                    if k == 1 and products is not None:
                        rope_products(products, slot, nth)

            def rotate_queries(h, hf):
                g.wait_ge(k_p, 2 * h + (hf + 1))
                if not isinstance(h, int) or h >= 1:
                    g.wait_ge(k_a, 2 * h + (hf - 1))
                for r in range(2):
                    ins = g.tensor_tensor(rot[:, hf, r, :], rp4[:, hf, 2 * r, :], rp4[:, hf, 2 * r + 1, :], ALU.add)
                ins.then_inc(k_r, 1)

            rope_products(0, 0, 1)
            rope_context(0, 0)
            rope_products(1, 1, 1)
            for hf in range(2):
                rotate_queries(0, hf)
            with g.Fori(1, LH) as h:
                for hf in range(2):
                    rotate_queries(h, hf)
            latent_pool(0, 0, 1, 2, 2)
            with g.Fori(0, B // 2 - 2) as j:
                own.enter(j, 10)
                for d in range(2):
                    b = 2 * j + (1 + d)
                    latent_pool(b, 1 - d, 2 * j + (2 + d), 2 * j + (3 + d), j + (2 + d))
            own.leave(B // 2 - 2)
            latent_pool(B - 3, 1, B - 2, B - 1, B // 2)
            latent_pool(B - 2, 0, B - 1, None, None)
            latent_pool(B - 1, 1, None, None, None)
            g.wait_ge(c_cn, B + 1)
            g.memset(one6[:], 1.0).then_inc(s_c6, 1)
            g.tensor_copy(identb[:], ident[:]).then_inc(s_c6, 1)

        @block.tensor
        def _(pe):
            pe.wait_ge(s_const, 6)
            ln_pe(pe, 0)
            pe.wait_ge(s_w1, 32)
            for hf in range(2):
                pe.wait_ge(s_xn, hf + 1)
                for m in range(4):
                    if hf == 1:
                        pe.wait_ge(s_pact, m + 1)
                    for c in range(KC):
                        mm = pe.matmul(bank(4 + m), w0[:, c, m * P:(m + 1) * P], half(xn, c, hf),
                                       start=c == 0, stop=c == KC - 1)
                    mm.then_inc(s_par, 1)
            ln_pe(pe, 1)
            pe.wait_ge(s_w2, 16 * 6)
            pe.wait_ge(s_xn, 3)

            def cross_project(i):
                pair = slice(2 * i, 2 * i + 2) if isinstance(i, int) else bass.ds(2 * i, 2)
                for m in range(4):
                    for c in range(KC):
                        mm = pe.matmul(PS[:, 0, m * P:(m + 1) * P], wxq[:, c, m * P:(m + 1) * P],
                                       xn[:, c, pair, :], start=c == 0, stop=c == KC - 1)
                mm.then_inc(x_qm, 1)
                for m in range(4):
                    mm = pe.matmul(PS[:, 1, m * P:(m + 1) * P], wxk[:, m * P:(m + 1) * P],
                                   ctxs[:, pair, :], start=True, stop=True)
                mm.then_inc(x_km, 1)
                pe.wait_ge(x_cp, i + 1)
                if not isinstance(i, int) or i >= 1:
                    pe.wait_ge(x_vc, i)
                if not isinstance(i, int) or i >= 2:
                    pe.wait_ge(x_oc, i - 1)
                for b in range(2):
                    mm = pe.matmul(PS[:, 2, b * C:(b + 1) * C], ctxp[:, b, :, :], wxv[:],
                                   start=True, stop=True)
                mm.then_inc(x_vm, 1)

            def cross_scores(i):
                pe.wait_ge(x_qc, i + 1)
                pe.wait_ge(x_kc, i + 1)
                if not isinstance(i, int) or i >= 1:
                    pe.wait_ge(x_sr, i)
                for c in range(4):
                    for r in range(4):
                        rows = slice(32 * r, 32 * r + 32)
                        for b in range(2):
                            mm = pe.matmul(PS[64 * b:64 * b + 64, 4 + r, TP * c:TP * c + T],
                                           qp[rows, c, b, :], kp[rows, c, b, 0:T], start=True, stop=True)
                mm.then_inc(x_sm, 1)

            def cross_values(i, slot, ahead):
                pe.wait_ge(x_pr, i + 1)
                for m in range(8):
                    mm = pe.transpose(PS[:, m // 4, (m % 4) * P:(m % 4) * P + P],
                                      pr[:, 2 * m:2 * m + 2, :], ident[:])
                mm.then_inc(x_tm, 1)
                pe.wait_ge(x_vc, ahead)
                pe.wait_ge(x_tc, i + 1)
                pe.sem_inc(s_gate, 1)
                for m in range(8):
                    for e in range(2):
                        r, c = m // 2, 2 * (m % 2) + e
                        for b in range(2):
                            rows = slice(64 * e, 64 * e + T)
                            at = (c // 2 * 2 + b) * T
                            mm = pe.matmul(PS[32 * r:32 * r + 32, 2 + e, at:at + T], vp[rows, slot, b, 4 * c + r, :],
                                           pt[rows, m, 64 * b:64 * b + T], start=True, stop=True)
                mm.then_inc(x_om, 1)

            for i in range(2):
                cross_project(i)
                cross_scores(i)
            pe.wait_ge(s_xn, 4)
            with pe.Fori(0, PAIRS // 2 - 1) as j:
                for d in range(2):
                    cross_values(2 * j + d, d, 2 * j + (2 + d))
                    cross_project(2 * j + (2 + d))
                    cross_scores(2 * j + (2 + d))
            cross_values(PAIRS - 2, 0, PAIRS)
            pe.wait_ge(x_oc, PAIRS - 1)
            cross_values(PAIRS - 1, 1, PAIRS)
            for hf in range(2):
                pe.wait_ge(x_oc, PAIRS)
                for m in range(KC):
                    for c in range(4):
                        mm = pe.matmul(bank(4 + 2 * hf + m), wxo[:, c, m * P:(m + 1) * P], half(oT, c, hf),
                                       start=c == 0, stop=c == 3)
                    mm.then_inc(x_wm, 1)
            ln_pe(pe, 2)
            pe.wait_ge(s_w3, 16 * 9)
            for i in range(PAIRS):
                if i % 4 == 0:
                    pe.wait_ge(s_xn, 5 + i // 4)
                for c in range(KC):
                    mm = pe.matmul(PS[:, 4 + i // 4, (i % 4) * E:(i % 4) * E + E],
                                   xn[:, c, 2 * i:2 * i + 2, :], wr[:, c, :], start=c == 0, stop=c == KC - 1)
            mm.then_inc(e_lm, 1)
            for n in range(4):
                hf, j = n // 2, n % 2
                if n >= 2:
                    pe.wait_ge(e_sp, n - 1)
                for k, w in enumerate((wsg, wsu)):
                    for c in range(KC):
                        mm = pe.matmul(bank(2 * j + k), w[:, c, j * P:(j + 1) * P], half(xn, c, hf),
                                       start=c == 0, stop=c == KC - 1)
                mm.then_inc(e_sg, 1)
            pe.wait_ge(e_sp, 4)

            def moe_hidden(n):
                hf, k, gb = n // KB, n % KB, 3 * (n % 2)
                if n >= 2:
                    pe.wait_ge(e_pd, n - 1)
                for c in range(KC):
                    mm = pe.matmul(bank(gb), wg[:, c, k * P:(k + 1) * P], half(xn, c, hf),
                                   start=c == 0, stop=c == KC - 1)
                mm.then_inc(e_gm, 1)
                for c in range(KC):
                    pe.matmul(bank(gb + 1), wu[:, c, k * P:(k + 1) * P], half(xn, c, hf),
                              start=c == 0, stop=c == KC - 1)

            def moe_weight(n):
                hf, k = n // KB, n % KB
                pe.matmul(bank(3 * (n % 2) + 2), mixb[:, k, :], coT[:, HB * hf:HB * hf + HB, 0:T],
                          start=True, stop=True).then_inc(e_um, 1)

            moe_hidden(0)
            moe_hidden(1)
            pe.wait_ge(e_co, 1)
            for i in range(PAIRS):
                mm = pe.transpose(PS[:, 6 + i // 4, (i % 4) * P:(i % 4) * P + P], expo[:, i, :], ident[:])
            mm.then_inc(e_tm, 1)
            pe.wait_ge(e_tc, 1)
            pe.wait_ge(e_mix, 1)
            moe_weight(0)
            moe_weight(1)
            for n in range(2, 2 * KB):
                moe_hidden(n)
                moe_weight(n)
            for hf in range(2):
                pe.wait_ge(e_ac, hf + 1)
                if hf == 1:
                    pe.wait_ge(s_xr, 7)
                for m in range(KC):
                    pe.matmul(bank(6 + m), wd[:, m * P:(m + 1) * P], cols(acc[:, hf, :]), start=True, stop=False)
                    for c in range(KC):
                        mm = pe.matmul(bank(6 + m), wsd[:, c, m * P:(m + 1) * P], cols(shr[:, hf, c, :]),
                                       start=False, stop=c == KC - 1)
                    mm.then_inc(e_dm, 1)
            ln_pe(pe, 3)
            pe.wait_ge(s_w4, 16 * 12)
            def ssm_dt(hf):
                pe.wait_ge(s_xn, 7 + hf)
                for c in range(KC):
                    mm = pe.matmul(bank(6 + hf, rows=slice(0, NH)), wdt[:, c, :], half(xn, c, hf),
                                   start=c == 0, stop=c == KC - 1)
                mm.then_inc(d_mm, 1)

            def ssm_bc(n):
                hf, x, bb = n // 2, n % 2, 3 * (n % 2)
                if n >= 2:
                    pe.wait_ge(b_n, n - 1)
                for s in range(2):
                    for c in range(KC):
                        mm = pe.matmul(bank(bb + s), wbc[:, c, 2 * x + s, :], half(xn, c, hf),
                                       start=c == 0, stop=c == KC - 1)
                mm.then_inc(b_mm, 1)

            def ssm_mean(n):
                pe.wait_ge(b_sq, n + 1)
                pe.matmul(bank(3 * (n % 2) + 2), avg[:], cols(bsq[n % 2]), start=True, stop=True).then_inc(b_ms, 1)

            def ssm_zx(i):
                before = {4: 4, 5: 4, 6: 5, 7: 6}.get(i, i)
                if before:
                    pe.wait_ge(z_si, before)
                    pe.wait_ge(z_u, before)
                for s in range(2):
                    for c in range(KC):
                        mm = pe.matmul(PS[:, zx_banks[i][s], :], xn[:, c, 2 * i:2 * i + 2, :], wzx[:, c, s * DI:(s + 1) * DI],
                                       start=c == 0, stop=c == KC - 1)
                mm.then_inc(z_mm, 1)

            ssm_dt(0)
            ssm_bc(0)
            ssm_dt(1)
            ssm_bc(1)
            pe.wait_ge(s_c4, 10)
            pe.wait_ge(d_dt, 2)
            for i in range(PAIRS):
                mm = pe.transpose(PS[:, 6, i * NH:(i + 1) * NH], dtc[:, 2 * i:2 * i + 2, :], ident[0:NH, 0:NH])
            mm.then_inc(d_tm, 1)
            ssm_mean(0)
            ssm_mean(1)
            pe.wait_ge(d_tc, 1)
            ssm_zx(0)
            ssm_bc(2)
            ssm_zx(1)
            ssm_bc(3)
            ssm_mean(2)
            ssm_zx(2)
            ssm_mean(3)
            ssm_zx(3)
            pe.wait_ge(b_n, 4)
            for i in range(4, PAIRS):
                ssm_zx(i)
            pe.wait_ge(z_u, PAIRS)
            pe.wait_ge(z_si, PAIRS)

            def ssm_mix(hp, slot):
                if not isinstance(hp, int) or hp >= 1:
                    pe.wait_ge(m_mt, hp)
                pe.wait_ge(m_rb, hp + 1)
                pe.wait_ge(m_rc, 2 * hp + 2)
                for b in range(B):
                    i, half_pairs = b // 2, PAIRS // 2
                    mm = pe.matmul(PS[64 * (b % 2):64 * (b % 2) + 64, 2 + i // half_pairs,
                                      i % half_pairs * 2 * T:(i % half_pairs + 1) * 2 * T],
                                   rb[:, slot, b * T:b * T + TP], rc[:, slot, b, :, :].rearrange("p h t -> p (h t)"),
                                   start=True, stop=True)
                mm.then_inc(m_g, 1)

            def ssm_y(hp, slot):
                if not isinstance(hp, int) or hp >= 2:
                    pe.wait_ge(m_yc, hp - 1)
                pe.wait_ge(m_u, 2 * hp + 2)
                pe.wait_ge(m_mt, hp + 1)
                for i in range(PAIRS):
                    mm = pe.matmul(PS[:, 4 + slot, i * 4 * HD:(i + 1) * 4 * HD],
                                   mt[:, slot, 2 * i:2 * i + 2, :].rearrange("p h t -> p (h t)"),
                                   uh[:, slot, i, :, :].rearrange("p b n -> p (b n)"), start=True, stop=True)
                mm.then_inc(m_y, 1)

            def ssm_tensor(k, p):
                if not isinstance(k, int) or 0 <= k < NP2:
                    ssm_mix(k, p)
                if not isinstance(k, int) or 1 <= k:
                    ssm_y(k - 1, 1 - p)

            for k in range(-3, 2):
                ssm_tensor(k, k % 2)
            with pe.Fori(0, SSM_TRIPS) as j:
                for d in range(2):
                    ssm_tensor(2 * j + (2 + d), d)
            for k in range(NP2 - 4, NP2 + 1):
                ssm_tensor(k, k % 2)
            def ssm_turn(hf):
                for i in range(4 * hf, 4 * hf + 4):
                    pe.wait_ge(g_n, i + 1)
                    if i >= 4:
                        pe.wait_ge(g_tc, i - 3)
                    for c in range(DI // P):
                        mm = pe.transpose(PS[:, i % 4, c * P:(c + 1) * P], ya[:, i, c * P:(c + 1) * P], ident[:])
                    mm.then_inc(g_tm, 1)

            def ssm_out(hf, m):
                pe.wait_ge(g_tc, 4 * hf + 4)
                for c in range(DI // P):
                    mm = pe.matmul(PS[:, 4 + 2 * hf + m, 0:NT], wmo[:, c, m * P:(m + 1) * P],
                                   gT[:, c, hf * NT:(hf + 1) * NT], start=c == 0, stop=c == DI // P - 1)
                mm.then_inc(g_wm, 1)

            ssm_turn(0)
            ssm_out(0, 0)
            ssm_turn(1)
            ssm_out(0, 1)
            ssm_out(1, 0)
            ssm_out(1, 1)
            ln_pe(pe, 4)
            pe.wait_ge(s_c5, 7)
            pe.wait_ge(s_xn, 10)

            def latent_project(h, slot, nth):
                pe.wait_ge(k_ld[slot], 96 * nth)
                if not isinstance(h, int) or h >= 1:
                    pe.wait_ge(k_wc, h)
                for r in range(2):
                    pe.matmul(PS[0:RQ, 6, r * DC:(r + 1) * DC], lwr[:, slot, r * RQ:(r + 1) * RQ], lwk[:, slot, :],
                              start=True, stop=True)
                pe.matmul(PS[0:DC, 6, 256:512], lwv[:, slot, :], lwo[:, slot, :], start=True, stop=True).then_inc(k_w, 1)
                if not isinstance(h, int) or h >= 1:
                    pe.wait_ge(k_qc, 2 * h)
                for hf in range(2):
                    for c in range(KC):
                        mm = pe.matmul(bank(hf), lwq[:, slot, c, :], xn[:, c, hf::2, 0:T], start=c == 0, stop=c == KC - 1)
                    mm.then_inc(k_q, 1)

            def latent_big(h, slot):
                for hf in range(2):
                    pe.wait_ge(k_qc, 2 * h + (hf + 1))
                    if not isinstance(h, int) or h >= 1:
                        pe.wait_ge(k_p, 2 * h + (hf - 1))
                    for r in range(2):
                        mm = pe.matmul(PS[0:RQ, 2 + 2 * hf + r, 0:NT], lwc[:, slot, r * RQ:(r + 1) * RQ], qh[:, hf, :],
                                       start=True, stop=True)
                    mm.then_inc(k_b, 1)

            def latent_absorb(h, slot):
                pe.wait_ge(k_r, 2 * h + 2)
                pe.wait_ge(k_lo, 2 * h + 1)
                pe.wait_ge(k_wc, h + 1)
                for r in range(2):
                    for hf in range(2):
                        mm = pe.matmul(PS[DC * hf:DC * hf + DC, 7, 0:NT], wab[:, slot, r, :], rot[:, hf, r, :],
                                       start=r == 0, stop=r == 1)
                mm.then_inc(k_a, 2)

            def keys_t(b, slot):
                pe.wait_ge(c_rp, b + 1)
                if not isinstance(b, int) or b >= 1:
                    pe.wait_ge(c_mn, b)
                if not isinstance(b, int) or b >= 2:
                    pe.wait_ge(c_cn, b - 1)
                for j in range(KT):
                    mm = pe.transpose(PS[:, j // 4, (j % 4) * KP:(j % 4) * KP + KP],
                                      kvr[:, slot, j, 0:2 * DC], ident[0:KP, 0:KP])
                mm.then_inc(c_tm, 1)

            latent_project(0, 0, 1)
            latent_big(0, 0)
            with pe.Fori(0, LH // 2 - 1) as j:
                for d in range(2):
                    h = 2 * j + (1 + d)
                    latent_project(h, (1 + d) % 2, j + (1 + d))
                    latent_big(h, (1 + d) % 2)
                    latent_absorb(2 * j + d, d)
            latent_project(LH - 1, 1, LH // 2)
            latent_big(LH - 1, 1)
            latent_absorb(LH - 2, 0)
            pe.wait_ge(k_p, 2 * LH)
            keys_t(0, 0)
            latent_absorb(LH - 1, 1)

            def row_scores(b, slot, n):
                k, j, rows = n // 3, n % 3, slice(DC * (n % 2), DC * (n % 2) + DC)
                if n == 0:
                    pe.wait_ge(c_khi, 3 * b + 3)
                    pe.wait_ge(c_klo, 3 * b + 3)
                    pe.wait_ge(c_qb, b + 1)
                if n >= 3:
                    pe.wait_ge(c_mr, PIECES * b + (n - 2))
                pe.matmul(PS[0:2 * T, j, 0:S // 3], (qb2, qb3)[n % 2][rows, slot, 2 * T * k:2 * T * (k + 1)],
                          khi[rows, slot, j * (S // 3):(j + 1) * (S // 3)], start=True, stop=True).then_inc(c_mm, 1)

            def max_t(b):
                pe.wait_ge(c_mx, b + 1)
                pe.transpose(PS[0:LH // 2, 2, 0:2 * T], rmx[:], ident[0:2 * T, 0:2 * T]).then_inc(c_mt, 1)

            def scores(b, slot, n):
                j, hf = n // 2, n % 2
                pe.wait_ge(c_ex, LS * b + (n + 1))
                keys = slice(j * KP, (j + 1) * KP)
                cut = slice(hf * NT, (hf + 1) * NT)
                pe.matmul(PS[0:KP, 3 + n % 3, 0:NT], khi[:, slot, keys], qb1[:, slot, cut], start=True, stop=False)
                pe.matmul(PS[0:KP, 3 + n % 3, 0:NT], klo[:, slot, keys], qb2[:, slot, cut],
                          start=False, stop=True).then_inc(c_sm, 1)

            def values(b, slot, j):
                pe.wait_ge(c_ex, LS * b + (2 * j + 5))
                if j == 0:
                    pe.wait_ge(c_cx, b + 1)
                for hf in range(2):
                    mm = pe.matmul(PS[DC * hf:DC * hf + DC, 6, 0:NT], kvr[:, slot, j, DC:2 * DC],
                                   pe3[:, (2 * j + hf) % 6, :], start=j == 0, stop=j == KT - 1)
                mm.then_inc(c_pv, 1)

            def prob_sums(b, k):
                pe.wait_ge(c_pa, 8 * b + (4 * k + 4))
                if k == 0 and (not isinstance(b, int) or b >= 1):
                    pe.wait_ge(c_ds, b)
                for q in range(4):
                    mm = pe.matmul(PS[32 * q:32 * q + 32, 7, 0:NT], ones[:], psm[:, q // 2, q % 2, :],
                                   start=k == 0, stop=k == 1)
                mm.then_inc(c_dn, 1)

            def spread_sums(b, rows):
                pe.wait_ge(c_ds, b + 1)
                pe.wait_ge(c_mx, rows)
                pe.matmul(PS[:, 0, 0:NT], pick[:], dsum[:], start=True, stop=True).then_inc(c_bc, 1)

            def latent_out(hf, m):
                for k in range(LH // 2):
                    mm = pe.matmul(bank(4 + 2 * hf + m), wvo[:, k, m * P:(m + 1) * P], cn[:, k, hf * HB:(hf + 1) * HB, :],
                                   start=k == 0, stop=k == LH // 2 - 1)
                mm.then_inc(c_om, 1)

            def latent_batch(b, slot, nth, last, prepare):
                rows = b + 1 if prepare is None else b + 2
                pe.wait_ge(c_row[slot], 16 * nth)
                for n in range(LS + 2):
                    if n < LS:
                        scores(b, slot, n)
                    if n % 2 == 1 and n >= 3:
                        values(b, slot, (n - 3) // 2)
                    if last is not None and n == 1:
                        prob_sums(last, 1)
                    if n == SUMS_AT:
                        prob_sums(b, 0)
                    if prepare is not None and n == KEYS_AT:
                        keys_t(prepare, 1 - slot)
                    if prepare is not None and 0 <= n - ROWS_AT < PIECES // 2:
                        for k in range(2):
                            row_scores(prepare, 1 - slot, 2 * (n - ROWS_AT) + k)
                    if prepare is not None and n == MAX_AT:
                        max_t(prepare)
                    if last is not None and n == MAX_AT:
                        spread_sums(last, rows)

            for n in range(PIECES):
                row_scores(0, 0, n)
            max_t(0)
            latent_batch(0, 0, 1, None, 1)
            with pe.Fori(0, B // 2 - 1) as j:
                for d in range(2):
                    b = 2 * j + (1 + d)
                    latent_batch(b, 1 - d, j + (1 + d), 2 * j + d, 2 * j + (2 + d))
            latent_batch(B - 1, 1, B // 2, B - 2, None)
            prob_sums(B - 1, 1)
            spread_sums(B - 1, B)
            pe.wait_ge(c_cn, B + 1)
            latent_out(0, 0)
            latent_out(0, 1)
            latent_out(1, 0)
            for i in range(PAIRS):
                if i == PAIRS // 2:
                    latent_out(1, 1)
                if i % (PAIRS // 2) == 0:
                    pe.wait_ge(c_xu, 1 + i // (PAIRS // 2))
                for c in range(KC):
                    mm = pe.transpose(PS[:, i // 2, (i % 2) * C + c * P:(i % 2) * C + (c + 1) * P],
                                      xT[:, c, 2 * i:2 * i + 2, :], ident[:])
                mm.then_inc(f_xm, 1)
            pb = PS[:].rearrange("p k n -> p (k n)").bitcast(BF16).rearrange("p (k n) -> p k n", k=8)
            pe.wait_ge(s_c6, 2)
            pe.wait_ge(f_ki, 1)
            for fc in range(KC):
                for dc in range(KC):
                    pe.transpose(pb[:, 6, (dc * KC + fc) * P:(dc * KC + fc + 1) * P], kwi[:, fc, dc * P:(dc + 1) * P], identb[:])
            for fc in range(KC):
                mm = pe.matmul(PS[:, 7, fc * P:(fc + 1) * P], one6[:], kdg[:, fc, :], start=True, stop=True)
            mm.then_inc(f_km, 1)
            for i in range(PAIRS):
                pe.wait_ge(f_xi, i + 1)
                pe.wait_ge(f_xc, PAIRS)
                if i >= 2:
                    pe.wait_ge(f_tc, i - 1)
                for c in range(KC):
                    mm = pe.transpose(pb[:, 4 + i % 2, c * P:(c + 1) * P], xi[:, i, c * P:(c + 1) * P], identb[:])
                mm.then_inc(f_tm, 1)
            pe.wait_ge(f_kc, 1)
            for i in range(PAIRS):
                pe.wait_ge(f_tc, i + 1)
                if i >= 4:
                    pe.wait_ge(f_yr, i - 3)
                for c in range(KC):
                    mm = pe.matmul(PS[:, i % 4, 0:C], xiT[:, c, i * P:(i + 1) * P], kwT[:, c, :],
                                   start=c == 0, stop=c == KC - 1)
                mm.then_inc(f_ym, 1)

        @block.scalar
        def _(act):
            act.wait_ge(s_const, 6)
            ln_act(act, 0)
            act.wait_ge(s_w1, 32)
            for hf in range(2):
                if hf == 1:
                    act.wait_ge(s_xr, 3)
                for m in range(4):
                    act.wait_ge(s_par, 4 * hf + m + 1)
                    o = (gate_s, val_s)[m // 2][:, m % 2, :]
                    act.activation(o, PS[:, 4 + m, 0:NT], (ACT.Sigmoid, ACT.Tanh)[m // 2],
                                   bias=b0[:, m:m + 1]).then_inc(s_pact, 1)
            ln_act(act, 1)

            def cross_copy_qv(i, slot):
                act.wait_ge(x_qm, i + 1)
                act.copy(qp[:].rearrange("p m b t -> p (m b t)"), PS[:, 0, :]).then_inc(x_qc, 1)
                act.wait_ge(x_vm, i + 1)
                act.copy(vp[:, slot, :, :, 0:XD], PS[:, 2, :].rearrange("p (b h d) -> p b h d", b=2, h=XH)).then_inc(x_vc, 1)

            def cross_exp(i):
                act.wait_ge(x_sh, i + 1)
                act.activation(pr[:, :, 0:T], sc[:], ACT.Exp).then_inc(x_ex, 1)

            def cross_copy_pt(i):
                act.wait_ge(x_tm, i + 1)
                act.copy(pt[:], PS[:, 0:2, :].rearrange("p k (m n) -> p (k m) n", n=P)).then_inc(x_tc, 1)

            cross_copy_qv(0, 0)
            cross_exp(0)
            cross_copy_qv(1, 1)
            with act.Fori(0, PAIRS // 2 - 1) as j:
                for d in range(2):
                    cross_copy_pt(2 * j + d)
                    cross_exp(2 * j + (1 + d))
                    cross_copy_qv(2 * j + (2 + d), d)
            cross_copy_pt(PAIRS - 2)
            cross_exp(PAIRS - 1)
            cross_copy_pt(PAIRS - 1)
            ln_act(act, 2)
            act.wait_ge(e_lm, 1)
            act.copy(logit[:].rearrange("p i e -> p (i e)"), PS[:, 4:6, :].rearrange("p k n -> p (k n)")).then_inc(e_lc, 1)
            def moe_shared_silu(n):
                act.wait_ge(e_sg, n + 1)
                if n >= 2:
                    act.wait_ge(e_sp, n - 1)
                act.activation(sgl[:, n % 2, :], PS[:, 2 * (n % 2), 0:NT], ACT.Silu).then_inc(e_ss, 1)

            def moe_silu(n):
                act.wait_ge(e_gm, n + 1)
                if n >= 2:
                    act.wait_ge(e_pd, n - 1)
                act.activation(sgl[:, n % 2, :], PS[:, 3 * (n % 2), 0:NT], ACT.Silu).then_inc(e_si, 1)

            moe_shared_silu(0)
            moe_shared_silu(1)
            act.wait_ge(e_sh, 1)
            act.activation(expo[:], expo[:], ACT.Exp).then_inc(e_ex, 1)
            moe_shared_silu(2)
            moe_shared_silu(3)
            act.wait_ge(e_sp, 4)
            moe_silu(0)
            moe_silu(1)
            act.wait_ge(e_tm, 1)
            act.copy(coT[:].rearrange("p b t -> p (b t)"), PS[:, 6:8, :].rearrange("p k n -> p (k n)")).then_inc(e_tc, 1)
            for n in range(2, 2 * KB):
                moe_silu(n)
            ln_act(act, 3)
            act.wait_ge(s_w4, 16 * 12)
            act.wait_ge(s_c4, 10)
            own = Own(act, own_a)
            act.wait_ge(d_ng, 1)
            own.step(act.activation(alog[:], alog[:], ACT.Exp))
            own.step(act.mul(alog[:], alog[:], -1.0))
            for hf in range(2):
                act.wait_ge(d_mm, hf + 1)
                raw = PS[0:NH, 6 + hf, 0:NT]
                act.activation(dts[:, 2 + hf, :], raw, ACT.Relu, bias=dtb[:])
                own.step(act.activation(dts[:, hf, :], raw, ACT.Abs, bias=dtb[:]))
                own.step(act.activation(dts[:, hf, :], dts[:, hf, :], ACT.Tanh, scale=0.5))
            for hf in range(2):
                act.activation(dts[:, hf, :], dts[:, hf, :], ACT.Ln, scale=0.5, bias=cst[0:NH, 0:1]).then_inc(d_ln, 1)
            for hf in range(2):
                act.wait_ge(d_dt, hf + 1)
                act.activation(aT[:, HB * hf:HB * hf + HB, :], dtc[:, HB * hf:HB * hf + HB, 0:T], ACT.Exp,
                               scale=alog[:]).then_inc(d_ex, 1)

            def ssm_square(n):
                act.wait_ge(b_mm, n + 1)
                if n >= 2:
                    act.wait_ge(b_ms, n - 1)
                act.activation(bsq[n % 2], PS[:, 3 * (n % 2), 0:NT], ACT.Square).then_inc(b_sq, 1)

            def ssm_std(n):
                act.wait_ge(b_ms, n + 1)
                if n >= 2:
                    act.wait_ge(b_n, n - 1)
                act.activation(bst[n % 2], PS[:, 3 * (n % 2) + 2, 0:NT], ACT.Sqrt, scale=2.0 * P / 128, bias=cst[:, 1:2]).then_inc(b_sd, 1)

            def ssm_silu(i):
                act.wait_ge(z_mm, i + 1)
                act.activation(siz[:, i, :], PS[:, zx_banks[i][0], :], ACT.Silu).then_inc(z_si, 1)

            for n in range(2):
                ssm_square(n)
            act.wait_ge(d_tm, 1)
            act.copy(dtt[:].rearrange("p i h -> p (i h)"), PS[:, 6, :]).then_inc(d_tc, 1)
            for n in range(2):
                ssm_std(n)
            ssm_silu(0)
            ssm_silu(1)
            ssm_square(2)
            ssm_square(3)
            ssm_std(2)
            ssm_std(3)

            def ssm_turns(hp, slot, nth):
                act.wait_ge(m_tbc[slot], 32 * nth)
                f = fcol[:, hp:hp + 1] if isinstance(hp, int) else fcol[:, bass.ds(hp, 1)]
                act.activation(frac[:, slot, :], frac[:, slot, :], ACT.Copy, scale=f).then_inc(m_tu, 1)

            def ssm_sines(hp, slot):
                act.wait_ge(m_fr, hp + 1)
                if not isinstance(hp, int) or hp >= 2:
                    act.wait_ge(m_tc, hp - 1)
                own.step(act.activation(cs[:, slot, :], frac[:, slot, :], ACT.Abs))
                act.activation(sn[:, slot, :], frac[:, slot, :], ACT.Sin, scale=TWO_PI)
                own.step(act.activation(cs[:, slot, :], cs[:, slot, :], ACT.Sin, scale=-TWO_PI, bias=cst[:, 2:3]))
                act.sem_inc(m_sin, 1)

            def ssm_copy_y(hp, slot):
                act.wait_ge(m_y, hp + 1)
                for h2 in range(2):
                    at = hp * 2 * HD + h2 * HD
                    at = slice(at, at + HD) if isinstance(hp, int) else bass.ds(at, HD)
                    y = PS[64 * h2:64 * h2 + 64, 4 + slot, 0:4 * HD * PAIRS].rearrange("p (i b n) -> p i b n", b=2, n=2 * HD)
                    for b2 in range(2):
                        ins = act.copy(ya[64 * b2:64 * b2 + 64, :, at], y[:, :, b2, h2 * HD:(h2 + 1) * HD])
                ins.then_inc(m_yc, 1)

            def ssm_scalar(k, p, nth):
                if not isinstance(k, int) or k + 3 < NP2:
                    ssm_turns(k + 3, 1 - p, nth)
                if not isinstance(k, int) or 1 <= k:
                    ssm_copy_y(k - 1, 1 - p)
                if not isinstance(k, int) or k + 3 < NP2:
                    ssm_sines(k + 3, 1 - p)

            for i in range(2, 4):
                ssm_silu(i)
            act.wait_ge(s_c4, 11)
            ssm_turns(0, 0, 1)
            ssm_silu(4)
            ssm_turns(1, 1, 1)
            ssm_sines(0, 0)
            for i in range(5, PAIRS):
                ssm_silu(i)
            ssm_sines(1, 1)
            for k in range(-1, 2):
                ssm_scalar(k, k % 2, (k + 3) // 2 + 1)
            with act.Fori(0, SSM_TRIPS) as j:
                own.enter(j, 4)
                for d in range(2):
                    ssm_scalar(2 * j + (2 + d), d, j + (3 + d))
            own.leave(SSM_TRIPS)
            for k in range(NP2 - 4, NP2 + 1):
                ssm_scalar(k, k % 2, (k + 3) // 2 + 1)
            for i in range(PAIRS):
                act.wait_ge(g_g, i + 1)
                act.activation(ysq[:, 0, 0:DI], ya[:, i, :], ACT.Square, accum_out=yss[:, i:i + 1]).then_inc(g_sq, 1)
                act.wait_ge(g_sq, i + 1)
                if i % 4 == 3:
                    act.activation(yss[:, i - 3:i + 1], yss[:, i - 3:i + 1], ACT.Sqrt, scale=1.0 / DI, bias=cst[:, 1:2]).then_inc(g_sd, 1)
            ln_act(act, 4)

            def latent_copies(h, pair, slot, absorb, place):
                act.wait_ge(k_w, h + 1)
                if not isinstance(h, int) or h >= 2:
                    act.wait_ge(k_a, 2 * h - 2)
                act.copy(wab[:, slot, :, :].rearrange("p r n -> p (r n)"), PS[0:RQ, 6, 0:2 * DC])
                rows = slice(DC * slot, DC * slot + DC)
                w = wvo[rows, pair, :] if isinstance(h, int) else wvo[rows, bass.ds(pair, 1), :].rearrange("p o n -> p (o n)")
                act.copy(w, PS[0:DC, 6, 256:512]).then_inc(k_wc, 1)
                for hf in range(2):
                    act.wait_ge(k_q, 2 * h + (hf + 1))
                    if not isinstance(h, int) or h >= 1:
                        act.wait_ge(k_b, 2 * h + (hf - 1))
                    act.copy(qh[:, hf, :], PS[:, hf, 0:NT]).then_inc(k_qc, 1)
                if absorb is not None:
                    latent_high(absorb, place)

            def latent_high(h, place):
                for hf in range(2):
                    act.wait_ge(k_a, 2 * h + 2)
                    hs = slice(place, place + 1) if isinstance(h, int) else bass.ds(place, 1)
                    rows = slice(DC * hf, DC * hf + DC)
                    act.copy(qa[rows, hf::2, hs, :].rearrange("p b o t -> p b (o t)"), bank(7, rows=rows)).then_inc(k_hi, 1)

            act.sem_inc(c_ex, 3)
            act.wait_ge(s_xn, 10)
            latent_copies(0, 0, 0, None, None)
            with act.Fori(0, LH // 2 - 1) as j:
                for d in range(2):
                    latent_copies(2 * j + (1 + d), j + d, (1 + d) % 2, 2 * j + d, j + LH // 2 * d)
            latent_copies(LH - 1, LH // 2 - 1, 1, LH - 2, LH // 2 - 1)
            def keys_high(b, slot, k):
                act.wait_ge(c_tm, b + 1)
                act.copy(khi[:, slot, k * (S // 3):(k + 1) * (S // 3)], PS[:, k, 0:S // 3]).then_inc(c_khi, 1)

            for k in range(3):
                keys_high(0, 0, k)
            latent_high(LH - 1, LH - 1)

            def max_row(b, slot):
                act.wait_ge(c_mt, b + 1)
                act.mul(rmn[:], PS[0:LH // 2, 2, 0:2 * T], -1.0).then_inc(c_mn, 1)
                act.wait_ge(c_mn, b + 1)
                act.dma_start(qb2[DC:DC + 1, slot, :].rearrange("o (k n) -> o k n", k=LH // 2), rmn[:]).then_inc(c_row[slot], 16)

            def latent_exp(b, slot, nth, prepare):
                for n in range(LS):
                    act.wait_ge(c_sm, LS * b + (n + 1))
                    if not isinstance(b, int) or b >= 1 or n >= 6:
                        act.wait_ge(c_pv, KT * b + ((n - 6) // 2 + 1))
                        k, tile = divmod(n // 2 - 3, 3)
                        act.wait_ge(c_pa, 8 * b + (2 * k + (1, 1, 2)[tile]))
                    act.activation(pe3[:, n % 6, :], PS[0:KP, 3 + n % 3, 0:NT], ACT.Exp).then_inc(c_ex, 1)
                    if prepare is not None and 0 <= n - KEYS_AT < 3:
                        keys_high(prepare, 1 - slot, n - KEYS_AT)
                    if prepare is not None and n == MAX_AT:
                        max_row(prepare, 1 - slot)

            max_row(0, 0)
            latent_exp(0, 0, 1, 1)
            with act.Fori(0, B // 2 - 1) as j:
                for d in range(2):
                    latent_exp(2 * j + (1 + d), 1 - d, None, 2 * j + (2 + d))
            latent_exp(B - 1, 1, None, None)
            pb = PS[:].rearrange("p k n -> p (k n)").bitcast(BF16).rearrange("p (k n) -> p k n", k=8)
            for i in range(PAIRS):
                act.wait_ge(f_xm, 2 * (i // 2) + 2)
                act.copy(xt[:, i, :], PS[:, i // 2, (i % 2) * C:(i % 2 + 1) * C]).then_inc(f_xc, 1)
            act.wait_ge(f_va, 1)
            act.activation(sx[:, 0, :], mv6[:, :, 1], ACT.Sqrt, bias=epsc[:]).then_inc(f_sd, 1)
            act.wait_ge(f_km, 1)
            act.copy(kwT[:].rearrange("p c f -> p (c f)"), pb[:, 6, 0:KC * C])
            act.copy(skb[:], PS[:, 7, 0:C]).then_inc(f_kc, 1)
            for i in range(PAIRS):
                act.wait_ge(f_tm, i + 1)
                act.copy(xiT[:, :, i * P:(i + 1) * P], pb[:, 4 + i % 2, 0:C].rearrange("p (c n) -> p c n", n=P)).then_inc(f_tc, 1)

        @block.vector
        def _(v):
            own = Own(v, own_v)
            v.wait_ge(s_const, 6)
            v.wait_ge(s_x, 16)
            for hf in range(2):
                v.nop().then_inc(s_xr, 1)
            ln_dve(v, own, 0)
            for hf in range(2):
                v.wait_ge(s_pact, 4 * hf + 4)
                own.step(v.memset(cols(gate_s[:].rearrange("p c n -> p (c n)"))[:, :, 0:1], 0.0))
                for c in range(KC):
                    own.done(v.tensor_tensor_scan(hid[:, c, :], gate_s[:, c, :], val_s[:, c, :], 0.0, ALU.mult, ALU.add))
                own.wait()
                for c in range(KC):
                    ins = v.tensor_tensor(half(xT, c, hf), half(xT, c, hf), cols(hid[:, c, :]), ALU.add)
                ins.then_inc(s_xr, 1)
                v.wait_ge(s_xr, 3 + hf)
            ln_dve(v, own, 1)

            def cross_copy_k(i):
                v.wait_ge(x_km, i + 1)
                v.tensor_copy(kp[:].rearrange("p m b t -> p (m b t)"), PS[:, 1, :]).then_inc(x_kc, 1)

            def cross_softmax(i):
                v.wait_ge(x_sm, i + 1)
                mask = maskc[:].unsqueeze(1).broadcast_to((P, 4, T))
                for r in range(4):
                    s_r = PS[:, 4 + r, 0:4 * TP].rearrange("p (c t) -> p c t", t=TP)[:, :, 0:T]
                    ins = v.scalar_tensor_tensor(sc[:, 4 * r:4 * r + 4, :], s_r, XD ** -0.5, mask,
                                                 ALU.mult, ALU.add)
                own.step(ins)
                v.sem_inc(x_sr, 1)
                own.step(v.tensor_reduce(mxs[:], sc[:], AX, ALU.max))
                v.tensor_tensor(sc[:], sc[:], mxs[:].unsqueeze(2).broadcast_to((P, XH, T)),
                                ALU.subtract).then_inc(x_sh, 1)
                v.wait_ge(x_ex, i + 1)
                own.step(v.tensor_reduce(sms[:], pr[:, :, 0:T], AX, ALU.add))
                own.step(v.reciprocal(sms[:], sms[:]))
                v.tensor_tensor(pr[:, :, 0:T], pr[:, :, 0:T], sms[:].unsqueeze(2).broadcast_to((P, XH, T)),
                                ALU.mult).then_inc(x_pr, 1)

            def cross_copy_o(i):
                v.wait_ge(x_om, i + 1)
                pair = slice(2 * i, 2 * i + 2) if isinstance(i, int) else bass.ds(2 * i, 2)
                for e in range(2):
                    ins = v.tensor_copy(oT[:, e::2, pair, 0:T],
                                        PS[:, 2 + e, 0:4 * T].rearrange("p (c b t) -> p c b t", c=2, b=2))
                ins.then_inc(x_oc, 1)

            cross_copy_k(0)
            cross_softmax(0)
            cross_copy_k(1)
            with v.Fori(0, PAIRS // 2 - 1) as j:
                own.enter(j, 8)
                for d in range(2):
                    cross_softmax(2 * j + (1 + d))
                    cross_copy_o(2 * j + d)
                    cross_copy_k(2 * j + (2 + d))
            own.leave(PAIRS // 2 - 1)
            cross_softmax(PAIRS - 1)
            for i in (PAIRS - 2, PAIRS - 1):
                cross_copy_o(i)
            for hf in range(2):
                for m in range(KC):
                    v.wait_ge(x_wm, 2 * hf + m + 1)
                    ins = v.tensor_tensor(half(xT, m, hf), half(xT, m, hf), bank(4 + 2 * hf + m), ALU.add)
                ins.then_inc(s_xr, 1)
            v.wait_ge(s_xr, 6)
            v.wait_ge(s_w3, 16 * 9)
            own.step(v.tensor_tensor(amps[:], amps[:], amps[:], ALU.mult))
            own.step(v.tensor_tensor(mix[:], amps[:, 0, :], amps[:, 1, :], ALU.add))
            own.step(v.tensor_reduce(msum[:], mix[:], AX, ALU.add))
            own.step(v.tensor_scalar(msum[:], msum[:], 1e-8, None, ALU.add))
            own.step(v.reciprocal(msum[:], msum[:]))
            own.step(v.tensor_scalar(mix[:], mix[:], msum[:], escale[:], ALU.mult, ALU.mult))
            v.tensor_copy(mixb[:], mix[:].unsqueeze(2).broadcast_to((P, KB, P))).then_inc(e_mix, 1)
            ln_dve(v, own, 2)
            v.wait_ge(e_lc, 1)
            v.wait_ge(s_keep, 1)
            for i in range(PAIRS):
                ins = v.max(top8[:, i, :], logit[:, i, :])
            own.step(ins)
            shape = (P, PAIRS, E)
            v.tensor_tensor(expo[:], logit[:], top8[:, :, 0:1].broadcast_to(shape), ALU.subtract).then_inc(e_sh, 1)

            def moe_shared_product(n):
                v.wait_ge(e_ss, n + 1)
                v.tensor_tensor(shr[:, n // 2, n % 2, :], sgl[:, n % 2, :], PS[:, 2 * (n % 2) + 1, 0:NT], ALU.mult).then_inc(e_sp, 1)

            own.done(v.tensor_tensor(above[:], logit[:], top8[:, :, TOPK - 1:TOPK].broadcast_to(shape), ALU.is_gt))
            own.step(v.tensor_tensor(level[:], logit[:], top8[:, :, TOPK - 1:TOPK].broadcast_to(shape), ALU.is_equal))
            moe_shared_product(0)
            own.done(v.tensor_reduce(room[:], above[:], AX, ALU.add))
            own.step(v.tensor_tensor_scan(place[:].rearrange("p i e -> p (i e)"), keep[:],
                                          level[:].rearrange("p i e -> p (i e)"), 0.0, ALU.mult, ALU.add))
            moe_shared_product(1)
            own.step(v.tensor_scalar(room[:], room[:], -1.0, float(TOPK), ALU.mult, ALU.add))
            own.step(v.tensor_tensor(place[:], place[:], room[:].unsqueeze(2).broadcast_to(shape), ALU.is_le))
            own.step(v.tensor_tensor(level[:], level[:], place[:], ALU.mult))
            own.step(v.tensor_tensor(level[:], level[:], above[:], ALU.add))
            moe_shared_product(2)
            v.wait_ge(e_ex, 1)
            own.step(v.tensor_reduce(zsum[:], expo[:], AX, ALU.add))
            own.step(v.tensor_tensor(expo[:], expo[:], level[:], ALU.mult))
            moe_shared_product(3)
            own.step(v.tensor_reduce(tsum[:], expo[:], AX, ALU.add))
            own.step(v.scalar_tensor_tensor(tsum[:], zsum[:], 1e-8, tsum[:], ALU.mult, ALU.add))
            own.step(v.reciprocal(tsum[:], tsum[:]))
            v.tensor_tensor(expo[:], expo[:], tsum[:].unsqueeze(2).broadcast_to(shape), ALU.mult).then_inc(e_co, 1)
            for hf in range(2):
                for k in range(KB):
                    n = hf * KB + k
                    gb = 3 * (n % 2)
                    v.wait_ge(e_si, n + 1)
                    v.wait_ge(e_um, n + 1)
                    own.step(v.tensor_tensor(gu[:, n % 2, :], sgl[:, n % 2, :], PS[:, gb + 1, 0:NT], ALU.mult))
                    o = acc[:, hf, :] if k == 0 else wgu[:]
                    v.tensor_tensor(o, gu[:, n % 2, :], PS[:, gb + 2, 0:NT], ALU.mult).then_inc(e_pd, 1)
                    v.wait_ge(e_pd, n + 1)
                    if k > 0:
                        own.step(v.tensor_tensor(acc[:, hf, :], acc[:, hf, :], wgu[:], ALU.add))
                v.wait_ge(e_sp, 4)
                v.sem_inc(e_ac, 1)
            for hf in range(2):
                for m in range(KC):
                    v.wait_ge(e_dm, 2 * hf + m + 1)
                    ins = v.tensor_tensor(half(xT, m, hf), half(xT, m, hf), bank(6 + m), ALU.add)
                ins.then_inc(s_xr, 1)
            v.wait_ge(s_xr, 8)
            v.wait_ge(s_w4, 16 * 12)
            v.wait_ge(s_c4, 11)
            v.tensor_scalar(alog[:], alog[:], 80.0, None, ALU.min).then_inc(d_ng, 1)
            ln_dve(v, own, 3)
            for hf in range(2):
                v.wait_ge(d_ln, hf + 1)
                v.tensor_tensor(dtc[:, HB * hf:HB * hf + HB, 0:T], cols(dts[:, 2 + hf, :]), cols(dts[:, hf, :]),
                                ALU.subtract).then_inc(d_dt, 1)
            for hf in range(2):
                v.wait_ge(d_dt, hf + 1)
                own.step(v.tensor_copy(dts[:, hf, :].rearrange("p (b t) -> p b t", t=T), dtc[:, HB * hf:HB * hf + HB, 0:T]))
                v.tensor_tensor_scan(cum[:, hf * NT:(hf + 1) * NT], keept[:], dts[:, hf, :], 0.0,
                                     ALU.mult, ALU.add).then_inc(d_cum, 1)
            for hf in range(2):
                v.wait_ge(d_ex, hf + 1)
                v.memset(aT[:, HB * hf:HB * hf + HB, 0:1], 0.0).then_inc(d_a, 1)

            def ssm_norm(n):
                hf, x, bb = n // 2, n % 2, 3 * (n % 2)
                v.wait_ge(b_sd, n + 1)
                own.step(v.reciprocal(bst[x], bst[x]))
                for s in range(2):
                    ins = v.tensor_tensor(bcn[:, 2 * x + s, hf * NT:(hf + 1) * NT], PS[:, bb + s, 0:NT], bst[x], ALU.mult)
                ins.then_inc(b_n, 1)

            def ssm_inputs_scaled(i):
                v.wait_ge(z_mm, i + 1)
                xs = PS[:, zx_banks[i][1], :].rearrange("p (h q) -> p h q", q=HD)
                v.tensor_tensor(dx[:, i, :].rearrange("p (h q) -> p h q", q=HD), xs,
                                dbc[:].unsqueeze(2).broadcast_to((P, NH, HD)), ALU.mult)
                v.tensor_tensor(ua[:, i, :].rearrange("p (h q) -> p h q", q=HD), xs,
                                dtt[:, i, :].unsqueeze(2).broadcast_to((P, NH, HD)), ALU.mult).then_inc(z_u, 1)

            ssm_norm(0)
            ssm_norm(1)
            v.wait_ge(d_tc, 1)
            ssm_inputs_scaled(0)
            ssm_inputs_scaled(1)
            ssm_norm(2)
            ssm_inputs_scaled(2)
            ssm_norm(3)
            v.wait_ge(b_n, 4)

            def ssm_rotation(hp, slot):
                v.wait_ge(m_tu, hp + 1)
                if not isinstance(hp, int) or hp >= 1:
                    v.wait_ge(m_fr, hp)
                own.step(v.tensor_scalar(turn[:], frac[:, slot, :], ROUND, -ROUND, ALU.add, ALU.add))
                v.tensor_tensor(frac[:, slot, :], frac[:, slot, :], turn[:], ALU.subtract).then_inc(m_fr, 1)

            def ssm_products(hp, slot):
                v.wait_ge(m_sin, hp + 1)
                for x, s in ((0, m_tb), (1, m_tc)):
                    if not isinstance(hp, int) or hp >= 1:
                        v.wait_ge((m_rb, m_rc)[x], (1 + x) * hp)
                    for k, tab in ((2 * x, cs), (2 * x + 1, sn)):
                        bk = bias[:, k, hp:hp + 1] if isinstance(hp, int) else bias[:, k, bass.ds(hp, 1)]
                        ins = v.scalar_tensor_tensor(rt[:, k, :], bcn[:, k, :], bk, tab[:, slot, :], ALU.add, ALU.mult)
                    ins.then_inc(s, 1)

            def ssm_scan(hp, slot, nth):
                v.wait_ge(m_abc[slot], 32 * nth)
                v.tensor_tensor_scan(dec[:], ab[:, slot, :], eye[:], 0.0, ALU.mult, ALU.add).then_inc(m_sc, 1)

            def ssm_decay(hp, slot):
                v.wait_ge(m_sc, hp + 1)
                if not isinstance(hp, int) or hp >= 2:
                    v.wait_ge(m_y, hp - 1)
                v.wait_ge(m_g, hp + 1)
                for q in range(2):
                    blocks = slice(q * PAIRS, (q + 1) * PAIRS)
                    ins = v.tensor_tensor(mt[:, slot, blocks, 0:T], bank(2 + q),
                                          dec[:].rearrange("p (n t) -> p n t", t=T)[:, blocks, :], ALU.mult)
                ins.then_inc(m_mt, 1)
                v.wait_ge(m_mt, hp + 1)

            def ssm_vector(k, p, nth):
                if not isinstance(k, int) or 0 <= k < NP2:
                    ssm_scan(k, p, nth)
                if not isinstance(k, int) or 0 <= k + 1 < NP2:
                    ssm_products(k + 1, 1 - p)
                if not isinstance(k, int) or 0 <= k < NP2:
                    ssm_decay(k, p)
                if not isinstance(k, int) or k + 3 < NP2:
                    ssm_rotation(k + 3, 1 - p)

            for k in range(-3, 0):
                ssm_inputs_scaled(k + 6)
                ssm_vector(k, k % 2, 1)
            ssm_inputs_scaled(6)
            ssm_inputs_scaled(7)
            for k in range(2):
                ssm_vector(k, k % 2, 1)
            with v.Fori(0, SSM_TRIPS) as j:
                own.enter(j, 2)
                for d in range(2):
                    ssm_vector(2 * j + (2 + d), d, j + 2)
            own.leave(SSM_TRIPS)
            for k in range(NP2 - 4, NP2):
                ssm_vector(k, k % 2, k // 2 + 1)
            v.wait_ge(m_yc, NH // 2)
            def ssm_gate(pairs):
                for i in pairs:
                    own.done(v.scalar_tensor_tensor(ya[:, i, :], ya[:, i, :], DS ** -0.5, dx[:, i, :], ALU.mult, ALU.add))
                own.wait()
                for i in pairs:
                    v.tensor_tensor(ya[:, i, :], ya[:, i, :], siz[:, i, :], ALU.mult).then_inc(g_g, 1)

            def ssm_normalise(hf):
                v.wait_ge(g_sd, hf + 1)
                own.step(v.reciprocal(yss[:, 4 * hf:4 * hf + 4], yss[:, 4 * hf:4 * hf + 4]))
                for i in range(4 * hf, 4 * hf + 4):
                    v.tensor_scalar(ya[:, i, :], ya[:, i, :], yss[:, i:i + 1], None, ALU.mult).then_inc(g_n, 1)

            def ssm_channels(hf):
                for i in range(4 * hf, 4 * hf + 4):
                    v.wait_ge(g_tm, i + 1)
                    for b2 in range(2):
                        o = gT[:, :, (2 * i + b2) * T:(2 * i + b2 + 1) * T]
                        s = PS[:, i % 4, :].rearrange("p (c n) -> p c n", n=P)[:, :, 64 * b2:64 * b2 + T]
                        ins = v.tensor_tensor(o, s, nw[:].unsqueeze(2).broadcast_to((P, DI // P, T)), ALU.mult)
                    ins.then_inc(g_tc, 1)

            ssm_gate(range(0, 2))
            ssm_gate(range(2, 4))
            ssm_gate(range(4, 6))
            ssm_normalise(0)
            ssm_gate(range(6, 8))
            ssm_channels(0)
            ssm_normalise(1)
            ssm_channels(1)
            for hf in range(2):
                for m in range(KC):
                    v.wait_ge(g_wm, 2 * hf + m + 1)
                    ins = v.tensor_tensor(half(xT, m, hf), half(xT, m, hf), bank(4 + 2 * hf + m), ALU.add)
                ins.then_inc(s_xr, 1)
            v.wait_ge(s_xr, 10)
            ln_dve(v, own, 4)
            v.sem_inc(k_lo, 1)
            v.sem_inc(c_cx, 1)
            v.sem_inc(c_cn, 1)
            v.wait_ge(s_w5, 48)

            def latent_products(h, hf):
                v.wait_ge(k_b, 2 * h + (hf + 1))
                if not isinstance(h, int) or h >= 1:
                    v.wait_ge(k_r, 2 * h + (hf - 1))
                for n, (r, k) in enumerate(((0, 0), (1, 1), (1, 2), (0, 3))):
                    ins = v.tensor_tensor(cols(rp4[:, hf, n, :]), bank(2 + 2 * hf + r, rows=slice(0, RQ)),
                                          rqt[:, k:k + 1, :].broadcast_to((RQ, HB, T)), ALU.mult)
                ins.then_inc(k_p, 1)

            def latent_low(h, place):
                for hf in range(2):
                    v.wait_ge(k_hi, 2 * h + (hf + 1))
                    hs = slice(place, place + 1) if isinstance(h, int) else bass.ds(place, 1)
                    high, low = (qa[DC * n:DC * n + DC, hf::2, hs, :].rearrange("p b o t -> p b (o t)") for n in (hf, 1 - hf))
                    v.tensor_tensor(low, bank(7, rows=slice(DC * hf, DC * hf + DC)), high, ALU.subtract).then_inc(k_lo, 1)

            for hf in range(2):
                latent_products(0, hf)
            with v.Fori(0, LH // 2 - 1) as j:
                for d in range(2):
                    for hf in range(2):
                        latent_products(2 * j + (1 + d), hf)
                    latent_low(2 * j + d, j + LH // 2 * d)
            for hf in range(2):
                latent_products(LH - 1, hf)
            latent_low(LH - 2, LH // 2 - 1)
            def keys_low(b, slot):
                for k in range(3):
                    v.wait_ge(c_khi, 3 * b + (k + 1))
                    third = slice(k * (S // 3), (k + 1) * (S // 3))
                    v.tensor_tensor(klo[0:DC, slot, third], PS[0:DC, k, 0:S // 3], khi[0:DC, slot, third],
                                    ALU.subtract).then_inc(c_klo, 1)

            keys_low(0, 0)
            latent_low(LH - 1, LH - 1)
            v.wait_ge(k_lo, 2 * LH + 1)

            def batch_queries(b, slot):
                src = qa[:, b:b + 1] if isinstance(b, int) else qa[:, bass.ds(b, 1)]
                src = src.rearrange("p o h t -> p (o h t)")
                v.tensor_copy(qb1[:, slot, :], src)
                high = src[DC * slot:DC * slot + DC]
                v.tensor_copy(qb3[DC:P, slot, :], high)
                v.tensor_copy(qb2[0:DC, slot, :], high).then_inc(c_qb, 1)

            def row_max(b):
                if not isinstance(b, int) or b >= 1:
                    v.wait_ge(c_mx, b)
                for n in range(PIECES):
                    v.wait_ge(c_mm, PIECES * b + (n + 1))
                    v.tensor_reduce(rmp[:, n:n + 1], PS[0:2 * T, n % 3, 0:S // 3], AX, ALU.max).then_inc(c_mr, 1)
                if not isinstance(b, int) or b >= 1:
                    v.wait_ge(c_mt, b)
                v.wait_ge(c_mr, PIECES * b + PIECES)
                v.tensor_reduce(rmx[:], rmp[:].rearrange("p (k j) -> p k j", j=3), AX, ALU.max).then_inc(c_mx, 1)

            def latent_sums(b):
                v.wait_ge(c_cn, b + 1)
                v.wait_ge(c_pv, KT * b + KT)
                v.tensor_copy(cx[:], PS[:, 6, 0:NT]).then_inc(c_cx, 1)

            def latent_denominators(b):
                v.wait_ge(c_dn, 2 * b + 2)
                v.tensor_copy(dsum[:], PS[:, 7, 0:NT]).then_inc(c_ds, 1)
                v.wait_ge(c_ds, b + 1)
                v.wait_ge(c_cx, b + 2)

            def latent_update(b):
                v.wait_ge(c_bc, b + 1)
                own.step(v.reciprocal(rden[:], PS[:, 0, 0:NT]))
                o = (cn[:, :, b:b + 1, :] if isinstance(b, int) else cn[:, :, bass.ds(b, 1), :]).rearrange("p k o t -> p k (o t)")
                v.tensor_tensor(o, cols(cx[:]), cols(rden[:]), ALU.mult).then_inc(c_cn, 1)

            batch_queries(0, 0)
            row_max(0)

            def latent_vector(b, slot, last, prepare):
                if last is not None:
                    latent_sums(last)
                if prepare is not None:
                    batch_queries(prepare, 1 - slot)
                if last is not None:
                    latent_denominators(last)
                if prepare is not None:
                    keys_low(prepare, 1 - slot)
                    row_max(prepare)
                if last is not None:
                    latent_update(last)

            latent_vector(0, 0, None, 1)
            with v.Fori(0, B // 2 - 1) as j:
                own.enter(j, 2)
                for d in range(2):
                    latent_vector(2 * j + (1 + d), 1 - d, 2 * j + d, 2 * j + (2 + d))
            own.leave(B // 2 - 1)
            latent_vector(B - 1, 1, B - 2, None)
            latent_sums(B - 1)
            latent_denominators(B - 1)
            latent_update(B - 1)

            def latent_add(hf):
                for m in range(KC):
                    v.wait_ge(c_om, 2 * hf + m + 1)
                    ins = v.tensor_tensor(half(xT, m, hf), half(xT, m, hf), bank(4 + 2 * hf + m), ALU.add)
                ins.then_inc(c_xu, 1)
            def quant_scale(s):
                own.step(v.tensor_scalar(s[:, 3], s[:, 0], 0.0, None, ALU.is_equal))
                own.step(v.scalar_tensor_tensor(s[:, 1], s[:, 0], 1.0 / 127.0, s[:, 3], ALU.mult, ALU.add))
                own.step(v.reciprocal(s[:, 2], s[:, 1]))

            def whole(o, a, inv):
                own.step(v.tensor_scalar(o, a, inv, ROUND, ALU.mult, ALU.add))
                own.step(v.tensor_scalar(o, o, -ROUND, 127.0, ALU.add, ALU.min))
                return v.tensor_scalar(o, o, -127.0, None, ALU.max)

            v.wait_ge(s_w6, 32)
            own.step(v.tensor_reduce(sk[:, 0, :], kw[:], AX, ALU.max, apply_absolute_value=True))
            own.step(v.tensor_reduce(sbq[:, 0:1], bq[:], AX, ALU.max, apply_absolute_value=True))
            quant_scale(sk)
            quant_scale(sbq[:].unsqueeze(2))
            for c in range(KC):
                own.step(v.tensor_scalar(kdg[:, c, :], ident[:], sk[:, 1, c:c + 1], None, ALU.mult))
                whole(kw[:, c, :], kw[:, c, :], sk[:, 2, c:c + 1]).then_inc(own_v, 1)
                own.n += 1
            own.wait()
            v.tensor_copy(kwi[:], kw[:]).then_inc(f_ki, 1)
            own.step(whole(bqi[:], bq[:], sbq[:, 2:3]))
            own.step(v.tensor_scalar(bq[:], bqi[:], sbq[:, 1:2], None, ALU.mult))
            latent_add(0)
            for i in range(PAIRS):
                if i == PAIRS // 2:
                    latent_add(1)
                v.wait_ge(f_xc, i + 1)
                own.done(v.bn_stats(st6[:, i, :], xt[:, i, :]))
            own.wait()
            for i in range(PAIRS):
                ins = v.bn_aggr(mv6[:, i, :], st6[:, i, :])
            ins.then_inc(f_va, 1)
            v.wait_ge(f_sd, 1)
            own.step(v.reciprocal(sx[:, 0, :], sx[:, 0, :]))
            for i in range(PAIRS):
                own.done(v.tensor_scalar(xq[:, i, :], xt[:, i, :], mv6[:, i, 0:1], sx[:, 0, i:i + 1], ALU.subtract, ALU.mult))
            own.wait()
            own.step(v.tensor_reduce(sx[:, 0, :], xq[:], AX, ALU.max, apply_absolute_value=True))
            quant_scale(sx)
            for lo in range(0, PAIRS, 4):
                tiles = slice(lo, lo + 4)
                for i in range(lo, lo + 4):
                    own.done(v.tensor_scalar(xq[:, i, :], xq[:, i, :], sx[:, 2, i:i + 1], ROUND, ALU.mult, ALU.add))
                own.wait()
                own.step(v.tensor_scalar(xq[:, tiles, :], xq[:, tiles, :], -ROUND, 127.0, ALU.add, ALU.min))
                v.tensor_scalar(xi[:, tiles, :], xq[:, tiles, :], -127.0, None, ALU.max).then_inc(f_xi, 4)
            v.wait_ge(f_kc, 1)
            for lo in range(0, PAIRS, 4):
                tiles = slice(lo, lo + 4)
                for i in range(lo, lo + 4):
                    v.wait_ge(f_ym, i + 1)
                    v.scalar_tensor_tensor(y6[:, i, :], PS[:, i % 4, 0:C], sx[:, 1, i:i + 1], skb[:], ALU.mult, ALU.mult).then_inc(f_yr, 1)
                v.wait_ge(f_yr, lo + 4)
                own.step(v.tensor_tensor(y6[:, tiles, :], y6[:, tiles, :], bq[:].unsqueeze(1).broadcast_to((P, 4, C)), ALU.add))
                own.step(v.tensor_scalar(y6[:, tiles, :], y6[:, tiles, :], 0.0, None, ALU.max))
                own.step(v.tensor_reduce(sy[:, 0, tiles], y6[:, tiles, :], AX, ALU.max))
                quant_scale(sy[:, :, tiles])
                for i in range(lo, lo + 4):
                    own.done(v.tensor_scalar(y6[:, i, :], y6[:, i, :], sy[:, 2, i:i + 1], ROUND, ALU.mult, ALU.add))
                own.wait()
                own.step(v.tensor_scalar(y6[:, tiles, :], y6[:, tiles, :], -ROUND, 127.0, ALU.add, ALU.min))
                own.step(v.tensor_scalar(y6[:, tiles, :], y6[:, tiles, :], -127.0, None, ALU.max))
                for i in range(lo, lo + 4):
                    v.scalar_tensor_tensor(y6[:, i, :], y6[:, i, :], sy[:, 1, i:i + 1], xt[:, i, :], ALU.mult, ALU.add).then_inc(f_o, 1)


def pad_time(a):
    import numpy as np
    o = np.zeros(a.shape[:-1] + (TP,), a.dtype)
    o[..., :T] = a
    return o


def layouts(inp):
    import numpy as np
    f = np.float32
    L = {}
    L["xT"] = pad_time(inp["x"].transpose(2, 0, 1))
    L["W0"] = inp["L0_attn_W"].T
    L["b0"] = inp["L0_attn_b"].reshape(4, P).T
    wq = inp["L0_xattn_Wq"].reshape(XH, XD, C)
    pq = np.zeros((C, XH, XDP), f)
    pq[:, :, :XD] = wq.transpose(2, 0, 1)
    L["Wxq"] = pq.reshape(C, XH * XDP)
    wkv = inp["L0_xattn_Wkv_expand"]
    pk = np.zeros((64, XH, XDP), f)
    pk[:, :, :XD] = wkv[:C].reshape(XH, XD, 64).transpose(2, 0, 1)
    L["Wxk"] = pk.reshape(64, XH * XDP)
    L["Wxv"] = wkv[C:].T
    po = np.zeros((XH, XDP, C), f)
    po[:, :XD, :] = inp["L0_xattn_Wout"].T.reshape(XH, XD, C)
    L["Wxo"] = po.reshape(XH * XDP, C)
    L["ctx56"] = pad_time(inp["ctx_512"][:, :T, :].transpose(2, 0, 1))
    q = np.arange(P) % TP
    L["causal"] = np.where(np.arange(T)[None, :] <= q[:, None], f(0), f(NEG)).astype(f)
    L["Wr"], L["Wg"], L["Wu"], L["Wd"] = (inp["L0_ffn_" + n] for n in ("w_router", "w_gate", "w_up", "w_down"))
    L["Wsg"], L["Wsu"], L["Wsd"] = (inp["L0_ffn_shared_w_" + n] for n in ("gate", "up", "down"))
    L["amps"] = inp["L0_ffn_amplitudes"].transpose(0, 2, 1)
    L["escale"] = inp["L0_ffn_expert_scale"].reshape(P, 1)
    win = inp["L1_attn_W_in"]
    L["Wzx"] = win[:, :2 * DI]
    up = np.r_[0:DS:2, 1:DS:2]
    sw = np.r_[1:DS:2, 0:DS:2]
    wb, wc = win[:, 2 * DI:2 * DI + DS], win[:, 2 * DI + DS:2 * DI + 2 * DS]
    L["Wbc"] = np.stack([np.tile(w[:, o], (1, 2)) for w in (wb, wc) for o in (up, sw)], 1)
    L["Wdt"] = win[:, 2 * DI + 2 * DS:]
    L["Wmo"] = inp["L1_attn_W_out"]
    L["fcol"] = np.tile(inp["L1_attn_rope_freqs"], (1, 2)).reshape(NH // 2, P).T
    bb, cb = inp["L1_attn_B_bias"], inp["L1_attn_C_bias"]
    L["bcbias"] = np.stack([w[:, o].reshape(NH // 2, P).T for w in (bb, cb) for o in (up, sw)], 1)
    L["dtb"] = inp["L1_attn_dt_bias"].reshape(NH, 1)
    L["alog"] = inp["L1_attn_A_log"].reshape(NH, 1)
    L["Dp"] = inp["L1_attn_D_param"].reshape(1, NH)
    L["nw"] = inp["L1_attn_norm_w"].reshape(DI // P, P).T
    L["sgn"] = (np.where(np.arange(P) % DS < DS // 2, -1.0, 1.0) / (2 * np.pi)).astype(f).reshape(P, 1)
    L["eye"] = np.tile((np.arange(P)[:, None] % TP == np.arange(T)[None, :]).astype(f), (1, 2 * PAIRS))
    L["ctx"] = inp["ctx_512"]
    L["Lwq"] = inp["L1_xattn_Wq"].reshape(LH, P, KC, P).transpose(0, 3, 2, 1)
    L["Lwc"] = inp["L1_xattn_w_kc_q"]
    L["Lwr"] = inp["L1_xattn_W_qr"].transpose(0, 2, 1)
    L["Lwk"] = inp["L1_xattn_W_kr"].transpose(0, 2, 1)
    L["Lwv"] = inp["L1_xattn_w_kc_kv"]
    L["Lwo"] = inp["L1_xattn_Wo"].reshape(C, LH, P).transpose(1, 2, 0)

    def rope(length, dim):
        inv = (1.0 / f(10000.0) ** (np.arange(0, dim, 2, dtype=f) / f(dim))).astype(f)
        a = np.arange(length, dtype=f)[:, None] * inv[None, :]
        sin, cos = np.repeat(np.sin(a), 2, -1), np.repeat(np.cos(a), 2, -1)
        sin[:, :dim // 2] *= -1
        return sin, cos

    sin, cos = rope(T, 2 * RQ)
    L["rqt"] = np.stack([cos[:, :RQ].T, sin[:, :RQ].T, cos[:, RQ:].T, sin[:, RQ:].T], 1)
    sin, cos = rope(S, DC)
    L["rkc"], L["rks"] = cos.reshape(KP, KT, DC), sin.reshape(KP, KT, DC)
    L["kT"] = inp["L1_ffn_kernel"].T
    L["fb"] = inp["L1_ffn_bias"].reshape(1, C)
    return {k: np.ascontiguousarray(a) for k, a in L.items()}


def kernel(**inputs):
    import numpy as _np
    import concourse.bacc as _bacc
    from concourse import mybir as _mybir
    from concourse.bass_utils import run_bass_kernel_spmd as _run

    nc = _bacc.Bacc("TRN2", target_bir_lowering=False, num_devices=1)
    arrays, aps = {}, {}
    for name, a in layouts({k: _np.asarray(v) for k, v in inputs.items()}).items():
        arrays[f"in_{name}_dram"] = a
        aps[name] = nc.dram_tensor(f"in_{name}_dram", a.shape, _mybir.dt.from_np(a.dtype), kind="ExternalInput").ap()
    out = nc.dram_tensor("out_dram", (B, T, C), F32, kind="ExternalOutput").ap()
    decoder(nc, aps, out)
    r = _run(nc, [arrays], core_ids=[0])
    return r.results[0]["out_dram"]
```
